# Optimizing a Trainium2 kernel written in Bass

```python
import numpy as np
import jax
import jax.numpy as jnp

def _softmax(x, axis=-1):
    return jax.nn.softmax(x, axis=axis)

def _gelu(x):
    return jax.nn.gelu(x, approximate=True)

def _silu(x):
    return jax.nn.silu(x)

def _sigmoid(x):
    return jax.nn.sigmoid(x)

def _layernorm(x, axis=-1, eps=1e-05):
    m = jnp.mean(x, axis=axis, keepdims=True)
    v = jnp.var(x, axis=axis, keepdims=True)
    return (x - m) / jnp.sqrt(v + eps)

def _scatter_add(tgt, idx, src, axis=0):
    return tgt.at[idx].add(src)

def _segment_sum(src, seg, n):
    return jax.ops.segment_sum(src, seg, n)
kernel_name = 'mk_seq_postln_d2_jaxref_r8_29ec37'

def setup_inputs(seed: int=0):
    np.random.seed(seed)
    _w = jnp.asarray

    def _L0_attn_setup():
        import jax, jax.numpy as jnp
        import numpy as np
        LN_EPS = 1e-05
        D_HEAD = 64

        def _layernorm(x, w, b):
            x = x - jnp.mean(x, axis=-1, keepdims=True)
            scale = jnp.sqrt(jnp.mean(x * x, axis=-1, keepdims=True) + LN_EPS)
            return x / scale * w + b
        key = jax.random.key(seed)
        ks = jax.random.split(key, 6)
        B, S, D, H, Dh = (2, 256, 128, 16, D_HEAD)
        std = 0.02
        return {'resid_pre': jax.random.normal(ks[0], (B, S, D), dtype=jnp.float32), 'W_Q': jax.random.normal(ks[1], (H, D, Dh), dtype=jnp.float32) * std, 'b_Q': jnp.zeros((H, Dh), dtype=jnp.float32), 'W_K': jax.random.normal(ks[2], (H, D, Dh), dtype=jnp.float32) * std, 'b_K': jnp.zeros((H, Dh), dtype=jnp.float32), 'W_V': jax.random.normal(ks[3], (H, D, Dh), dtype=jnp.float32) * std, 'b_V': jnp.zeros((H, Dh), dtype=jnp.float32), 'W_O': jax.random.normal(ks[4], (H, Dh, D), dtype=jnp.float32) * std, 'b_O': jnp.zeros((D,), dtype=jnp.float32), 'ln1_w': jnp.ones((D,), dtype=jnp.float32), 'ln1_b': jnp.zeros((D,), dtype=jnp.float32), 'ln2_w': jnp.ones((D,), dtype=jnp.float32), 'ln2_b': jnp.zeros((D,), dtype=jnp.float32)}
    _L0_attn_in = _L0_attn_setup()

    def _L0_ffn_setup():
        import jax, jax.numpy as jnp
        import numpy as np
        B, S, D, E, H = (2, 128, 128, 16, 256)
        TOP_K = 2
        TEMP = 1.0
        key = jax.random.key(seed)
        ks = jax.random.split(key, 4)
        sc_d = 1.0 / np.sqrt(D)
        sc_h = 1.0 / np.sqrt(H)
        return {'x': jax.random.normal(ks[0], (B, S, D), dtype=jnp.float32), 'Wr': jax.random.normal(ks[1], (D, E), dtype=jnp.float32) * sc_d, 'br': jnp.zeros((E,), dtype=jnp.float32), 'W1': jax.random.normal(ks[2], (E, D, H), dtype=jnp.float32) * sc_d, 'b1': jnp.zeros((E, H), dtype=jnp.float32), 'W2': jax.random.normal(ks[3], (E, H, D), dtype=jnp.float32) * sc_h, 'b2': jnp.zeros((E, D), dtype=jnp.float32)}
    _L0_ffn_in = _L0_ffn_setup()

    def _L1_attn_setup():
        import jax, jax.numpy as jnp
        import numpy as np
        B, N, D = (8, 256, 128)
        key = jax.random.key(seed)
        k1, k2, k3, k4 = jax.random.split(key, 4)
        data = jax.random.normal(k1, (B, N, D), dtype=jnp.float32)
        W1 = jax.random.normal(k2, (1, D), dtype=jnp.float32) * 0.02
        b1 = jnp.zeros((D,), dtype=jnp.float32)
        W2 = jax.random.normal(k3, (2 * D, D), dtype=jnp.float32) * 0.02
        return {'data': data, 'W1': W1, 'b1': b1, 'W2': W2}
    _L1_attn_in = _L1_attn_setup()

    def _L1_ffn_setup():
        import jax, jax.numpy as jnp
        import numpy as np
        DIM = 128
        DEPTH = 2
        HEADS = 8
        DIM_HEAD = 64
        WINDOW = 64
        INNER = HEADS * DIM_HEAD
        HID = int(DIM * 4 * 2 / 3)
        B, N = (2, 1024)
        QK_SCALE = 8.0

        def shift_token(t):
            t1, t2 = jnp.split(t, 2, axis=-1)
            t2 = jnp.pad(t2, ((0, 0), (1, 0), (0, 0)))[:, :-1]
            return jnp.concatenate([t1, t2], axis=-1)

        def l2norm(t):
            return t / jnp.clip(jnp.linalg.norm(t, axis=-1, keepdims=True), 1e-12)

        def rotate_half(x):
            x1, x2 = jnp.split(x, 2, axis=-1)
            return jnp.concatenate([-x2, x1], axis=-1)

        def rotary_xpos(q, k):
            n = q.shape[-2]
            half_idx = jnp.arange(0, DIM_HEAD, 2, dtype=jnp.float32)
            inv_freq = 1.0 / 10000.0 ** (half_idx / DIM_HEAD)
            t = jnp.arange(n, dtype=jnp.float32)
            freqs = t[:, None] * inv_freq[None, :]
            freqs = jnp.concatenate([freqs, freqs], axis=-1)
            base = (half_idx + 0.4 * DIM_HEAD) / (1.4 * DIM_HEAD)
            power = (t - n // 2) / float(WINDOW // 2)
            scale = base[None, :] ** power[:, None]
            scale = jnp.concatenate([scale, scale], axis=-1)
            cos, sin = (jnp.cos(freqs), jnp.sin(freqs))
            q = q * cos * scale + rotate_half(q) * sin * scale
            k = k * cos / scale + rotate_half(k) * sin / scale
            return (q, k)

        def local_attention(q, k, v):
            b, h, n, d = q.shape
            w = n // WINDOW
            bq = q.reshape(b, h, w, WINDOW, d) * QK_SCALE
            bk = k.reshape(b, h, w, WINDOW, d)
            bv = v.reshape(b, h, w, WINDOW, d)

            def look_around(t):
                p = jnp.pad(t, ((0, 0), (0, 0), (1, 0), (0, 0), (0, 0)))
                return jnp.concatenate([p[:, :, :w], p[:, :, 1:]], axis=3)
            bk, bv = (look_around(bk), look_around(bv))
            bt = jnp.arange(n).reshape(w, WINDOW)
            btp = jnp.pad(bt, ((1, 0), (0, 0)), constant_values=-1)
            btk = jnp.concatenate([btp[:w], btp[1:]], axis=1)
            sim = jnp.einsum('bhwid,bhwjd->bhwij', bq, bk)
            i = bt[:, :, None]
            j = btk[:, None, :]
            mask = (i < j) | (i > j + WINDOW) | (j == -1)
            sim = jnp.where(mask, -jnp.finfo(sim.dtype).max, sim)
            attn = jax.nn.softmax(sim, axis=-1)
            out = jnp.einsum('bhwij,bhwjd->bhwid', attn, bv)
            return out.reshape(b, h, n, d)

        def _layer(x, wqkv, qs, ksc, wo, lg, lb, w1, b1, w2, b2):
            b, n, _ = x.shape
            h = shift_token(x)
            qkv = h @ wqkv
            q, k, v = jnp.split(qkv, 3, axis=-1)
            to_heads = lambda t: t.reshape(b, n, HEADS, DIM_HEAD).transpose(0, 2, 1, 3)
            q, k, v = (to_heads(q), to_heads(k), to_heads(v))
            q = l2norm(q) * qs
            k = l2norm(k) * ksc
            q, k = rotary_xpos(q, k)
            o = local_attention(q, k, v)
            o = o.transpose(0, 2, 1, 3).reshape(b, n, INNER)
            x = x + o @ wo
            h = shift_token(x)
            mu = h.mean(-1, keepdims=True)
            var = h.var(-1, keepdims=True)
            h = (h - mu) / jnp.sqrt(var + 1e-05) * lg + lb
            h = h @ w1 + b1
            a, g = jnp.split(h, 2, axis=-1)
            h = a * jax.nn.gelu(g, approximate=False)
            x = x + h @ w2 + b2
            return x
        key = jax.random.key(seed)
        ks = jax.random.split(key, 6)
        return {'x': jax.random.normal(ks[0], (B, N, DIM), jnp.float32), 'wqkv': jax.random.normal(ks[1], (DEPTH, DIM, 3 * INNER), jnp.float32) * 0.02, 'q_scale': jnp.ones((DEPTH, DIM_HEAD), jnp.float32), 'k_scale': jnp.ones((DEPTH, DIM_HEAD), jnp.float32), 'wo': jax.random.normal(ks[2], (DEPTH, INNER, DIM), jnp.float32) * 0.02, 'ln_g': jnp.ones((DEPTH, DIM), jnp.float32), 'ln_b': jnp.zeros((DEPTH, DIM), jnp.float32), 'w1': jax.random.normal(ks[3], (DEPTH, DIM, 2 * HID), jnp.float32) * 0.02, 'b1': jnp.zeros((DEPTH, 2 * HID), jnp.float32), 'w2': jax.random.normal(ks[4], (DEPTH, HID, DIM), jnp.float32) * 0.02, 'b2': jnp.zeros((DEPTH, DIM), jnp.float32)}
    _L1_ffn_in = _L1_ffn_setup()
    _d = {'L0_attn_resid_pre': _L0_attn_in['resid_pre'], 'L0_attn_W_Q': _L0_attn_in['W_Q'], 'L0_attn_b_Q': _L0_attn_in['b_Q'], 'L0_attn_W_K': _L0_attn_in['W_K'], 'L0_attn_b_K': _L0_attn_in['b_K'], 'L0_attn_W_V': _L0_attn_in['W_V'], 'L0_attn_b_V': _L0_attn_in['b_V'], 'L0_attn_W_O': _L0_attn_in['W_O'], 'L0_attn_b_O': _L0_attn_in['b_O'], 'L0_attn_ln1_w': _L0_attn_in['ln1_w'], 'L0_attn_ln1_b': _L0_attn_in['ln1_b'], 'L0_attn_ln2_w': _L0_attn_in['ln2_w'], 'L0_attn_ln2_b': _L0_attn_in['ln2_b'], 'L0_ffn_Wr': _L0_ffn_in['Wr'], 'L0_ffn_br': _L0_ffn_in['br'], 'L0_ffn_W1': _L0_ffn_in['W1'], 'L0_ffn_b1': _L0_ffn_in['b1'], 'L0_ffn_W2': _L0_ffn_in['W2'], 'L0_ffn_b2': _L0_ffn_in['b2'], 'L1_attn_W1': _L1_attn_in['W1'], 'L1_attn_b1': _L1_attn_in['b1'], 'L1_attn_W2': _L1_attn_in['W2'], 'L1_ffn_wqkv': _L1_ffn_in['wqkv'], 'L1_ffn_q_scale': _L1_ffn_in['q_scale'], 'L1_ffn_k_scale': _L1_ffn_in['k_scale'], 'L1_ffn_wo': _L1_ffn_in['wo'], 'L1_ffn_ln_g': _L1_ffn_in['ln_g'], 'L1_ffn_ln_b': _L1_ffn_in['ln_b'], 'L1_ffn_w1': _L1_ffn_in['w1'], 'L1_ffn_b1': _L1_ffn_in['b1'], 'L1_ffn_w2': _L1_ffn_in['w2'], 'L1_ffn_b2': _L1_ffn_in['b2']}
    _x0 = _d['L0_attn_resid_pre']
    _d['L0_attn_resid_pre'] = jax.random.normal(jax.random.fold_in(jax.random.key(seed), 1), (8, 256, 128), dtype=_x0.dtype)
    del _x0
    return _d

def reference(L0_attn_resid_pre, L0_attn_W_Q, L0_attn_b_Q, L0_attn_W_K, L0_attn_b_K, L0_attn_W_V, L0_attn_b_V, L0_attn_W_O, L0_attn_b_O, L0_attn_ln1_w, L0_attn_ln1_b, L0_attn_ln2_w, L0_attn_ln2_b, L0_ffn_Wr, L0_ffn_br, L0_ffn_W1, L0_ffn_b1, L0_ffn_W2, L0_ffn_b2, L1_attn_W1, L1_attn_b1, L1_attn_W2, L1_ffn_wqkv, L1_ffn_q_scale, L1_ffn_k_scale, L1_ffn_wo, L1_ffn_ln_g, L1_ffn_ln_b, L1_ffn_w1, L1_ffn_b1, L1_ffn_w2, L1_ffn_b2):

    def _L0_attn_ref(resid_pre, W_Q, b_Q, W_K, b_K, W_V, b_V, W_O, b_O, ln1_w, ln1_b, ln2_w, ln2_b):
        import jax, jax.numpy as jnp
        import numpy as np
        LN_EPS = 1e-05
        D_HEAD = 64

        def _layernorm(x, w, b):
            x = x - jnp.mean(x, axis=-1, keepdims=True)
            scale = jnp.sqrt(jnp.mean(x * x, axis=-1, keepdims=True) + LN_EPS)
            return x / scale * w + b
        x = _layernorm(resid_pre, ln1_w, ln1_b)
        q = jnp.einsum('hdk,bsd->bshk', W_Q, x) + b_Q
        k = jnp.einsum('hdk,bsd->bshk', W_K, x) + b_K
        v = jnp.einsum('hdk,bsd->bshk', W_V, x) + b_V
        scores = jnp.einsum('bqhk,bphk->bhqp', q, k) / jnp.sqrt(jnp.asarray(D_HEAD, dtype=q.dtype))
        S = scores.shape[-1]
        causal = jnp.tril(jnp.ones((S, S), dtype=bool))
        scores = jnp.where(causal, scores, jnp.asarray(0.0, dtype=scores.dtype))
        pattern = jax.nn.softmax(scores, axis=-1)
        z = jnp.einsum('bhqp,bphk->bqhk', pattern, v)
        attn_out = jnp.einsum('bqhk,hkd->bqd', z, W_O) + b_O
        resid_mid = resid_pre + attn_out
        resid_post = resid_mid + _layernorm(resid_mid, ln2_w, ln2_b)
        return resid_post

    def _L0_ffn_ref(x, Wr, br, W1, b1, W2, b2):
        import jax, jax.numpy as jnp
        import numpy as np
        B, S, D, E, H = (2, 128, 128, 16, 256)
        TOP_K = 2
        TEMP = 1.0
        token_shape = x.shape[:-1]
        d = x.shape[-1]
        xt = x.reshape(-1, d)
        T = xt.shape[0]
        logits = (xt @ Wr + br) / TEMP
        probs = jax.nn.softmax(logits, axis=-1)
        w, idx = jax.lax.top_k(probs, TOP_K)
        w = w / jnp.clip(jnp.sum(w, axis=-1, keepdims=True), 1e-09)
        comb = jnp.zeros((T, E), dtype=xt.dtype)
        comb = comb.at[jnp.arange(T)[:, None], idx].add(w)
        h = jax.nn.gelu(jnp.einsum('td,edh->teh', xt, W1) + b1, approximate=False)
        o = jnp.einsum('teh,eho->teo', h, W2) + b2
        y = jnp.einsum('teo,te->to', o, comb)
        y = xt + y
        return y.reshape(*token_shape, d)

    def _L1_attn_ref(data, W1, b1, W2):
        import jax, jax.numpy as jnp
        import numpy as np
        B, N, D = (8, 256, 128)
        sq = jnp.sum(data * data, axis=-1, keepdims=True)
        normed = data * jax.lax.rsqrt(jnp.maximum(sq, 1e-12))
        sim = jnp.einsum('bnd,bmd->bnm', normed, normed)
        counter = jnp.sum(jax.nn.relu(sim), axis=-1, keepdims=True)
        counter = jax.nn.softplus(counter @ W1 + b1)
        out = jnp.concatenate([data, counter], axis=-1) @ W2
        return out

    def _L1_ffn_ref(x, wqkv, q_scale, k_scale, wo, ln_g, ln_b, w1, b1, w2, b2):
        import jax, jax.numpy as jnp
        import numpy as np
        DIM = 128
        DEPTH = 2
        HEADS = 8
        DIM_HEAD = 64
        WINDOW = 64
        INNER = HEADS * DIM_HEAD
        HID = int(DIM * 4 * 2 / 3)
        B, N = (2, 1024)
        QK_SCALE = 8.0

        def shift_token(t):
            t1, t2 = jnp.split(t, 2, axis=-1)
            t2 = jnp.pad(t2, ((0, 0), (1, 0), (0, 0)))[:, :-1]
            return jnp.concatenate([t1, t2], axis=-1)

        def l2norm(t):
            return t / jnp.clip(jnp.linalg.norm(t, axis=-1, keepdims=True), 1e-12)

        def rotate_half(x):
            x1, x2 = jnp.split(x, 2, axis=-1)
            return jnp.concatenate([-x2, x1], axis=-1)

        def rotary_xpos(q, k):
            n = q.shape[-2]
            half_idx = jnp.arange(0, DIM_HEAD, 2, dtype=jnp.float32)
            inv_freq = 1.0 / 10000.0 ** (half_idx / DIM_HEAD)
            t = jnp.arange(n, dtype=jnp.float32)
            freqs = t[:, None] * inv_freq[None, :]
            freqs = jnp.concatenate([freqs, freqs], axis=-1)
            base = (half_idx + 0.4 * DIM_HEAD) / (1.4 * DIM_HEAD)
            power = (t - n // 2) / float(WINDOW // 2)
            scale = base[None, :] ** power[:, None]
            scale = jnp.concatenate([scale, scale], axis=-1)
            cos, sin = (jnp.cos(freqs), jnp.sin(freqs))
            q = q * cos * scale + rotate_half(q) * sin * scale
            k = k * cos / scale + rotate_half(k) * sin / scale
            return (q, k)

        def local_attention(q, k, v):
            b, h, n, d = q.shape
            w = n // WINDOW
            bq = q.reshape(b, h, w, WINDOW, d) * QK_SCALE
            bk = k.reshape(b, h, w, WINDOW, d)
            bv = v.reshape(b, h, w, WINDOW, d)

            def look_around(t):
                p = jnp.pad(t, ((0, 0), (0, 0), (1, 0), (0, 0), (0, 0)))
                return jnp.concatenate([p[:, :, :w], p[:, :, 1:]], axis=3)
            bk, bv = (look_around(bk), look_around(bv))
            bt = jnp.arange(n).reshape(w, WINDOW)
            btp = jnp.pad(bt, ((1, 0), (0, 0)), constant_values=-1)
            btk = jnp.concatenate([btp[:w], btp[1:]], axis=1)
            sim = jnp.einsum('bhwid,bhwjd->bhwij', bq, bk)
            i = bt[:, :, None]
            j = btk[:, None, :]
            mask = (i < j) | (i > j + WINDOW) | (j == -1)
            sim = jnp.where(mask, -jnp.finfo(sim.dtype).max, sim)
            attn = jax.nn.softmax(sim, axis=-1)
            out = jnp.einsum('bhwij,bhwjd->bhwid', attn, bv)
            return out.reshape(b, h, n, d)

        def _layer(x, wqkv, qs, ksc, wo, lg, lb, w1, b1, w2, b2):
            b, n, _ = x.shape
            h = shift_token(x)
            qkv = h @ wqkv
            q, k, v = jnp.split(qkv, 3, axis=-1)
            to_heads = lambda t: t.reshape(b, n, HEADS, DIM_HEAD).transpose(0, 2, 1, 3)
            q, k, v = (to_heads(q), to_heads(k), to_heads(v))
            q = l2norm(q) * qs
            k = l2norm(k) * ksc
            q, k = rotary_xpos(q, k)
            o = local_attention(q, k, v)
            o = o.transpose(0, 2, 1, 3).reshape(b, n, INNER)
            x = x + o @ wo
            h = shift_token(x)
            mu = h.mean(-1, keepdims=True)
            var = h.var(-1, keepdims=True)
            h = (h - mu) / jnp.sqrt(var + 1e-05) * lg + lb
            h = h @ w1 + b1
            a, g = jnp.split(h, 2, axis=-1)
            h = a * jax.nn.gelu(g, approximate=False)
            x = x + h @ w2 + b2
            return x
        for l in range(DEPTH):
            x = _layer(x, wqkv[l], q_scale[l], k_scale[l], wo[l], ln_g[l], ln_b[l], w1[l], b1[l], w2[l], b2[l])
        return x
    x = L0_attn_resid_pre
    x = _layernorm(x + _L0_attn_ref(x, L0_attn_W_Q, L0_attn_b_Q, L0_attn_W_K, L0_attn_b_K, L0_attn_W_V, L0_attn_b_V, L0_attn_W_O, L0_attn_b_O, L0_attn_ln1_w, L0_attn_ln1_b, L0_attn_ln2_w, L0_attn_ln2_b), axis=-1)
    x = _layernorm(x + _L0_ffn_ref(x, L0_ffn_Wr, L0_ffn_br, L0_ffn_W1, L0_ffn_b1, L0_ffn_W2, L0_ffn_b2), axis=-1)
    x = _layernorm(x + _L1_attn_ref(x, L1_attn_W1, L1_attn_b1, L1_attn_W2), axis=-1)
    x = _layernorm(x + _L1_ffn_ref(x, L1_ffn_wqkv, L1_ffn_q_scale, L1_ffn_k_scale, L1_ffn_wo, L1_ffn_ln_g, L1_ffn_ln_b, L1_ffn_w1, L1_ffn_b1, L1_ffn_w2, L1_ffn_b2), axis=-1)
    return x

_drawn_inputs = setup_inputs


def setup_inputs(seed=0):
    import zlib

    import numpy as np

    out = dict(_drawn_inputs(seed))
    spreads = {'L0_attn_b_Q': (0.0, 0.8),
     'L0_attn_b_K': (0.0, 2.0),
     'L0_attn_b_V': (0.0, 0.1),
     'L0_attn_b_O': (0.0, 0.1),
     'L0_attn_ln1_w': (1.0, 0.6),
     'L0_attn_ln1_b': (0.0, 0.284),
     'L0_attn_ln2_w': (1.0, 0.2),
     'L0_attn_ln2_b': (0.0, 0.1),
     'L0_ffn_br': (0.0, 0.1),
     'L0_ffn_b1': (0.0, 0.338),
     'L0_ffn_b2': (0.0, 0.1),
     'L1_attn_b1': (0.0, 0.774),
     'L1_ffn_q_scale': (1.0, 0.6),
     'L1_ffn_k_scale': (1.0, 0.6),
     'L1_ffn_ln_g': (1.0, 0.6),
     'L1_ffn_ln_b': (0.0, 0.8),
     'L1_ffn_b1': (0.0, 0.8),
     'L1_ffn_b2': (0.0, 0.557)}
    factors = {'L0_attn_W_Q': 8.0,
     'L0_attn_W_K': 8.0,
     'L1_ffn_wqkv': 2.834,
     'L1_ffn_wo': 2.9,
     'L1_ffn_w1': 6.579,
     'L1_ffn_w2': 6.459}
    for name, (base, spread) in spreads.items():
        noise = np.random.default_rng([zlib.crc32(name.encode()), seed]).standard_normal(out[name].shape)
        drawn = base * np.exp(spread * noise) if base else spread * noise
        out[name] = jnp.asarray(drawn.astype(out[name].dtype))
    for name, factor in factors.items():
        out[name] = (out[name] * factor).astype(out[name].dtype)
    return out
```

```python
import concourse.bass as bass
from concourse import mybir
from contextlib import ExitStack

F32 = mybir.dt.float32
BF16 = mybir.dt.bfloat16
I32 = mybir.dt.int32
ALU = mybir.AluOpType
ACT = mybir.ActivationFunctionType
AX = mybir.AxisListType

P = 128
D = 128
B, S = 8, 256
TB = S // P
NT = B * TB
CH = 4
NC = NT // CH
EPS = 1e-5

H0, DH = 16, 64
PAIRS0 = H0 // 2
SLOTS = B * PAIRS0
WCOLS = 3 * P + 2

NE, HE = 16, 256
KE = HE // P

LAYERS, H1, WIN = 2, 8, 64
INNER = H1 * DH
PAIRS1 = H1 // 2
HID = 341
FCH = [(0, 128), (128, 128), (256, HID - 256)]
SCRATCH = 11264
NEG = -1e30

R_BQ, R_BK, R_BV, R_BO, R_LN1W, R_LN1B, R_CB1 = 0, 8, 16, 24, 25, 26, 27
R_B1, R_B2, R_LG, R_LB, R_FB1 = 28, 60, 62, 64, 66
FREE = 1


def build_program(nc, A, out):
    with ExitStack() as ctx:
        def sb(name, shape, dt=F32):
            return ctx.enter_context(nc.sbuf_tensor(name, shape, dt))

        def sem(name):
            return ctx.enter_context(nc.semaphore(name))

        psum = ctx.enter_context(nc.psum_tensor("psum", [P, 8, 512], F32))

        def bank(k):
            return psum[:, k, :]

        ident = sb("ident", [P, P])
        identb = sb("identb", [P, P], BF16)
        causal = sb("causal", [P, P])
        band0 = sb("band0", [P, 2, P], BF16)
        band1 = sb("band1", [P, 2, 192], BF16)
        shift = sb("shift", [P, P])
        carry = sb("carry", [P, P])
        mhalf = sb("mhalf", [P, 4])
        onecol = sb("onecol", [P, 1])
        zrow = sb("zrow", [P, 1])
        vrows = sb("vrows", [P, P])
        vec = sb("vec", [P, P])
        bo_eff = sb("bo_eff", [P, 1])
        w_qkv0 = sb("w_qkv0", [P, PAIRS0, WCOLS])
        w_o0 = sb("w_o0", [P, PAIRS0, D])
        ln2w = sb("ln2w", [P, D])
        ln2b = sb("ln2b", [P, D])
        w_r = sb("w_r", [P, NE])
        br = sb("br", [P, NE])
        b2e = sb("b2e", [NE, D])
        w1c = sb("w1c", [P, D])
        w2c = sb("w2c", [P, 2, D])
        wqkv1 = sb("wqkv1", [P, LAYERS, 3 * INNER])
        wo1 = sb("wo1", [P, LAYERS, PAIRS1, D])
        wf1 = sb("wf1", [P, LAYERS, 2 * HID])
        wf2 = sb("wf2", [P, LAYERS, 3, D])
        tab = sb("tab", [P, 4, TB, DH])
        qks = sb("qks", [P, 2, LAYERS, DH])
        rot = sb("rot", [P, LAYERS, 4, TB, DH])

        x0 = sb("x0", [P, NT, D])
        acc = sb("acc", [P, NT, D])
        x3 = sb("x3", [P, NT, D])
        x4 = acc
        big = sb("big", [P, SLOTS * S])
        zT = big[:, :].rearrange("p (g n) -> p g n", n=S)
        scratch = sb("scratch", [P, SCRATCH])
        at = [0, 0]

        def shaped(v, dims):
            if len(dims) == 1:
                return v
            names = "abcd"[:len(dims)]
            return v.rearrange(f"p ({' '.join(names)}) -> p {' '.join(names)}", **dict(zip(names, dims)))

        def carve(which, dims, dt=F32):
            n = 1
            for d in dims:
                n *= d
            a = at[which]
            at[which] = a + n
            assert at[which] <= (SLOTS * S, SCRATCH)[which], (which, at)
            return shaped((big, scratch)[which][:, a:a + n], dims)

        def from_big(*dims):
            return carve(0, dims)

        def from_scratch(*dims):
            return carve(1, dims)
        xT = sb("xT", [P, NT * P])
        comb = sb("comb", [P, NT, NE])

        st = sb("st", [P, 2, CH, 6])
        mv = sb("mv", [P, 2, CH, 2])
        ve = sb("ve", [P, 2, CH])
        rstd = sb("rstd", [P, 2, CH])

        x_in = sem("x_in")
        w_in = sem("w_in")
        rows_zero = sem("rows_zero")
        rows_in = sem("rows_in")
        const_ready = sem("const_ready")
        vec_ps = sem("vec_ps")
        vec_ready = sem("vec_ready")
        bo_ps = sem("bo_ps")
        phase_done = sem("phase_done")

        def apart(eng):
            eng.wait_ge(const_ready, 1)

        def end_phase(eng, n):
            eng.drain().then_inc(phase_done, 1)
            eng.wait_ge(phase_done, 4 * n)

        a_var, a_rstd, a_xn, a_tr, a_xt = (sem(f"a_{n}") for n in ("var", "rstd", "xn", "tr", "xt"))
        xn = sb("xn", [P, CH, D])

        wst = [from_scratch(WCOLS) for i in range(2)]
        xst = [from_scratch(S) for i in range(2)]
        qT = [from_scratch(S) for i in range(2)]
        kZ = [from_scratch(2, S) for i in range(2)]
        vS = [from_scratch(TB, P) for i in range(2)]
        pr = [from_scratch(TB, 2, S) for i in range(2)]
        pt = [from_scratch(TB * S) for i in range(2)]
        mx = from_scratch(4)
        nb = [from_scratch(4) for i in range(2)]
        sm = [from_scratch(4) for i in range(2)]
        rs = from_scratch(4)
        w_staged = [sem(f"w_staged{i}") for i in range(2)]
        x_staged = [sem(f"x_staged{i}") for i in range(2)]
        kz_zero = sem("kz_zero")
        s0_zero = sem("s0_zero")
        qk_ready, v_ready, qk_sb, v_sb, scores_ready, negmax_ready, exp_ready, probs_ready = (
            sem(n) for n in ("qk_ready", "v_ready", "qk_sb", "v_sb", "scores_ready", "negmax_ready",
                             "exp_ready", "probs_ready"))
        pT_ready = [sem(f"pT_ready{i}") for i in range(2)]
        pt_sb = [sem(f"pt_sb{i}") for i in range(2)]
        z_ready, z_sb = sem("z_ready"), sem("z_sb")

        at[1] = 0
        oT = from_scratch(CH * P)
        mid = from_scratch(CH, D)
        uC = from_scratch(CH, D)
        x1c = from_scratch(CH, D)
        xt1c = from_scratch(CH * P)
        lg = from_scratch(CH, NE)
        ex = from_scratch(CH, NE)
        r4 = from_scratch(CH)
        m8 = from_scratch(CH, 8)
        top2 = from_scratch(CH, 8)
        rest = from_scratch(CH, NE)
        combc = from_scratch(CH, NE)
        combT = from_scratch(CH * P)[0:NE]
        (c_o, c_oT, c_tr, c_mid, c_u, c_var, c_rstd, c_x1, c_xtps, c_xt, c_lg, c_sub, c_exp, c_comb,
         c_ctps, c_ct, c_yb, c_acc) = (sem(f"c_{n}") for n in (
             "o", "oT", "tr", "mid", "u", "var", "rstd", "x1", "xtps", "xt", "lg", "sub", "exp",
             "comb", "ctps", "ct", "yb", "acc"))

        at[0] = 0
        w1e = [sb(f"w1e{i}", [P, HE]) for i in range(2)]
        w2e = [sb(f"w2e{i}", [P, KE, D]) for i in range(2)]
        gE = [from_big(KE, CH * P) for i in range(2)]
        b1x = [from_big(KE) for i in range(2)]
        we_in = [sem(f"we_in{i}") for i in range(2)]
        u_ready, g_ready, y_ready, acc_done = (sem(n) for n in ("u_ready", "g_ready", "y_ready", "acc_done"))

        at[0] = 0

        def two(make, *dims):
            return [make(*dims) for _ in range(2)]

        x2 = two(from_big, TB, D)
        sqj = two(from_big, TB, D)
        ssq = two(from_big, TB)
        mq = two(from_big, TB)
        rn = two(from_big, TB)
        nrm = two(from_big, TB, D)
        xnT = two(from_big, 2 * S)
        rel = two(from_big, TB * S)
        zb = two(from_big, S)
        az = two(from_big, S)
        sp = two(from_big, S)
        oE = two(from_big, S)
        (e_var, e_rstd, e_x2, e_ssq, e_mq, e_rn, e_nrm, e_xnps, e_xn, e_sim, e_rel, e_ctr, e_log, e_sp,
         e_o, e_osb, e_oT, e_x3) = (sem(f"e_{n}") for n in (
             "var", "rstd", "x2", "ssq", "mq", "rn", "nrm", "xnps", "xn", "sim", "rel", "ctr", "log",
             "sp", "o", "osb", "oT", "x3"))

        at[0], at[1] = 0, 0
        v1 = two(from_big, TB, INNER)
        sq1 = two(from_big, 2 * INNER)
        t1 = two(from_big, 2 * INNER)
        t2 = two(from_big, 2 * INNER)
        qk = two(from_big, 2 * INNER)
        q1T = two(from_big, PAIRS1, S)
        k1Z = two(from_big, PAIRS1, 2, S)
        xc = two(from_scratch, TB, D)
        hT = two(from_scratch, S)
        p0 = two(from_scratch, 2, P)
        p1 = two(from_scratch, 2, S)
        pt1 = two(from_scratch, 3 * P)
        ss = two(from_scratch, TB, 2 * H1)
        yi = sb("yi", [P, TB, 2 * H1], I32)
        rqk = two(from_scratch, TB, 2 * H1)
        ny = sb("ny", [P, TB, 2 * H1])
        rq8 = two(from_scratch, TB, H1)
        nrq8 = two(from_scratch, TB, H1)
        mx1 = two(from_scratch, TB, 2)
        nb1 = two(from_scratch, TB, 2)
        sm1 = two(from_scratch, TB, 2)
        rs1 = two(from_scratch, TB, 2)
        oT1 = two(from_scratch, PAIRS1, S)
        yT = two(from_scratch, S)
        xm = two(from_scratch, TB, D)
        hb = two(from_scratch, TB, D)
        h2T = two(from_scratch, S)
        gl = two(from_scratch, 3, S)
        hg = two(from_scratch, 3, S)
        fT = two(from_scratch, S)
        (f_xc, f_xcT, f_hT, f_qkv, f_sq, f_rot, f_rn, f_add, f_kn, f_trps, f_trsb, f_s, f_nb, f_e, f_p,
         f_t, f_pt0, f_pt1, f_z, f_zsb, f_wo, f_wosb, f_woT, f_xm, f_sh, f_hb, f_var, f_rstd, f_hn,
         f_h2ps, f_h2, f_g, f_a, f_gl, f_hg, f_w2, f_w2sb, f_w2T, f_x, f_zero) = (
             sem(f"f_{n}") for n in (
                 "xc", "xcT", "hT", "qkv", "sq", "rot", "rn", "add", "kn", "trps", "trsb", "s", "nb",
                 "e", "p", "t", "pt0", "pt1", "z", "zsb", "wo", "wosb", "woT", "xm", "sh", "hb",
                 "var", "rstd", "hn", "h2ps", "h2", "g", "a", "gl", "hg", "w2", "w2sb", "w2T", "x",
                 "zero"))
        out_sem = sem("out_sem")
        x5 = x0

        def run_slots(eng, slot):
            for g in (-2, -1):
                slot(g, g % 2)
            with eng.Fori(0, SLOTS // 2 - 1) as i:
                for s in range(2):
                    slot(i * 2 + s, s)
            for g in (SLOTS - 2, SLOTS - 1):
                slot(g, g % 2)

        N_ROWS = 23
        block = ctx.enter_context(nc.Block())

        @block.sync
        def _(sp_):
            sp_.dma_start(x0[:], A["L0_attn_resid_pre"].rearrange("b (t p) d -> p (b t) d", p=P)).then_inc(x_in, 16)
            sp_.wait_ge(rows_zero, 1)

            def rows(r, n, src, w=P):
                sp_.dma_start(vrows[r:r + n, 0:w], src).then_inc(rows_in, 16)

            one = lambda name: A[name].rearrange("(a d) -> a d", a=1)
            rows(R_LN1W, 1, one("L0_attn_ln1_w"))
            rows(R_LN1B, 1, one("L0_attn_ln1_b"))
            for r, name in ((R_BQ, "Q"), (R_BK, "K"), (R_BV, "V")):
                rows(r, PAIRS0, A[f"L0_attn_b_{name}"].rearrange("(a two) k -> a (two k)", two=2))
            rows(R_BO, 1, one("L0_attn_b_O"))
            rows(R_CB1, 1, one("L1_attn_b1"))
            rows(R_B1, NE * KE, A["L0_ffn_b1"].rearrange("e (k p) -> (e k) p", p=P))
            rows(R_B2, LAYERS, A["L1_ffn_b2"])
            rows(R_LG, LAYERS, A["L1_ffn_ln_g"])
            rows(R_LB, LAYERS, A["L1_ffn_ln_b"])
            for la in range(LAYERS):
                for half in range(2):
                    for c, (o, w) in enumerate(FCH):
                        rows(R_FB1 + 6 * la + 3 * half + c, 1,
                             A["L1_ffn_b1"][la:la + 1, half * HID + o:half * HID + o + w], w)
            n = [0]

            def load(dst, src):
                sp_.dma_start(dst, src).then_inc(w_in, 16)
                n[0] += 1

            for j, name in enumerate("QKV"):
                for h in range(2):
                    o = j * P + h * DH
                    load(w_qkv0[:, :, o:o + DH],
                         A[f"L0_attn_W_{name}"].rearrange("(a two) d k -> two d a k", two=2)[h])
            load(w_o0[:], A["L0_attn_W_O"].rearrange("h k d -> (h k) d").rearrange("(a p) d -> p a d", p=P))
            load(ln2w[:], A["L0_attn_ln2_w"].partition_broadcast(P))
            load(ln2b[:], A["L0_attn_ln2_b"].partition_broadcast(P))
            load(w_r[:], A["L0_ffn_Wr"])
            load(br[:], A["L0_ffn_br"].partition_broadcast(P))
            load(b2e[:], A["L0_ffn_b2"])
            load(w1c[:], A["L1_attn_W1"].rearrange("a d -> (a d)").partition_broadcast(P))
            load(w2c[:], A["L1_attn_W2"].rearrange("(a p) d -> p a d", p=P))
            load(tab[:], A["tables"].rearrange("j (t p) k -> p j t k", p=P))
            for j, name in enumerate(("q", "k")):
                load(qks[:, j], A[f"L1_ffn_{name}_scale"].rearrange("a b -> (a b)").partition_broadcast(P)
                     .rearrange("p (a b) -> p a b", a=LAYERS))
            load(wqkv1[:], A["L1_ffn_wqkv"].rearrange("l p n -> p l n"))
            load(wo1[:], A["L1_ffn_wo"].rearrange("l (a p) d -> p l a d", p=P))
            load(wf1[:], A["L1_ffn_w1"].rearrange("l p n -> p l n"))
            for la in range(LAYERS):
                load(wf2[:, la, 0:2, :], A["L1_ffn_w2"][la, 0:256, :].rearrange("(c p) d -> p c d", p=P))
                load(wf2[0:HID - 256, la, 2, :], A["L1_ffn_w2"][la, 256:HID, :])
            assert n[0] == N_W
            for e in range(2):
                sp_.dma_start(w1e[e][:], A["L0_ffn_W1"][e]).then_inc(we_in[e], 16)
                sp_.dma_start(w2e[e][:], A["L0_ffn_W2"][e].rearrange("(k p) d -> p k d", p=P)).then_inc(we_in[e], 16)
            sp_.wait_ge(phase_done, 4)
            with sp_.Fori(0, B) as b:
                with sp_.Fori(0, PAIRS0 // 2) as pp:
                    for s in range(2):
                        g = b * PAIRS0 + pp * 2 + s
                        sp_.wait_ge(v_ready, g + 1)
                        sp_.wait_ge(qk_sb, g + 1)
                        sp_.dma_start(wst[s][:], w_qkv0[:, pp * 2 + s, :]).then_inc(w_staged[s], 16)
                        sp_.dma_start(xst[s][:], xT[:, bass.ds(b * S, S)]).then_inc(x_staged[s], 16)
            with sp_.Fori(1, NE // 2) as i:
                for e in range(2):
                    sp_.wait_ge(y_ready, i * (2 * NC) + ((e - 1) * NC + 2))
                    sp_.dma_start(w1e[e][:], A["L0_ffn_W1"][i * 2 + e]).then_inc(we_in[e], 16)
                    sp_.dma_start(w2e[e][:], A["L0_ffn_W2"][i * 2 + e].rearrange("(k p) d -> p k d", p=P)).then_inc(we_in[e], 16)
            sp_.wait_ge(f_x, LAYERS * B + FREE)
            sp_.dma_start(out.rearrange("b (t p) d -> p (b t) d", p=P), x5[:]).then_inc(out_sem, 16)
            sp_.wait_ge(out_sem, 16)

        @block.gpsimd
        def _(pool):
            pool.memset(mhalf[:], -0.5)
            pool.memset(onecol[:], 1.0)
            pool.memset(ident[:], 0.0)
            pool.memset(causal[:], 1.0)
            pool.memset(band0[:], 0.0)
            pool.memset(band1[:], 0.0)
            pool.memset(shift[:], 0.0)
            pool.memset(carry[:], 0.0)
            pool.drain()
            pool.affine_select(out=ident[:], in_=ident[:], compare_op=ALU.not_equal, fill=1.0, base=0,
                               pattern=[[-1, P]], channel_multiplier=1)
            pool.affine_select(out=causal[:], in_=causal[:], compare_op=ALU.is_ge, fill=0.0, base=0,
                               pattern=[[-1, P]], channel_multiplier=1)
            pool.affine_select(out=band0[:], in_=band0[:], compare_op=ALU.is_ge, fill=NEG, base=0,
                               pattern=[[0, 2], [-1, P]], channel_multiplier=1)
            pool.affine_select(out=band1[:], in_=band1[:], compare_op=ALU.is_ge, fill=NEG, base=WIN,
                               pattern=[[0, 2], [-1, 192]], channel_multiplier=1)
            pool.affine_select(out=shift[:], in_=shift[:], compare_op=ALU.not_equal, fill=1.0, base=1,
                               pattern=[[-1, P]], channel_multiplier=1)
            pool.affine_select(out=carry[:], in_=carry[:], compare_op=ALU.not_equal, fill=1.0,
                               base=-(P - 1), pattern=[[-1, P]], channel_multiplier=1)
            pool.drain()
            pool.affine_select(out=band0[:], in_=band0[:], compare_op=ALU.is_ge, fill=NEG, base=WIN,
                               pattern=[[0, 2], [1, P]], channel_multiplier=-1)
            pool.affine_select(out=band1[:], in_=band1[:], compare_op=ALU.is_ge, fill=NEG, base=0,
                               pattern=[[0, 2], [1, 192]], channel_multiplier=-1)
            pool.tensor_copy(identb[:], ident[:])
            pool.drain().then_inc(const_ready, 1)
            with pool.Fori(0, NC) as c:
                pool.wait_ge(a_var, c + 1)
                pool.tensor_tensor(rstd[:, 0, :], ve[:, 0, :], mhalf[:], ALU.pow).then_inc(a_rstd, 1)
            end_phase(pool, 1)
            for s in range(2):
                pool.memset(kZ[s][64:P, 0, :], 0.0)
                pool.memset(kZ[s][0:64, 1, :], 0.0)
            pool.drain().then_inc(kz_zero, 1)
            end_phase(pool, 2)
            pool.memset(top2[:], -1.0)
            with pool.Fori(0, NC) as c:
                pool.wait_ge(c_mid, c + 1)
                pool.tensor_tensor(uC[:], mid[:], x0[:, bass.ds(c * CH, CH), :], ALU.add)
                pool.drain()
                pool.tensor_tensor(uC[:], uC[:], ln2b[:].unsqueeze(1).to_broadcast([P, CH, D]), ALU.add).then_inc(c_u, 1)
                for k in range(2):
                    pool.wait_ge(c_var, c * 2 + k + 1)
                    pool.tensor_tensor(rstd[:, k, :], ve[:, k, :], mhalf[:], ALU.pow).then_inc(c_rstd, 1)
            end_phase(pool, 3)
            end_phase(pool, 4)
            with pool.Fori(0, B // 2) as i:
                for s in range(2):
                    pool.wait_ge(e_var, i * 4 + s + 1)
                    pool.tensor_tensor(rstd[:, s, 0:TB], ve[:, s, 0:TB], mhalf[:, 0:TB], ALU.pow).then_inc(e_rstd, 1)
                for s in range(2):
                    pool.wait_ge(e_mq, i * 2 + s + 1)
                    pool.tensor_tensor(rn[s][:], mq[s][:], mhalf[:, 0:TB], ALU.pow).then_inc(e_rn, 1)
                for s in range(2):
                    pool.wait_ge(e_var, i * 4 + s + 3)
                    pool.tensor_tensor(rstd[:, s, 0:TB], ve[:, s, 0:TB], mhalf[:, 0:TB], ALU.pow).then_inc(e_rstd, 1)
            end_phase(pool, 5)
            for s in range(2):
                pool.memset(k1Z[s][64:P, :, 0, :], 0.0)
                pool.drain()
                pool.memset(k1Z[s][0:64, :, 1, :], 0.0)
                pool.drain()
                pool.memset(p1[s][:, :, 0:WIN], 0.0)
                pool.drain()
                pool.memset(hT[s][64:P, 0:1], 0.0)
                pool.drain()
            pool.drain().then_inc(f_zero, 1)
            for la in range(LAYERS):
                src = (x3, x4)[la]
                with pool.Fori(0, B // 2) as i:
                    n0 = i * 2 + la * B
                    for s in range(2):
                        pool.wait_ge(f_xm, n0 + s + 1)
                        if la:
                            pool.wait_ge(f_x, B + FREE)
                        pool.tensor_copy(xc[s][:], src[:, bass.ds(i * 4 + s * 2, TB), :]).then_inc(f_xc, 1)
                    for s in range(2):
                        for t in range(TB):
                            m = n0 * 2 + s * 2 + t
                            pool.wait_ge(f_rot, m + 1)
                            pool.wait_ge(f_trps, (n0 + s) * 4 + 1)
                            pool.tensor_tensor(qk[t], t1[t], t2[t], ALU.add).then_inc(f_add, 1)
                        pool.drain()
                        pool.wait_ge(f_rn, n0 + s + 1)
                        for t in range(TB):
                            kk = qk[t][:, INNER:].rearrange("p (h k) -> p h k", h=H1)
                            pool.tensor_tensor(kk, kk, rqk[s][:, t, H1:].unsqueeze(2).to_broadcast([P, H1, DH]),
                                               ALU.mult)
                        pool.drain().then_inc(f_kn, 1)
                    for s in range(2):
                        nv = (i * 2 + la * B + s) if la == 0 else (i * 4 + B + s)
                        pool.wait_ge(f_var, nv + 1)
                        pool.tensor_tensor(rstd[:, s, 0:TB], ve[:, s, 0:TB], mhalf[:, 0:TB], ALU.pow).then_inc(f_rstd, 1)
                    if la == LAYERS - 1:
                        for s in range(2):
                            pool.wait_ge(f_var, i * 4 + B + 2 + s + 1)
                            pool.tensor_tensor(rstd[:, s, 0:TB], ve[:, s, 0:TB], mhalf[:, 0:TB], ALU.pow).then_inc(f_rstd, 1)

        @block.scalar
        def _(act):
            act.wait_ge(vec_ps, 1)
            act.activation(vec[:], bank(0)[:, 0:P], ACT.Copy).then_inc(vec_ready, 1)
            act.wait_ge(bo_ps, 1)
            act.activation(bo_eff[:], bank(1)[:, 0:1], ACT.Identity, bias=vec[:, R_BO:R_BO + 1])
            act.wait_ge(w_in, 16 * N_W)
            act.activation(w_qkv0[:, :, 3 * P], vec[:, R_BQ:R_BQ + PAIRS0], ACT.Copy)
            act.activation(w_qkv0[:, :, 3 * P + 1], vec[:, R_BK:R_BK + PAIRS0], ACT.Copy)
            act.sem_inc(a_xt, FREE)
            with act.Fori(0, NC) as c:
                act.wait_ge(a_tr, c + 1 + FREE)
                apart(act)
                act.activation(xT[:, bass.ds(c * CH * P, CH * P)], bank(0), ACT.Identity,
                               scale=vec[:, R_LN1W:R_LN1W + 1], bias=vec[:, R_LN1B:R_LN1B + 1]).then_inc(a_xt, 1)
            end_phase(act, 1)
            act.wait_ge(kz_zero, 1)

            def qk_evac(g, s):
                act.wait_ge(qk_ready, g + 1)
                act.activation(qT[s][:], bank(0)[:, 0:S], ACT.Identity, bias=wst[s][:, 3 * P:3 * P + 1])
                act.activation(kZ[s][0:64, 0, :], bank(0)[0:64, S:2 * S], ACT.Identity,
                               bias=wst[s][0:64, 3 * P + 1:3 * P + 2])
                act.activation(kZ[s][64:P, 1, :], bank(0)[64:P, S:2 * S], ACT.Identity,
                               bias=wst[s][64:P, 3 * P + 1:3 * P + 2]).then_inc(qk_sb, 1)

            def exps(g, s):
                act.wait_ge(negmax_ready, g + 1)
                for t in range(TB):
                    for h in range(2):
                        last = act.activation(pr[s][:, t, h, :], bank(2 + t)[:, h * S:(h + 1) * S], ACT.Exp,
                                              bias=nb[s][:, 2 * t + h:2 * t + h + 1], scale=DH ** -0.5,
                                              accum_out=sm[s][:, 2 * t + h:2 * t + h + 1])
                last.then_inc(exp_ready, 1)

            def pt_evac(g, s):
                act.wait_ge(pT_ready[0], g + 1)
                act.wait_ge(z_ready, g + FREE)
                act.activation(pt[0][:], bank(4), ACT.Copy).then_inc(pt_sb[0], 1)

            def z_evac(g, s):
                act.wait_ge(z_ready, g + 1 + FREE)
                apart(act)
                act.activation(zT[:, g, :], bank(6)[:, 0:S], ACT.Copy).then_inc(z_sb, 1)

            act.sem_inc(qk_sb, 2)
            act.sem_inc(z_sb, FREE)
            act.sem_inc(exp_ready, FREE)

            def slot(g, s):
                if not isinstance(g, int) or g >= 0:
                    pt_evac(g, s)
                if not isinstance(g, int) or 0 <= g + 1 < SLOTS:
                    exps(g + 1, 1 - s)
                if not isinstance(g, int) or g >= 0:
                    z_evac(g, s)
                if not isinstance(g, int) or g + 2 < SLOTS:
                    qk_evac(g + 2, s)

            run_slots(act, slot)
            end_phase(act, 2)
            act.sem_inc(c_oT, FREE)
            with act.Fori(0, NC) as c:
                act.wait_ge(c_o, c + 1)
                act.activation(oT[:], bank(0), ACT.Identity, bias=bo_eff[:]).then_inc(c_oT, 1)
                act.wait_ge(c_xtps, c + 1)
                act.activation(xt1c[:], bank(2), ACT.Copy)
                act.activation(xT[:, bass.ds(c * CH * P, CH * P)], bank(2), ACT.Copy).then_inc(c_xt, 1)
                act.wait_ge(c_sub, c + 1)
                act.activation(ex[:], lg[:], ACT.Exp).then_inc(c_exp, 1)
                act.wait_ge(c_ctps, c + 1)
                act.activation(combT[:], bank(4)[0:NE, :], ACT.Copy).then_inc(c_ct, 1)
            end_phase(act, 3)
            act.sem_inc(g_ready, 2)

            def gelu(n, u, e):
                if u % NC == 0:
                    act.activation(b1x[u // NC], vec[:, bass.ds(e * KE + R_B1, KE)], ACT.Copy)
                    act.drain()
                act.wait_ge(u_ready, n + 1)
                act.wait_ge(y_ready, n + 1)
                for kt in range(KE):
                    last = act.activation(gE[u % 2][:, kt, :], bank(2 * (u % 2) + kt), ACT.Gelu,
                                          bias=b1x[u // NC][:, kt:kt + 1])
                last.then_inc(g_ready, 1)

            with act.Fori(0, NE // 2) as i:
                for u in range(2 * NC):
                    gelu(i * 2 * NC + u, u, i * 2 + u // NC)
            end_phase(act, 4)
            with act.Fori(0, B // 2) as i:
                for s in range(2):
                    act.wait_ge(e_x2, i * 2 + s + 1)
                    for t in range(TB):
                        last = act.activation(sqj[s][:, t, :], x2[s][:, t, :], ACT.Square,
                                              accum_out=ssq[s][:, t:t + 1])
                    last.then_inc(e_ssq, 1)
                for s in range(2):
                    act.wait_ge(e_xnps, i * 2 + s + 1)
                    act.activation(xnT[s][:], bank(s), ACT.Copy).then_inc(e_xn, 1)
                for s in range(2):
                    act.wait_ge(e_sim, i * 2 + s + 1)
                    act.activation(rel[s][:], bank(2 + s), ACT.Relu).then_inc(e_rel, 1)
                for s in range(2):
                    act.wait_ge(e_ctr, i * 2 + s + 1)
                    act.activation(zb[s][:], bank(4 + s)[:, 0:S], ACT.Identity, bias=vec[:, R_CB1:R_CB1 + 1])
                act.drain()
                for s in range(2):
                    act.activation(az[s][:], zb[s][:], ACT.Abs)
                act.drain()
                for s in range(2):
                    act.activation(az[s][:], az[s][:], ACT.Exp, scale=-1.0)
                act.drain()
                for s in range(2):
                    act.activation(az[s][:], az[s][:], ACT.Ln, bias=onecol[:]).then_inc(e_log, 1)
                for s in range(2):
                    act.wait_ge(e_o, i * 2 + s + 1)
                    act.activation(oE[s][:], bank(6 + s)[:, 0:S], ACT.Copy).then_inc(e_osb, 1)
            end_phase(act, 5)
            act.wait_ge(f_zero, 1)
            for la in range(LAYERS):
                with act.Fori(0, B // 2) as i:
                    n0 = i * 2 + la * B
                    it = i + la * (B // 2)
                    for s in range(2):
                        act.wait_ge(f_xcT, n0 + s + 1)
                        act.activation(hT[s][0:64, :], bank(s)[0:64, 0:S], ACT.Copy)
                        act.activation(hT[s][64:P, 1:S], bank(s)[64:P, 0:S - 1], ACT.Copy).then_inc(f_hT, 1)
                    for s in range(2):
                        for t in range(TB):
                            m = (n0 + s) * 2 + t
                            act.wait_ge(f_qkv, m + 1)
                            for j in range(2):
                                act.activation(sq1[t][:, j * INNER:(j + 1) * INNER], bank(2 + 3 * t + j), ACT.Square)
                            act.activation(v1[s][:, t, :], bank(4 + 3 * t), ACT.Copy).then_inc(f_sq, 1)
                    for s in range(2):
                        for u in range(4):
                            act.wait_ge(f_trps, (n0 + s) * 4 + u + 1 + FREE)
                            src = bank(u % 2).rearrange("p (a n) -> p a n", a=2)
                            a = 2 * (u % 2)
                            if u < 2:
                                act.activation(q1T[s][:, a:a + 2, :], src, ACT.Copy).then_inc(f_trsb, 1)
                            else:
                                act.activation(k1Z[s][0:64, a:a + 2, 0, :], src[0:64], ACT.Copy)
                                act.activation(k1Z[s][64:P, a:a + 2, 1, :], src[64:P], ACT.Copy).then_inc(f_trsb, 1)

                    def expo(j):
                        s, a = j % 2, j // 2
                        act.wait_ge(f_nb, it * 8 + j + 1)
                        sbank = [(2, 3), (0, 1)][s]
                        for t in range(TB):
                            for h in range(2):
                                if t == 0:
                                    o, src = p0[s][:, h, :], bank(sbank[0])[:, h * P:(h + 1) * P]
                                else:
                                    o, src = p1[s][:, h, WIN:S], bank(sbank[1])[:, h * 192:(h + 1) * 192]
                                last = act.activation(o, src, ACT.Exp, bias=nb1[s][:, t, h:h + 1],
                                                      scale=rq8[s][:, t, 2 * a + h:2 * a + h + 1],
                                                      accum_out=sm1[s][:, t, h:h + 1])
                        last.then_inc(f_e, 1)

                    expo(0)
                    for j in range(8):
                        s, a = j % 2, j // 2
                        if j < 7:
                            expo(j + 1)
                        act.wait_ge(f_t, it * 8 + j + 1)
                        act.activation(pt1[0][:], bank(4)[:, 0:3 * P], ACT.Copy).then_inc(f_pt0, 1)
                        act.wait_ge(f_z, it * 8 + j + 1)
                        act.activation(oT1[s][:, a, :], bank(6)[:, 0:S], ACT.Copy).then_inc(f_zsb, 1)
                    for s in range(2):
                        act.wait_ge(f_wo, n0 + s + 1)
                        act.activation(yT[s][:], bank(7 - s)[:, 0:S], ACT.Copy).then_inc(f_wosb, 1)
                    for s in range(2):
                        act.wait_ge(f_sh, n0 + s + 1)
                        act.activation(hb[s][:, :, 64:P], bank(4 + s)[:, 0:P].rearrange("p (t k) -> p t k", t=TB), ACT.Copy)
                        act.activation(hb[s][:, :, 0:64], xm[s][:, :, 0:64], ACT.Copy).then_inc(f_hb, 1)
                    for s in range(2):
                        act.wait_ge(f_h2ps, n0 + s + 1)
                        act.activation(h2T[s][:], bank(4 + s)[:, S:2 * S], ACT.Identity,
                                       scale=vec[:, R_LG + la:R_LG + la + 1],
                                       bias=vec[:, R_LB + la:R_LB + la + 1]).then_inc(f_h2, 1)
                    for s in range(2):
                        act.wait_ge(f_g, n0 + s + 1)
                        for c, (o, w) in enumerate(FCH):
                            r = R_FB1 + 6 * la + 3 + c
                            last = act.activation(gl[s][0:w, c, :], bank(2 + c // 2)[0:w, (c % 2) * S:(c % 2 + 1) * S],
                                                  ACT.Gelu, bias=vec[0:w, r:r + 1])
                        last.then_inc(f_gl, 1)
                    for s in range(2):
                        act.wait_ge(f_w2, n0 + s + 1)
                        act.activation(fT[s][:], bank(7 - s)[:, 0:S], ACT.Identity,
                                       bias=vec[:, R_B2 + la:R_B2 + la + 1]).then_inc(f_w2sb, 1)

        @block.tensor
        def _(pe):
            pe.wait_ge(const_ready, 1)
            pe.wait_ge(rows_in, 16 * N_ROWS)
            pe.transpose(bank(0)[:, 0:P], vrows[:], ident[:]).then_inc(vec_ps, 1)
            pe.wait_ge(vec_ready, 1)
            pe.wait_ge(w_in, 16 * N_W)
            for a in range(PAIRS0):
                mm = pe.matmul(bank(1)[:, 0:1], w_o0[:, a, :], vec[:, R_BV + a:R_BV + a + 1],
                               start=(a == 0), stop=(a == PAIRS0 - 1))
            mm.then_inc(bo_ps, 1)
            pe.sem_inc(a_tr, FREE)
            with pe.Fori(0, NC) as c:
                pe.wait_ge(a_xn, c + 1)
                pe.wait_ge(a_xt, c + FREE)
                for t in range(CH):
                    mm = pe.transpose(bank(0)[:, t * P:(t + 1) * P], xn[:, t, :], ident[:])
                mm.then_inc(a_tr, 1)
            end_phase(pe, 1)
            pe.wait_ge(s0_zero, 1)
            pe.sem_inc(v_ready, 2)
            pe.sem_inc(z_ready, FREE)

            def project(g, s, turn):
                pe.wait_ge(w_staged[s], (turn + 1) * 16)
                pe.wait_ge(x_staged[s], (turn + 1) * 16)
                pe.wait_ge(qk_sb, g + 1 + FREE)
                for j in range(2):
                    mm = pe.matmul(bank(0)[:, j * S:(j + 1) * S], wst[s][:, j * P:(j + 1) * P], xst[s][:],
                                   start=True, stop=True)
                mm.then_inc(qk_ready, 1)
                pe.wait_ge(v_sb, g + FREE)
                for t in range(TB):
                    mm = pe.matmul(bank(1)[:, t * P:(t + 1) * P], xst[s][:, t * P:(t + 1) * P],
                                   wst[s][:, 2 * P:3 * P], start=True, stop=True)
                mm.then_inc(v_ready, 1)

            def scores(g, s):
                pe.wait_ge(qk_sb, g + 1 + 2)
                pe.wait_ge(exp_ready, g + FREE)
                pe.matmul(bank(2).rearrange("p (h n) -> p h n", h=2)[:, :, 0:P], qT[s][:, 0:P],
                          kZ[s][:, :, 0:P], start=True, stop=True)
                pe.matmul(bank(3), qT[s][:, P:S], kZ[s][:].rearrange("p h n -> p (h n)"),
                          start=True, stop=True).then_inc(scores_ready, 1)

            def turn_probs(g, s):
                pe.wait_ge(probs_ready, g + 1)
                for h in range(2):
                    pe.wait_ge(pt_sb[h], g + FREE)
                    for kt in range(TB):
                        for t in range(TB):
                            mm = pe.transpose(bank(4 + h)[:, kt * S + t * P:kt * S + (t + 1) * P],
                                              pr[s][:, t, h, kt * P:(kt + 1) * P], ident[:])
                    mm.then_inc(pT_ready[h], 1)

            def values(g, s):
                pe.wait_ge(pt_sb[0], g + 1 + FREE)
                pe.wait_ge(pt_sb[1], g + 1 + FREE)
                pe.wait_ge(v_sb, g + 1 + FREE)
                pe.wait_ge(z_sb, g + FREE)
                for kt in range(TB):
                    for h in range(2):
                        mm = pe.matmul(bank(6)[h * 64:(h + 1) * 64, 0:S], vS[s][:, kt, h * 64:(h + 1) * 64],
                                       pt[h][:, kt * S:(kt + 1) * S], start=(kt == 0), stop=(kt == TB - 1))
                mm.then_inc(z_ready, 1)

            pe.wait_ge(phase_done, 4)

            def slot(g, s):
                full = not isinstance(g, int)
                if full or g >= 0:
                    turn_probs(g, s)
                if full or g + 2 < SLOTS:
                    project(g + 2, s, turn_of(g, s) + 1)
                if full or g >= 0:
                    values(g, s)
                if full or g + 2 < SLOTS:
                    scores(g + 2, s)

            def turn_of(g, s):
                return g // 2 if isinstance(g, int) else half[0]

            half = [None]
            for g in (-2, -1):
                slot(g, g % 2)
            with pe.Fori(0, SLOTS // 2 - 1) as i:
                half[0] = i
                for s in range(2):
                    slot(i * 2 + s, s)
            for g in (SLOTS - 2, SLOTS - 1):
                slot(g, g % 2)
            end_phase(pe, 2)
            zT4 = big[:, :].rearrange("p (b a n) -> p b a n", b=B, a=PAIRS0)
            pe.sem_inc(c_tr, FREE)
            with pe.Fori(0, NC) as c:
                pe.wait_ge(c_oT, c + FREE)
                for a in range(PAIRS0):
                    mm = pe.matmul(bank(0), w_o0[:, a, :], zT4[:, bass.ds(c * 2, 2), a, :],
                                   start=(a == 0), stop=(a == PAIRS0 - 1))
                mm.then_inc(c_o, 1)
                pe.wait_ge(c_oT, c + 1 + FREE)
                for t in range(CH):
                    mm = pe.transpose(bank(1)[:, t * P:(t + 1) * P], oT[:, t * P:(t + 1) * P], ident[:])
                mm.then_inc(c_tr, 1)
                pe.wait_ge(c_x1, c + 1)
                for t in range(CH):
                    mm = pe.transpose(bank(2)[:, t * P:(t + 1) * P], x1c[:, t, :], ident[:])
                mm.then_inc(c_xtps, 1)
                pe.wait_ge(c_xt, c + 1)
                for t in range(CH):
                    mm = pe.matmul(bank(3)[:, t * NE:(t + 1) * NE], xt1c[:, t * P:(t + 1) * P], w_r[:],
                                   start=True, stop=True)
                mm.then_inc(c_lg, 1)
                pe.wait_ge(c_comb, c + 1)
                for t in range(CH):
                    mm = pe.transpose(bank(4)[0:NE, t * P:(t + 1) * P], combc[:, t, :], ident[:])
                mm.then_inc(c_ctps, 1)
                pe.wait_ge(c_ct, c + 1)
                for t in range(CH):
                    mm = pe.matmul(bank(5)[:, t * P:(t + 1) * P], combT[:, t * P:(t + 1) * P], b2e[:],
                                   start=True, stop=True)
                mm.then_inc(c_yb, 1)
            end_phase(pe, 3)
            pe.sem_inc(y_ready, 2)

            def up(n, u, turn):
                if u % NC == 0:
                    pe.wait_ge(we_in[u // NC % 2], (turn + 1) * 32)
                pe.wait_ge(g_ready, n + 1)
                for kt in range(KE):
                    mm = pe.matmul(bank(2 * (u % 2) + kt), w1e[u // NC % 2][:, kt * P:(kt + 1) * P],
                                   xT[:, (u % NC) * CH * P:(u % NC + 1) * CH * P], start=True, stop=True)
                mm.then_inc(u_ready, 1)

            def down(n, u):
                pe.wait_ge(g_ready, n + 1 + 2)
                pe.wait_ge(acc_done, n + 1)
                for t in range(CH):
                    for kt in range(KE):
                        mm = pe.matmul(bank(4 + u % 2)[:, t * P:(t + 1) * P], gE[u % 2][:, kt, t * P:(t + 1) * P],
                                       w2e[u // NC][:, kt, :], start=(kt == 0), stop=(kt == KE - 1))
                mm.then_inc(y_ready, 1)

            up(0, 0, 0)
            with pe.Fori(0, NE // 2 - 1) as i:
                for u in range(2 * NC):
                    up(i * 2 * NC + u + 1, u + 1, i + (u + 1) // (2 * NC))
                    down(i * 2 * NC + u, u)
            for u in range(2 * NC):
                n = (NE // 2 - 1) * 2 * NC + u
                if u + 1 < 2 * NC:
                    up(n + 1, u + 1, NE // 2 - 1)
                down(n, u)
            end_phase(pe, 4)
            with pe.Fori(0, B // 2) as i:
                for s in range(2):
                    pe.wait_ge(e_nrm, i * 2 + s + 1)
                    for t in range(TB):
                        pe.transpose(bank(s)[:, t * P:(t + 1) * P], x2[s][:, t, :], ident[:])
                        mm = pe.transpose(bank(s)[:, S + t * P:S + (t + 1) * P], nrm[s][:, t, :], ident[:])
                    mm.then_inc(e_xnps, 1)
                for s in range(2):
                    pe.wait_ge(e_xn, i * 2 + s + 1)
                    for t in range(TB):
                        mm = pe.matmul(bank(2 + s)[:, t * S:(t + 1) * S], xnT[s][:, S + t * P:S + (t + 1) * P],
                                       xnT[s][:, S:2 * S], start=True, stop=True)
                    mm.then_inc(e_sim, 1)
                for s in range(2):
                    pe.wait_ge(e_rel, i * 2 + s + 1)
                    for t in range(TB):
                        mm = pe.matmul(bank(4 + s)[:, 0:S], w1c[:], rel[s][:, t * S:(t + 1) * S],
                                       start=(t == 0), stop=(t == TB - 1))
                    mm.then_inc(e_ctr, 1)
                for s in range(2):
                    pe.wait_ge(e_sp, i * 2 + s + 1)
                    pe.matmul(bank(6 + s)[:, 0:S], w2c[:, 0, :], xnT[s][:, 0:S], start=True, stop=False)
                    pe.matmul(bank(6 + s)[:, 0:S], w2c[:, 1, :], sp[s][:], start=False, stop=True).then_inc(e_o, 1)
                for s in range(2):
                    pe.wait_ge(e_osb, i * 2 + s + 1)
                    for t in range(TB):
                        mm = pe.transpose(bank(6 + s)[:, S + t * P:S + (t + 1) * P], oE[s][:, t * P:(t + 1) * P], ident[:])
                    mm.then_inc(e_oT, 1)
                pe.wait_ge(e_x3, i * 2 + 2)
            end_phase(pe, 5)
            pe.wait_ge(f_zero, 1)
            pe.sem_inc(f_trps, FREE)
            for la in range(LAYERS):
                with pe.Fori(0, B // 2) as i:
                    n0 = i * 2 + la * B
                    it = i + la * (B // 2)
                    for s in range(2):
                        pe.wait_ge(f_xc, n0 + s + 1)
                        for t in range(TB):
                            mm = pe.transpose(bank(s)[:, t * P:(t + 1) * P], xc[s][:, t, :], ident[:])
                        mm.then_inc(f_xcT, 1)
                    for s in range(2):
                        pe.wait_ge(f_hT, n0 + s + 1)
                        for t in range(TB):
                            if s == 1:
                                pe.wait_ge(f_rot, n0 * 2 + t + 1)
                            for j in range(3):
                                mm = pe.matmul(bank(2 + 3 * t + j), hT[s][:, t * P:(t + 1) * P],
                                               wqkv1[:, la, j * INNER:(j + 1) * INNER], start=True, stop=True)
                            mm.then_inc(f_qkv, 1)
                    for s in range(2):
                        pe.wait_ge(f_kn, n0 + s + 1)
                        for u in range(4):
                            if s == 1 or u >= 2:
                                pe.wait_ge(f_trsb, n0 * 4 + s * 4 + u - 1)
                            j, a = u // 2, 2 * (u % 2)
                            for b_ in range(2):
                                for t in range(TB):
                                    o = j * INNER + (a + b_) * P
                                    mm = pe.transpose(bank(u % 2)[:, b_ * S + t * P:b_ * S + (t + 1) * P],
                                                      qk[t][:, o:o + P], ident[:])
                            mm.then_inc(f_trps, 1)

                    def sc(j):
                        s, a = j % 2, j // 2
                        sbank = [(2, 3), (0, 1)][s]
                        if j == 0:
                            pe.wait_ge(f_trsb, n0 * 4 + 8)
                            pe.wait_ge(f_rot, n0 * 2 + 4)
                        if j >= 2:
                            pe.wait_ge(f_e, it * 8 + j - 1)
                        o = bank(sbank[0])[:, 0:2 * P].rearrange("p (h n) -> p h n", h=2)
                        pe.matmul(o, q1T[s][:, a, 0:P], k1Z[s][:, a, :, 0:P], start=True, stop=False)
                        pe.matmul(o, identb[:], band0[:], start=False, stop=True)
                        o = bank(sbank[1])[:, 0:384].rearrange("p (h n) -> p h n", h=2)
                        pe.matmul(o, q1T[s][:, a, P:S], k1Z[s][:, a, :, WIN:S], start=True, stop=False)
                        pe.matmul(o, identb[:], band1[:], start=False, stop=True).then_inc(f_s, 1)

                    sc(0)
                    for j in range(8):
                        s, a = j % 2, j // 2
                        if j < 7:
                            sc(j + 1)
                        pe.wait_ge(f_p, it * 8 + j + 1)
                        if j:
                            pe.wait_ge(f_pt0, it * 8 + j)
                            pe.wait_ge(f_pt1, it * 8 + j)
                        for h in range(2):
                            pe.transpose(bank(4 + h)[:, 0:P], p0[s][:, h, :], ident[:])
                            for kt in range(TB):
                                mm = pe.transpose(bank(4 + h)[:, (kt + 1) * P:(kt + 2) * P],
                                                  p1[s][:, h, kt * P:(kt + 1) * P], ident[:])
                        mm.then_inc(f_t, 1)
                        pe.wait_ge(f_pt0, it * 8 + j + 1)
                        pe.wait_ge(f_pt1, it * 8 + j + 1)
                        if j:
                            pe.wait_ge(f_zsb, it * 8 + j)
                        for h in range(2):
                            v = v1[s][:, :, (2 * a + h) * DH:(2 * a + h + 1) * DH]
                            o = bank(6)[h * 64:(h + 1) * 64]
                            pe.matmul(o[:, 0:S], v[:, 0, :], pt1[h][:, 0:S], start=True, stop=False,
                                      skip_group_check=True)
                            mm = pe.matmul(o[:, P:S], v[:, 1, :], pt1[h][:, S:3 * P], start=False, stop=True,
                                           skip_group_check=True)
                        mm.then_inc(f_z, 1)
                    pe.wait_ge(f_zsb, it * 8 + 8)
                    for s in range(2):
                        for a in range(PAIRS1):
                            mm = pe.matmul(bank(7 - s)[:, 0:S], wo1[:, la, a, :], oT1[s][:, a, :],
                                           start=(a == 0), stop=(a == PAIRS1 - 1))
                        mm.then_inc(f_wo, 1)
                    for s in range(2):
                        pe.wait_ge(f_wosb, n0 + s + 1)
                        for t in range(TB):
                            mm = pe.transpose(bank(7 - s)[:, S + t * P:S + (t + 1) * P], yT[s][:, t * P:(t + 1) * P], ident[:])
                        mm.then_inc(f_woT, 1)
                    for s in range(2):
                        pe.wait_ge(f_xm, n0 + s + 1 + 2)
                        pe.matmul(bank(4 + s)[:, 0:P].rearrange("p (t k) -> p t k", t=TB), shift[:],
                                  xm[s][:, :, 64:P], start=True, stop=False, skip_group_check=True)
                        pe.matmul(bank(4 + s)[:, 64:P], carry[:], xm[s][:, 0, 64:P], start=False,
                                  stop=True, skip_group_check=True).then_inc(f_sh, 1)
                    for s in range(2):
                        pe.wait_ge(f_hn, n0 + s + 1)
                        for t in range(TB):
                            mm = pe.transpose(bank(4 + s)[:, S + t * P:S + (t + 1) * P], hb[s][:, t, :], ident[:])
                        mm.then_inc(f_h2ps, 1)
                    for s in range(2):
                        pe.wait_ge(f_h2, n0 + s + 1)
                        if s == 1:
                            pe.wait_ge(f_gl, n0 + 1)
                        for half_, sm_, b0 in ((1, f_g, 2), (0, f_a, 0)):
                            if half_ == 0 and s == 1:
                                pe.wait_ge(f_hg, n0 + 1)
                            for c, (o, w) in enumerate(FCH):
                                mm = pe.matmul(bank(b0 + c // 2)[0:w, (c % 2) * S:(c % 2 + 1) * S],
                                               wf1[:, la, half_ * HID + o:half_ * HID + o + w], h2T[s][:],
                                               start=True, stop=True)
                            mm.then_inc(sm_, 1)
                    for s in range(2):
                        pe.wait_ge(f_hg, n0 + s + 1)
                        for c, (o, w) in enumerate(FCH):
                            mm = pe.matmul(bank(7 - s)[:, 0:S], wf2[0:w, la, c, :], hg[s][0:w, c, :],
                                           start=(c == 0), stop=(c == 2))
                        mm.then_inc(f_w2, 1)
                    for s in range(2):
                        pe.wait_ge(f_w2sb, n0 + s + 1)
                        for t in range(TB):
                            mm = pe.transpose(bank(7 - s)[:, S + t * P:S + (t + 1) * P], fT[s][:, t * P:(t + 1) * P], ident[:])
                        mm.then_inc(f_w2T, 1)
                    pe.wait_ge(f_x, n0 + 2 + FREE)

        @block.vector
        def _(dve):
            def ln_stats(src, n, k, ready):
                for t in range(n):
                    dve.bn_stats(st[:, k, t, :], src(t))
                dve.drain()
                for t in range(n):
                    dve.bn_aggr(mv[:, k, t, :], st[:, k, t, :])
                dve.drain()
                dve.tensor_scalar(ve[:, k, 0:n], mv[:, k, 0:n, 1], EPS, None, ALU.add).then_inc(ready, 1)

            def ln_apply(dst, src, n, k):
                for t in range(n):
                    last = dve.tensor_scalar(dst(t), src(t), mv[:, k, t, 0:1], rstd[:, k, t:t + 1],
                                             ALU.subtract, ALU.mult)
                return last

            dve.memset(vrows[:], 0.0).then_inc(rows_zero, 1)
            dve.wait_ge(w_in, 16 * N_W)
            for la in range(LAYERS):
                for j in range(2):
                    for t in range(TB):
                        dve.tensor_tensor(rot[:, la, 2 * j, t, :], tab[:, 2 * j, t, :], qks[:, j, la, :], ALU.mult)
                        for a, b_ in ((0, 32), (32, 0)):
                            dve.tensor_tensor(rot[:, la, 2 * j + 1, t, a:a + 32], tab[:, 2 * j + 1, t, a:a + 32],
                                              qks[:, j, la, b_:b_ + 32], ALU.mult)
            dve.wait_ge(x_in, 16)
            with dve.Fori(0, NC) as c:
                ln_stats(lambda t: x0[:, c * CH + t, :], CH, 0, a_var)
                dve.wait_ge(a_rstd, c + 1)
                dve.wait_ge(a_tr, c + FREE)
                ln_apply(lambda t: xn[:, t, :], lambda t: x0[:, c * CH + t, :], CH, 0).then_inc(a_xn, 1)
            end_phase(dve, 1)
            dve.memset(bank(2).rearrange("p (h n) -> p h n", h=2)[:, :, P:S], 0.0).then_inc(s0_zero, 1)
            dve.sem_inc(v_sb, FREE)
            dve.sem_inc(pt_sb[0], FREE)
            dve.sem_inc(pt_sb[1], FREE)
            mask = causal[:].unsqueeze(1).to_broadcast([P, 2, P])

            def negmax(g, s):
                dve.wait_ge(scores_ready, g + 1)
                for t in range(TB):
                    d = bank(2 + t).rearrange("p (h n) -> p h n", h=2)[:, :, t * P:(t + 1) * P]
                    dve.tensor_tensor(d, d, mask, ALU.mult)
                dve.drain()
                dve.tensor_reduce(mx[:, 0:2], bank(2).rearrange("p (h n) -> p h n", h=2)[:, :, 0:P], AX.X, ALU.max)
                dve.tensor_reduce(mx[:, 2:4], bank(3).rearrange("p (h n) -> p h n", h=2), AX.X, ALU.max)
                dve.drain()
                dve.tensor_scalar(nb[s][:, 0:2], mx[:, 0:2], -DH ** -0.5, 0.0, ALU.mult, ALU.min)
                dve.tensor_scalar(nb[s][:, 2:4], mx[:, 2:4], -DH ** -0.5, None, ALU.mult).then_inc(negmax_ready, 1)

            def normalise(g, s):
                dve.wait_ge(exp_ready, g + 1 + FREE)
                dve.reciprocal(rs[:], sm[s][:])
                dve.drain()
                for t in range(TB):
                    for h in range(2):
                        last = dve.tensor_scalar(pr[s][:, t, h, :], pr[s][:, t, h, :], rs[:, 2 * t + h:2 * t + h + 1],
                                                 None, ALU.mult)
                last.then_inc(probs_ready, 1)

            def pt_evac(g, s):
                dve.wait_ge(pT_ready[1], g + 1)
                dve.wait_ge(z_ready, g + FREE)
                dve.tensor_copy(pt[1][:], bank(5)).then_inc(pt_sb[1], 1)

            def v_evac(g, s):
                dve.wait_ge(v_ready, g + 1 + 2)
                if not isinstance(g, int) or g >= 2:
                    dve.wait_ge(z_ready, g - 1 + FREE)
                dve.tensor_copy(vS[s][:].rearrange("p t n -> p (t n)"), bank(1)[:, 0:S]).then_inc(v_sb, 1)

            def slot(g, s):
                full = not isinstance(g, int)
                if full or 0 <= g + 1 < SLOTS:
                    negmax(g + 1, 1 - s)
                if full or g >= 0:
                    pt_evac(g, s)
                if full or 0 <= g + 1 < SLOTS:
                    normalise(g + 1, 1 - s)
                if full or g + 2 < SLOTS:
                    v_evac(g + 2, s)

            run_slots(dve, slot)
            end_phase(dve, 2)
            bc = lambda v, n: v.unsqueeze(2).to_broadcast([P, CH, n])
            with dve.Fori(0, NC) as c:
                x0c = x0[:, bass.ds(c * CH, CH), :]
                dve.wait_ge(c_tr, c + 1 + FREE)
                dve.tensor_tensor(mid[:], bank(1).rearrange("p (t d) -> p t d", t=CH), x0c, ALU.add)
                dve.drain().then_inc(c_mid, 1)
                ln_stats(lambda t: mid[:, t, :], CH, 0, c_var)
                dve.wait_ge(c_rstd, c * 2 + 1)
                ln_apply(lambda t: x1c[:, t, :], lambda t: mid[:, t, :], CH, 0)
                dve.drain()
                dve.tensor_tensor(x1c[:], x1c[:], ln2w[:].unsqueeze(1).to_broadcast([P, CH, D]), ALU.mult)
                dve.drain()
                dve.wait_ge(c_u, c + 1)
                dve.tensor_tensor(x1c[:], x1c[:], uC[:], ALU.add)
                dve.drain()
                ln_stats(lambda t: x1c[:, t, :], CH, 1, c_var)
                dve.wait_ge(c_rstd, c * 2 + 2)
                ln_apply(lambda t: x1c[:, t, :], lambda t: x1c[:, t, :], CH, 1).then_inc(c_x1, 1)
                dve.wait_ge(c_lg, c + 1)
                dve.tensor_tensor(lg[:], bank(3)[:, 0:CH * NE].rearrange("p (t e) -> p t e", t=CH),
                                  br[:].unsqueeze(1).to_broadcast([P, CH, NE]), ALU.add)
                dve.drain()
                dve.tensor_reduce(r4[:], lg[:], AX.X, ALU.max)
                dve.drain()
                dve.tensor_tensor(lg[:], lg[:], bc(r4[:], NE), ALU.subtract).then_inc(c_sub, 1)
                dve.wait_ge(c_exp, c + 1)
                dve.tensor_reduce(r4[:], ex[:], AX.X, ALU.add)
                dve.drain()
                dve.reciprocal(r4[:], r4[:])
                dve.drain()
                dve.tensor_tensor(ex[:], ex[:], bc(r4[:], NE), ALU.mult)
                dve.drain()
                for t in range(CH):
                    dve.max(m8[:, t, :], ex[:, t, :])
                dve.drain()
                dve.tensor_copy(top2[:, :, 0:2], m8[:, :, 0:2])
                dve.tensor_tensor(r4[:], m8[:, :, 0], m8[:, :, 1], ALU.add)
                dve.drain()
                dve.tensor_scalar(r4[:], r4[:], 1e-9, None, ALU.max)
                for t in range(CH):
                    dve.match_replace(rest[:, t, :], top2[:, t, :], ex[:, t, :], 0.0)
                dve.drain()
                dve.reciprocal(r4[:], r4[:])
                dve.tensor_tensor(rest[:], ex[:], rest[:], ALU.subtract)
                dve.drain()
                dve.tensor_tensor(combc[:], rest[:], bc(r4[:], NE), ALU.mult)
                dve.tensor_tensor(comb[:, bass.ds(c * CH, CH), :], rest[:], bc(r4[:], NE), ALU.mult).then_inc(c_comb, 1)
                dve.wait_ge(c_yb, c + 1)
                dve.scalar_tensor_tensor(acc[:, bass.ds(c * CH, CH), :].rearrange("p t d -> p (t d)"),
                                         x1c[:].rearrange("p t d -> p (t d)"), 2.0, bank(5),
                                         ALU.mult, ALU.add).then_inc(c_acc, 1)
                dve.drain()
            end_phase(dve, 3)
            dve.sem_inc(acc_done, 2)
            with dve.Fori(0, NE // 2) as i:
                for u in range(2 * NC):
                    dve.wait_ge(y_ready, i * 2 * NC + u + 1 + 2)
                    for t in range(CH):
                        tt = (u % NC) * CH + t
                        last = dve.scalar_tensor_tensor(
                            acc[:, tt, :], bank(4 + u % 2)[:, t * P:(t + 1) * P],
                            comb[:, tt, bass.ds(i * 2 + u // NC, 1)], acc[:, tt, :], ALU.mult, ALU.add)
                    dve.drain().then_inc(acc_done, 1)
            end_phase(dve, 4)
            with dve.Fori(0, B // 2) as i:
                b0 = i * 4
                for s in range(2):
                    ln_stats(lambda t: acc[:, b0 + (2 * s + t), :], TB, s, e_var)
                for s in range(2):
                    dve.wait_ge(e_rstd, i * 4 + s + 1)
                    ln_apply(lambda t: x2[s][:, t, :], lambda t: acc[:, b0 + (2 * s + t), :], TB, s).then_inc(e_x2, 1)
                for s in range(2):
                    dve.wait_ge(e_ssq, i * 2 + s + 1)
                    dve.tensor_scalar(mq[s][:], ssq[s][:], 1e-12, None, ALU.max).then_inc(e_mq, 1)
                dve.drain()
                for s in range(2):
                    dve.wait_ge(e_rn, i * 2 + s + 1)
                    for t in range(TB):
                        last = dve.tensor_scalar(nrm[s][:, t, :], x2[s][:, t, :], rn[s][:, t:t + 1], None, ALU.mult)
                    last.then_inc(e_nrm, 1)
                for s in range(2):
                    dve.wait_ge(e_log, i * 2 + s + 1)
                    dve.scalar_tensor_tensor(sp[s][:], zb[s][:], 0.0, az[s][:], ALU.max, ALU.add).then_inc(e_sp, 1)
                for s in range(2):
                    dve.wait_ge(e_oT, i * 2 + s + 1)
                    dve.tensor_tensor(x2[s][:], x2[s][:], bank(6 + s)[:, S:2 * S].rearrange("p (t d) -> p t d", t=TB), ALU.add)
                    dve.drain()
                    ln_stats(lambda t: x2[s][:, t, :], TB, s, e_var)
                for s in range(2):
                    dve.wait_ge(e_rstd, i * 4 + s + 3)
                    ln_apply(lambda t: x3[:, b0 + (2 * s + t), :], lambda t: x2[s][:, t, :], TB, s).then_inc(e_x3, 1)
                dve.drain()
            end_phase(dve, 5)
            dve.wait_ge(f_zero, 1)
            dve.sem_inc(f_xm, 2)
            dve.sem_inc(f_x, FREE)
            for la in range(LAYERS):
                dst = (x4, x5)[la]
                with dve.Fori(0, B // 2) as i:
                    n0 = i * 2 + la * B
                    it = i + la * (B // 2)
                    for s in range(2):
                        for t in range(TB):
                            dve.wait_ge(f_sq, (n0 + s) * 2 + t + 1)
                            if s == 1:
                                dve.wait_ge(f_add, (n0 + s) * 2 + t - 1)
                            dve.tensor_reduce(ss[s][:, t, :], sq1[t].rearrange("p (h k) -> p h k", k=DH), AX.X, ALU.add)
                            for j in range(2):
                                src = bank(2 + 3 * t + j).rearrange("p (h k) -> p h k", k=DH)
                                o1 = t1[t][:, j * INNER:(j + 1) * INNER].rearrange("p (h k) -> p h k", k=DH)
                                o2 = t2[t][:, j * INNER:(j + 1) * INNER].rearrange("p (h k) -> p h k", k=DH)
                                ca = rot[:, la, 2 * j, t, :].unsqueeze(1).to_broadcast([P, H1, DH])
                                cb = rot[:, la, 2 * j + 1, t, :].unsqueeze(1).to_broadcast([P, H1, DH])
                                dve.tensor_tensor(o1, src, ca, ALU.mult)
                                dve.tensor_tensor(o2[:, :, 0:32], src[:, :, 32:64], cb[:, :, 0:32], ALU.mult)
                                last = dve.tensor_tensor(o2[:, :, 32:64], src[:, :, 0:32], cb[:, :, 32:64], ALU.mult)
                            last.then_inc(f_rot, 1)
                        dve.drain()
                        x_ = ss[s][:]
                        y_ = rqk[s][:]
                        dve.tensor_scalar(x_, x_, 1e-24, None, ALU.max)
                        dve.drain()
                        dve.tensor_scalar(yi[:], x_.bitcast(I32), 1, None, ALU.logical_shift_right)
                        dve.drain()
                        dve.tensor_scalar(y_.bitcast(I32), yi[:], -1.0, float(0x5f3759df), ALU.mult, ALU.add)
                        dve.drain()
                        for _ in range(3):
                            dve.tensor_tensor(ny[:], y_, y_, ALU.mult)
                            dve.drain()
                            dve.tensor_tensor(ny[:], ny[:], x_, ALU.mult)
                            dve.drain()
                            dve.tensor_scalar(ny[:], ny[:], -0.5, 1.5, ALU.mult, ALU.add)
                            dve.drain()
                            dve.tensor_tensor(y_, y_, ny[:], ALU.mult)
                            dve.drain()
                        dve.tensor_scalar(rq8[s][:], rqk[s][:, :, 0:H1], 8.0, None, ALU.mult)
                        dve.tensor_scalar(nrq8[s][:], rqk[s][:, :, 0:H1], -8.0, None, ALU.mult).then_inc(f_rn, 1)
                    dve.drain()

                    def nmax(j):
                        s, a = j % 2, j // 2
                        sbank = [(2, 3), (0, 1)][s]
                        dve.wait_ge(f_s, it * 8 + j + 1)
                        dve.tensor_reduce(mx1[s][:, 0, :], bank(sbank[0])[:, 0:2 * P].rearrange("p (h n) -> p h n", h=2), AX.X, ALU.max)
                        dve.tensor_reduce(mx1[s][:, 1, :], bank(sbank[1])[:, 0:384].rearrange("p (h n) -> p h n", h=2), AX.X, ALU.max)
                        dve.drain()
                        dve.tensor_tensor(nb1[s][:], mx1[s][:], nrq8[s][:, :, 2 * a:2 * a + 2], ALU.mult).then_inc(f_nb, 1)

                    nmax(0)
                    for j in range(8):
                        s, a = j % 2, j // 2
                        if j < 7:
                            nmax(j + 1)
                        dve.wait_ge(f_e, it * 8 + j + 1)
                        dve.reciprocal(rs1[s][:], sm1[s][:])
                        dve.drain()
                        for h in range(2):
                            dve.tensor_scalar(p0[s][:, h, :], p0[s][:, h, :], rs1[s][:, 0, h:h + 1], None, ALU.mult)
                            last = dve.tensor_scalar(p1[s][:, h, WIN:S], p1[s][:, h, WIN:S], rs1[s][:, 1, h:h + 1], None, ALU.mult)
                        last.then_inc(f_p, 1)
                        dve.wait_ge(f_t, it * 8 + j + 1)
                        dve.tensor_copy(pt1[1][:], bank(5)[:, 0:3 * P]).then_inc(f_pt1, 1)
                    for s in range(2):
                        dve.wait_ge(f_woT, n0 + s + 1)
                        dve.tensor_tensor(xm[s][:], xc[s][:], bank(7 - s)[:, S:2 * S].rearrange("p (t d) -> p t d", t=TB), ALU.add).then_inc(f_xm, 1)
                    for s in range(2):
                        dve.wait_ge(f_hb, n0 + s + 1)
                        ln_stats(lambda t: hb[s][:, t, :], TB, s, f_var)
                    for s in range(2):
                        dve.wait_ge(f_rstd, n0 + s + 1 if la == 0 else i * 4 + (B + s + 1))
                        ln_apply(lambda t: hb[s][:, t, :], lambda t: hb[s][:, t, :], TB, s).then_inc(f_hn, 1)
                    for s in range(2):
                        dve.wait_ge(f_gl, n0 + s + 1)
                        dve.wait_ge(f_a, n0 + s + 1)
                        for c, (o, w) in enumerate(FCH):
                            r = R_FB1 + 6 * la + c
                            last = dve.scalar_tensor_tensor(
                                hg[s][0:w, c, :], bank(c // 2)[0:w, (c % 2) * S:(c % 2 + 1) * S], vec[0:w, r:r + 1],
                                gl[s][0:w, c, :], ALU.add, ALU.mult)
                        last.then_inc(f_hg, 1)
                    for s in range(2):
                        dve.wait_ge(f_w2T, n0 + s + 1)
                        res = bank(7 - s)[:, S:2 * S].rearrange("p (t d) -> p t d", t=TB)
                        if la == 0:
                            dve.tensor_tensor(dst[:, bass.ds(i * 4 + 2 * s, TB), :], xm[s][:], res, ALU.add).then_inc(f_x, 1)
                        else:
                            dve.tensor_tensor(xm[s][:], xm[s][:], res, ALU.add)
                            dve.drain()
                            dve.tensor_tensor(xm[s][:], xm[s][:], x3[:, bass.ds(i * 4 + 2 * s, TB), :], ALU.add)
                            dve.drain()
                            ln_stats(lambda t: xm[s][:, t, :], TB, s, f_var)
                    if la == LAYERS - 1:
                        for s in range(2):
                            dve.wait_ge(f_rstd, i * 4 + (B + 2 + s + 1))
                            ln_apply(lambda t: dst[:, i * 4 + (2 * s + t), :], lambda t: xm[s][:, t, :], TB, s).then_inc(f_x, 1)
                    dve.drain()


N_W = 24


_INS = ['L0_attn_resid_pre', 'L0_attn_W_Q', 'L0_attn_b_Q', 'L0_attn_W_K', 'L0_attn_b_K', 'L0_attn_W_V',
        'L0_attn_b_V', 'L0_attn_W_O', 'L0_attn_b_O', 'L0_attn_ln1_w', 'L0_attn_ln1_b', 'L0_attn_ln2_w',
        'L0_attn_ln2_b', 'L0_ffn_Wr', 'L0_ffn_br', 'L0_ffn_W1', 'L0_ffn_b1', 'L0_ffn_W2', 'L0_ffn_b2',
        'L1_attn_W1', 'L1_attn_b1', 'L1_attn_W2', 'L1_ffn_wqkv', 'L1_ffn_q_scale', 'L1_ffn_k_scale',
        'L1_ffn_wo', 'L1_ffn_ln_g', 'L1_ffn_ln_b', 'L1_ffn_w1', 'L1_ffn_b1', 'L1_ffn_w2', 'L1_ffn_b2']


def rotary_tables():
    import numpy as np
    half = np.arange(0, DH, 2, dtype=np.float32)
    inv = (1.0 / np.float32(10000.0) ** (half / np.float32(DH))).astype(np.float32)
    t = np.arange(S, dtype=np.float32)
    freqs = t[:, None] * inv[None, :]
    base = ((half + np.float32(0.4 * DH)) / np.float32(1.4 * DH)).astype(np.float32)
    power = ((t - S // 2) / np.float32(WIN // 2)).astype(np.float32)
    scale = (base[None, :] ** power[:, None]).astype(np.float32)
    cos, sin = np.cos(freqs), np.sin(freqs)
    return np.stack([np.concatenate([cos * scale, cos * scale], -1),
                     np.concatenate([-sin * scale, sin * scale], -1),
                     np.concatenate([cos / scale, cos / scale], -1),
                     np.concatenate([-sin / scale, sin / scale], -1)]).astype(np.float32)


def kernel(**inputs):
    import numpy as np
    import concourse.bacc as bacc
    from concourse.bass_utils import run_bass_kernel_spmd

    nc = bacc.Bacc("TRN2", target_bir_lowering=False, num_devices=1)
    arrays, A = {}, {}
    for name in _INS + ["tables"]:
        a = rotary_tables() if name == "tables" else np.ascontiguousarray(inputs[name])
        arrays[f"in_{name}"] = a
        A[name] = nc.dram_tensor(f"in_{name}", a.shape, mybir.dt.from_np(a.dtype), kind="ExternalInput").ap()
    out = nc.dram_tensor("out_0", (B, S, D), F32, kind="ExternalOutput").ap()
    build_program(nc, A, out)
    r = run_bass_kernel_spmd(nc, [arrays], core_ids=[0])
    return r.results[0]["out_0"]
```

```python
import concourse.bass as bass
from concourse import mybir
from contextlib import ExitStack

F32 = mybir.dt.float32
BF16 = mybir.dt.bfloat16
I32 = mybir.dt.int32
ALU = mybir.AluOpType
ACT = mybir.ActivationFunctionType
AX = mybir.AxisListType

P = 128
D = 128
B, S = 8, 256
TB = S // P
NT = B * TB
CH = 4
NC = NT // CH
EPS = 1e-5

H0, DH = 16, 64
PAIRS0 = H0 // 2
SLOTS = B * PAIRS0
WCOLS = 3 * P + 2

NE, HE = 16, 256
KE = HE // P

LAYERS, H1, WIN = 2, 8, 64
INNER = H1 * DH
PAIRS1 = H1 // 2
HID = 341
FCH = [(0, 128), (128, 128), (256, HID - 256)]
SCRATCH = 11264
NEG = -1e30

R_BQ, R_BK, R_BV, R_BO, R_LN1W, R_LN1B, R_CB1 = 0, 8, 16, 24, 25, 26, 27
R_B1, R_LV = 28, 60
LV = 8
MBANK, RBANK, GBANK = (4, 4, 5, 4), (5, 4, 5, 4), (7, 6, 7)
FREE = 1


def build_program(nc, A, out):
    with ExitStack() as ctx:
        def sb(name, shape, dt=F32):
            return ctx.enter_context(nc.sbuf_tensor(name, shape, dt))

        def sem(name):
            return ctx.enter_context(nc.semaphore(name))

        psum = ctx.enter_context(nc.psum_tensor("psum", [P, 8, 512], F32))

        def bank(k):
            return psum[:, k, :]

        ident = sb("ident", [P, P])
        identb = sb("identb", [P, P], BF16)
        causal = sb("causal", [P, P])
        band0 = sb("band0", [P, 2, P], BF16)
        band1 = sb("band1", [P, 2, 192], BF16)
        shift = sb("shift", [P, P])
        carry = sb("carry", [P, P])
        mhalf = sb("mhalf", [P, TB * H1])
        onecol = sb("onecol", [P, 1])
        zrow = sb("zrow", [P, 1])
        vrows = sb("vrows", [P, P])
        vec = sb("vec", [P, P])
        bo_eff = sb("bo_eff", [P, 1])
        w_qkv0 = sb("w_qkv0", [P, PAIRS0, WCOLS])
        w_o0 = sb("w_o0", [P, PAIRS0, D])
        ln2w = sb("ln2w", [P, D])
        ln2b = sb("ln2b", [P, D])
        w_r = sb("w_r", [P, NE])
        br = sb("br", [P, NE])
        b2e = sb("b2e", [NE, D])
        w1c = sb("w1c", [P, D])
        w2c = sb("w2c", [P, 2, D])
        wqkv1 = sb("wqkv1", [P, 3 * INNER])
        wo1 = sb("wo1", [P, PAIRS1, D])
        wf1 = sb("wf1", [P, 2 * HID])
        wf2 = sb("wf2", [P, 3, D])
        lv = sb("lv", [P, LV])
        rotc = sb("rotc", [P, 4, TB, DH])
        tab = sb("tab", [P, 4, TB, DH])
        qks = sb("qks", [P, 2, LAYERS, DH])
        rot = sb("rot", [P, LAYERS, 4, TB, DH])

        stream = sb("stream", [P, 3 * NT, D])
        x3 = stream[:, 0:NT, :]
        acc = stream[:, NT:2 * NT, :]
        x0 = stream[:, 2 * NT:3 * NT, :]
        x5 = x0
        big = sb("big", [P, SLOTS * S])
        zT = big[:, :].rearrange("p (g n) -> p g n", n=S)
        scratch = sb("scratch", [P, SCRATCH])
        at = [0, 0]

        def shaped(v, dims):
            if len(dims) == 1:
                return v
            names = "abcd"[:len(dims)]
            return v.rearrange(f"p ({' '.join(names)}) -> p {' '.join(names)}", **dict(zip(names, dims)))

        def carve(which, dims, dt=F32):
            n = 1
            for d in dims:
                n *= d
            a = at[which]
            at[which] = a + n
            assert at[which] <= (SLOTS * S, SCRATCH)[which], (which, at)
            return shaped((big, scratch)[which][:, a:a + n], dims)

        def from_big(*dims):
            return carve(0, dims)

        def from_scratch(*dims):
            return carve(1, dims)
        xT = sb("xT", [P, NT * P])
        comb = sb("comb", [P, NT, NE])

        st = sb("st", [P, 2, CH, 6])
        mv = sb("mv", [P, 2, CH, 2])
        ve = sb("ve", [P, 2, CH])
        rstd = sb("rstd", [P, 2, CH])

        x_in = sem("x_in")
        w_in = sem("w_in")
        rows_zero = sem("rows_zero")
        rows_in = sem("rows_in")
        const_ready = sem("const_ready")
        vec_ps = sem("vec_ps")
        vec_ready = sem("vec_ready")
        bo_ps = sem("bo_ps")
        phase_done = sem("phase_done")

        def apart(eng):
            eng.wait_ge(const_ready, 1)

        def end_phase(eng, n):
            eng.drain().then_inc(phase_done, 1)
            eng.wait_ge(phase_done, 4 * n)

        a_var, a_rstd, a_xn, a_tr, a_xt = (sem(f"a_{n}") for n in ("var", "rstd", "xn", "tr", "xt"))
        xn = sb("xn", [P, CH, D])

        wst = [from_scratch(WCOLS) for i in range(2)]
        xst = [from_scratch(S) for i in range(2)]
        qT = [from_scratch(S) for i in range(2)]
        kZ = [from_scratch(2, S) for i in range(2)]
        vS = [from_scratch(TB, P) for i in range(2)]
        pr = [from_scratch(TB, 2, S) for i in range(2)]
        pt = [from_scratch(TB * S) for i in range(2)]
        mx = from_scratch(4)
        nb = [from_scratch(4) for i in range(2)]
        sm = [from_scratch(4) for i in range(2)]
        rs = from_scratch(4)
        w_staged = [sem(f"w_staged{i}") for i in range(2)]
        x_staged = [sem(f"x_staged{i}") for i in range(2)]
        kz_zero = sem("kz_zero")
        s0_zero = sem("s0_zero")
        qk_ready, v_ready, qk_sb, v_sb, scores_ready, negmax_ready, exp_ready, probs_ready = (
            sem(n) for n in ("qk_ready", "v_ready", "qk_sb", "v_sb", "scores_ready", "negmax_ready",
                             "exp_ready", "probs_ready"))
        pT_ready = [sem(f"pT_ready{i}") for i in range(2)]
        pt_sb = [sem(f"pt_sb{i}") for i in range(2)]
        z_ready, z_sb = sem("z_ready"), sem("z_sb")

        at[1] = 0
        oT = from_scratch(CH * P)
        mid = from_scratch(CH, D)
        uC = from_scratch(CH, D)
        x1c = from_scratch(CH, D)
        xt1c = from_scratch(CH * P)
        lg = from_scratch(CH, NE)
        ex = from_scratch(CH, NE)
        r4 = from_scratch(CH)
        m8 = from_scratch(CH, 8)
        top2 = from_scratch(CH, 8)
        rest = from_scratch(CH, NE)
        combc = from_scratch(CH, NE)
        combT = from_scratch(CH * P)[0:NE]
        (c_o, c_oT, c_tr, c_mid, c_u, c_var, c_rstd, c_x1, c_xtps, c_xt, c_lg, c_sub, c_exp, c_comb,
         c_ctps, c_ct, c_yb, c_acc) = (sem(f"c_{n}") for n in (
             "o", "oT", "tr", "mid", "u", "var", "rstd", "x1", "xtps", "xt", "lg", "sub", "exp",
             "comb", "ctps", "ct", "yb", "acc"))

        at[0] = 0
        w1e = [sb(f"w1e{i}", [P, HE]) for i in range(2)]
        w2e = [sb(f"w2e{i}", [P, KE, D]) for i in range(2)]
        gE = [from_big(KE, CH * P) for i in range(2)]
        b1x = [from_big(KE) for i in range(2)]
        we_in = [sem(f"we_in{i}") for i in range(2)]
        u_ready, g_ready, y_ready, acc_done = (sem(n) for n in ("u_ready", "g_ready", "y_ready", "acc_done"))

        at[0] = 0

        def two(make, *dims):
            return [make(*dims) for _ in range(2)]

        x2 = two(from_big, TB, D)
        sqj = two(from_big, TB, D)
        ssq = two(from_big, TB)
        mq = two(from_big, TB)
        rn = two(from_big, TB)
        nrm = two(from_big, TB, D)
        xnT = two(from_big, 2 * S)
        rel = two(from_big, TB * S)
        zb = two(from_big, S)
        az = two(from_big, S)
        sp = two(from_big, S)
        oE = two(from_big, S)
        (e_var, e_rstd, e_x2, e_ssq, e_mq, e_rn, e_nrm, e_xnps, e_xn, e_sim, e_rel, e_ctr, e_log, e_sp,
         e_o, e_osb, e_oT, e_x3) = (sem(f"e_{n}") for n in (
             "var", "rstd", "x2", "ssq", "mq", "rn", "nrm", "xnps", "xn", "sim", "rel", "ctr", "log",
             "sp", "o", "osb", "oT", "x3"))

        at[0], at[1] = 0, 0
        v1 = two(from_big, TB, INNER)
        sq1 = two(from_big, INNER)
        t1 = two(from_big, INNER)
        t2 = two(from_big, INNER)
        qk = [two(from_big, 2 * INNER) for _ in range(2)]
        q1T = two(from_big, PAIRS1, S)
        k1Z = two(from_big, PAIRS1, 2, S)
        xc = from_scratch(TB, D)
        hT = two(from_scratch, S)
        p0 = two(from_scratch, 2, P)
        p1 = two(from_scratch, 2, S)
        pt1 = two(from_scratch, 3 * P)
        ss = from_scratch(TB, 2 * H1)
        rqk = from_scratch(TB, 2 * H1)
        rq8 = two(from_scratch, TB, H1)
        nrq8 = two(from_scratch, TB, H1)
        mx1 = two(from_scratch, TB, 2)
        nb1 = two(from_scratch, TB, 2)
        sm1 = two(from_scratch, TB, 2)
        rs1 = two(from_scratch, TB, 2)
        oT1 = two(from_scratch, PAIRS1, S)
        xm = two(from_scratch, TB, D)
        hn = from_scratch(TB, D)
        h2T = from_scratch(S)
        gl = from_scratch(3, S)
        hg = from_scratch(3, S)
        UNITS = LAYERS * B
        (f_xc, f_xT, f_hT, f_qk, f_sq, f_rot, f_add, f_ss, f_rk, f_kn, f_rq, f_rq8, f_vps, f_v, f_tr, f_trs,
         f_s, f_nb, f_e, f_p, f_t, f_pt0, f_pt1, f_z, f_zsb, f_wo, f_xm, f_sh, f_var, f_rstd, f_hn,
         f_h2ps, f_h2, f_ga, f_gl, f_hg, f_w2, f_x, f_zero, f_wqk, f_wv, f_wwo, f_wf1, f_wf2) = (
             sem(f"f_{n}") for n in (
                 "xc", "xT", "hT", "qk", "sq", "rot", "add", "ss", "rk", "kn", "rq", "rq8", "vps", "v", "tr",
                 "trs", "s", "nb", "e", "p", "t", "pt0", "pt1", "z", "zsb", "wo", "xm", "sh", "var", "rstd",
                 "hn", "h2ps", "h2", "ga", "gl", "hg", "w2", "x", "zero", "wqk", "wv", "wwo", "wf1", "wf2"))
        layer_in = sem("layer_in")
        h_var, h_rstd, h_out = sem("h_var"), sem("h_rstd"), sem("h_out")

        def live(m):
            return not isinstance(m, int) or 0 <= m < UNITS

        def later(count):
            return not isinstance(count, int) or count > 0

        def run_steps(eng, step):
            full = (2, 12)
            for n in range(-3, full[0]):
                step(n, n % 2)
            with eng.Fori(0, (full[1] - full[0]) // 2) as i:
                for s in range(2):
                    step(i * 2 + (full[0] + s), s)
            for n in range(full[1], UNITS + 2):
                step(n, n % 2)

        out_sem = sem("out_sem")

        def run_slots(eng, slot):
            for g in (-2, -1):
                slot(g, g % 2)
            with eng.Fori(0, SLOTS // 2 - 1) as i:
                for s in range(2):
                    slot(i * 2 + s, s)
            for g in (SLOTS - 2, SLOTS - 1):
                slot(g, g % 2)

        N_ROWS = 24
        block = ctx.enter_context(nc.Block())

        @block.sync
        def _(sp_):
            sp_.dma_start(x0[:], A["L0_attn_resid_pre"].rearrange("b (t p) d -> p (b t) d", p=P)).then_inc(x_in, 16)
            sp_.wait_ge(rows_zero, 1)

            def rows(r, n, src, w=P):
                sp_.dma_start(vrows[r:r + n, 0:w], src).then_inc(rows_in, 16)

            one = lambda name: A[name].rearrange("(a d) -> a d", a=1)
            rows(R_LN1W, 1, one("L0_attn_ln1_w"))
            rows(R_LN1B, 1, one("L0_attn_ln1_b"))
            for r, name in ((R_BQ, "Q"), (R_BK, "K"), (R_BV, "V")):
                rows(r, PAIRS0, A[f"L0_attn_b_{name}"].rearrange("(a two) k -> a (two k)", two=2))
            rows(R_BO, 1, one("L0_attn_b_O"))
            rows(R_CB1, 1, one("L1_attn_b1"))
            rows(R_B1, NE * KE, A["L0_ffn_b1"].rearrange("e (k p) -> (e k) p", p=P))
            for la in range(LAYERS):
                rows(R_LV + LV * la, 1, A["L1_ffn_ln_g"][la:la + 1, :])
                rows(R_LV + LV * la + 1, 1, A["L1_ffn_ln_b"][la:la + 1, :])
                for half in range(2):
                    for c, (o, w) in enumerate(FCH):
                        rows(R_LV + LV * la + 2 + 3 * half + c, 1,
                             A["L1_ffn_b1"][la:la + 1, half * HID + o:half * HID + o + w], w)
            n = [0]

            def layer1_load(load, la, parts):
                if "qk" in parts:
                    load(wqkv1[:, 0:2 * INNER], A["L1_ffn_wqkv"][la, :, 0:2 * INNER])
                if "v" in parts:
                    load(wqkv1[:, 2 * INNER:], A["L1_ffn_wqkv"][la, :, 2 * INNER:])
                if "o" in parts:
                    load(wo1[:], A["L1_ffn_wo"][la].rearrange("(a p) d -> p a d", p=P))
                if "f1" in parts:
                    load(wf1[:], A["L1_ffn_w1"][la])
                if "f2" in parts:
                    load(wf2[:, 0:2, :], A["L1_ffn_w2"][la, 0:256, :].rearrange("(c p) d -> p c d", p=P))
                    load(wf2[0:HID - 256, 2, :], A["L1_ffn_w2"][la, 256:HID, :])
                    load(wf2[HID - 256:HID - 255, 2, :], A["L1_ffn_b2"][la:la + 1, :])

            def load(dst, src):
                sp_.dma_start(dst, src).then_inc(w_in, 16)
                n[0] += 1

            for j, name in enumerate("QKV"):
                for h in range(2):
                    o = j * P + h * DH
                    load(w_qkv0[:, :, o:o + DH],
                         A[f"L0_attn_W_{name}"].rearrange("(a two) d k -> two d a k", two=2)[h])
            load(w_o0[:], A["L0_attn_W_O"].rearrange("h k d -> (h k) d").rearrange("(a p) d -> p a d", p=P))
            load(ln2w[:], A["L0_attn_ln2_w"].partition_broadcast(P))
            load(ln2b[:], A["L0_attn_ln2_b"].partition_broadcast(P))
            load(w_r[:], A["L0_ffn_Wr"])
            load(br[:], A["L0_ffn_br"].partition_broadcast(P))
            load(b2e[:], A["L0_ffn_b2"])
            load(w1c[:], A["L1_attn_W1"].rearrange("a d -> (a d)").partition_broadcast(P))
            load(w2c[:], A["L1_attn_W2"].rearrange("(a p) d -> p a d", p=P))
            load(tab[:], A["tables"].rearrange("j (t p) k -> p j t k", p=P))
            for j, name in enumerate(("q", "k")):
                load(qks[:, j], A[f"L1_ffn_{name}_scale"].rearrange("a b -> (a b)").partition_broadcast(P)
                     .rearrange("p (a b) -> p a b", a=LAYERS))
            layer1_load(load, 0, ("qk", "v", "o", "f1", "f2"))
            assert n[0] == N_W
            for e in range(2):
                sp_.dma_start(w1e[e][:], A["L0_ffn_W1"][e]).then_inc(we_in[e], 16)
                sp_.dma_start(w2e[e][:], A["L0_ffn_W2"][e].rearrange("(k p) d -> p k d", p=P)).then_inc(we_in[e], 16)
            sp_.wait_ge(phase_done, 4)
            with sp_.Fori(0, B) as b:
                with sp_.Fori(0, PAIRS0 // 2) as pp:
                    for s in range(2):
                        g = b * PAIRS0 + pp * 2 + s
                        sp_.wait_ge(v_ready, g + 1)
                        sp_.wait_ge(qk_sb, g + 1)
                        sp_.dma_start(wst[s][:], w_qkv0[:, pp * 2 + s, :]).then_inc(w_staged[s], 16)
                        sp_.dma_start(xst[s][:], xT[:, bass.ds(b * S, S)]).then_inc(x_staged[s], 16)
            with sp_.Fori(1, NE // 2) as i:
                for e in range(2):
                    sp_.wait_ge(y_ready, i * (2 * NC) + ((e - 1) * NC + 2))
                    sp_.dma_start(w1e[e][:], A["L0_ffn_W1"][i * 2 + e]).then_inc(we_in[e], 16)
                    sp_.dma_start(w2e[e][:], A["L0_ffn_W2"][i * 2 + e].rearrange("(k p) d -> p k d", p=P)).then_inc(we_in[e], 16)
            sp_.wait_ge(phase_done, 20)
            sp_.dma_start(lv[:], vec[:, R_LV:R_LV + LV]).then_inc(layer_in, 16)
            sp_.dma_start(rotc[:], rot[:, 0]).then_inc(layer_in, 16)
            sp_.wait_ge(layer_in, 32)
            n_in = [32]

            def second(dst, src_):
                sp_.dma_start(dst, src_).then_inc(layer_in, 16)
                n_in[0] += 16

            for ready in (f_wqk, f_wv, f_wwo, f_wf1, f_wf2):
                sp_.sem_inc(ready, B)
            sp_.wait_ge(f_rot, 4 * B)
            second(rotc[:], rot[:, 1])
            layer1_load(second, 1, ("qk",))
            sp_.wait_ge(layer_in, n_in[0])
            sp_.sem_inc(f_wqk, B)
            sp_.wait_ge(f_vps, 2 * B)
            layer1_load(second, 1, ("v",))
            sp_.wait_ge(layer_in, n_in[0])
            sp_.sem_inc(f_wv, B)
            sp_.wait_ge(f_wo, B)
            layer1_load(second, 1, ("o",))
            sp_.wait_ge(layer_in, n_in[0])
            sp_.sem_inc(f_wwo, B)
            sp_.wait_ge(f_hg, 3 * B)
            second(lv[:], vec[:, R_LV + LV:R_LV + 2 * LV])
            layer1_load(second, 1, ("f1",))
            sp_.wait_ge(layer_in, n_in[0])
            sp_.sem_inc(f_wf1, B)
            sp_.wait_ge(f_w2, B)
            layer1_load(second, 1, ("f2",))
            sp_.wait_ge(layer_in, n_in[0])
            sp_.sem_inc(f_wf2, B)
            outc = out.rearrange("b (t p) d -> p (b t) d", p=P)
            for c in range(NC):
                sp_.wait_ge(h_out, c + 1)
                sp_.dma_start(outc[:, c * CH:(c + 1) * CH, :], x5[:, c * CH:(c + 1) * CH, :]).then_inc(out_sem, 16)
            sp_.wait_ge(out_sem, 16 * NC)

        @block.gpsimd
        def _(pool):
            pool.memset(mhalf[:], -0.5)
            pool.memset(onecol[:], 1.0)
            pool.memset(ident[:], 0.0)
            pool.memset(causal[:], 1.0)
            pool.memset(band0[:], 0.0)
            pool.memset(band1[:], 0.0)
            pool.memset(shift[:], 0.0)
            pool.memset(carry[:], 0.0)
            pool.drain()
            pool.affine_select(out=ident[:], in_=ident[:], compare_op=ALU.not_equal, fill=1.0, base=0,
                               pattern=[[-1, P]], channel_multiplier=1)
            pool.affine_select(out=causal[:], in_=causal[:], compare_op=ALU.is_ge, fill=0.0, base=0,
                               pattern=[[-1, P]], channel_multiplier=1)
            pool.affine_select(out=band0[:], in_=band0[:], compare_op=ALU.is_ge, fill=NEG, base=0,
                               pattern=[[0, 2], [-1, P]], channel_multiplier=1)
            pool.affine_select(out=band1[:], in_=band1[:], compare_op=ALU.is_ge, fill=NEG, base=WIN,
                               pattern=[[0, 2], [-1, 192]], channel_multiplier=1)
            pool.affine_select(out=shift[:], in_=shift[:], compare_op=ALU.not_equal, fill=1.0, base=1,
                               pattern=[[-1, P]], channel_multiplier=1)
            pool.affine_select(out=carry[:], in_=carry[:], compare_op=ALU.not_equal, fill=1.0,
                               base=-(P - 1), pattern=[[-1, P]], channel_multiplier=1)
            pool.drain()
            pool.affine_select(out=band0[:], in_=band0[:], compare_op=ALU.is_ge, fill=NEG, base=WIN,
                               pattern=[[0, 2], [1, P]], channel_multiplier=-1)
            pool.affine_select(out=band1[:], in_=band1[:], compare_op=ALU.is_ge, fill=NEG, base=0,
                               pattern=[[0, 2], [1, 192]], channel_multiplier=-1)
            pool.tensor_copy(identb[:], ident[:])
            pool.drain().then_inc(const_ready, 1)
            with pool.Fori(0, NC) as c:
                pool.wait_ge(a_var, c + 1)
                pool.tensor_tensor(rstd[:, 0, :], ve[:, 0, :], mhalf[:, 0:CH], ALU.pow).then_inc(a_rstd, 1)
            end_phase(pool, 1)
            for s in range(2):
                pool.memset(kZ[s][64:P, 0, :], 0.0)
                pool.memset(kZ[s][0:64, 1, :], 0.0)
            pool.drain().then_inc(kz_zero, 1)
            end_phase(pool, 2)
            pool.memset(top2[:], -1.0)
            with pool.Fori(0, NC) as c:
                pool.wait_ge(c_mid, c + 1)
                pool.tensor_tensor(uC[:], mid[:], x0[:, bass.ds(c * CH, CH), :], ALU.add)
                pool.drain()
                pool.tensor_tensor(uC[:], uC[:], ln2b[:].unsqueeze(1).to_broadcast([P, CH, D]), ALU.add).then_inc(c_u, 1)
                for k in range(2):
                    pool.wait_ge(c_var, c * 2 + k + 1)
                    pool.tensor_tensor(rstd[:, k, :], ve[:, k, :], mhalf[:, 0:CH], ALU.pow).then_inc(c_rstd, 1)
            end_phase(pool, 3)
            end_phase(pool, 4)
            with pool.Fori(0, B // 2) as i:
                for s in range(2):
                    pool.wait_ge(e_var, i * 4 + s + 1)
                    pool.tensor_tensor(rstd[:, s, 0:TB], ve[:, s, 0:TB], mhalf[:, 0:TB], ALU.pow).then_inc(e_rstd, 1)
                for s in range(2):
                    pool.wait_ge(e_mq, i * 2 + s + 1)
                    pool.tensor_tensor(rn[s][:], mq[s][:], mhalf[:, 0:TB], ALU.pow).then_inc(e_rn, 1)
                for s in range(2):
                    pool.wait_ge(e_var, i * 4 + s + 3)
                    pool.tensor_tensor(rstd[:, s, 0:TB], ve[:, s, 0:TB], mhalf[:, 0:TB], ALU.pow).then_inc(e_rstd, 1)
            end_phase(pool, 5)
            for s in range(2):
                pool.memset(k1Z[s][64:P, :, 0, :], 0.0)
                pool.drain()
                pool.memset(k1Z[s][0:64, :, 1, :], 0.0)
                pool.drain()
                pool.memset(p1[s][:, :, 0:WIN], 0.0)
                pool.drain()
                pool.memset(hT[s][64:P, 0:1], 0.0)
                pool.drain()
            pool.memset(hg[64:P, 2, :], 1.0)
            pool.drain().then_inc(f_zero, 1)
            half = mhalf[:].rearrange("p (t h) -> p t h", t=TB)

            def copy_x(m):
                pool.wait_ge(f_x, m + 1)
                if later(m):
                    pool.wait_ge(f_xT, m)
                apart(pool)
                pool.tensor_copy(xc[:], stream[:, bass.ds(m * TB, TB), :]).then_inc(f_xc, 1)

            def add_rot(m, s, i):
                j, t = 1 - i // 2, i % 2
                if later(m * 4 - 4):
                    pool.wait_ge(f_tr, m * 4 - 4)
                pool.wait_ge(f_rot, m * 4 + i + 1)
                pool.tensor_tensor(qk[s][t][:, j * INNER:(j + 1) * INNER], t1[i % 2], t2[i % 2],
                                   ALU.add).then_inc(f_add, 1)

            def inverse_norm(m, j):
                pool.wait_ge(f_ss, m * 2 + 2 - j)
                if j == 0 and later(m):
                    pool.wait_ge(f_rq8, m)
                o = rqk[:, :, j * H1:(j + 1) * H1]
                pool.tensor_tensor(o, ss[:, :, j * H1:(j + 1) * H1], half, ALU.pow).then_inc((f_rq, f_rk)[j], 1)

            def scale_keys(m, s):
                pool.drain()
                for t in range(TB):
                    kk = qk[s][t][:, INNER:].rearrange("p (h k) -> p h k", h=H1)
                    last = pool.tensor_tensor(kk, kk, rqk[:, t, H1:].unsqueeze(2).to_broadcast([P, H1, DH]), ALU.mult)
                last.then_inc(f_kn, 1)

            def ln_rstd(m):
                pool.wait_ge(f_var, m + 1)
                pool.tensor_tensor(rstd[:, 0, 0:TB], ve[:, 0, 0:TB], mhalf[:, 0:TB], ALU.pow).then_inc(f_rstd, 1)

            def step(n, s):
                if live(n + 3):
                    copy_x(n + 3)
                if live(n + 2):
                    add_rot(n + 2, s, 0)
                if live(n - 1):
                    ln_rstd(n - 1)
                if live(n + 2):
                    add_rot(n + 2, s, 1)
                    inverse_norm(n + 2, 1)
                    scale_keys(n + 2, s)
                    add_rot(n + 2, s, 2)
                    add_rot(n + 2, s, 3)
                    inverse_norm(n + 2, 0)

            run_steps(pool, step)
            end_phase(pool, 6)
            for c in range(NC):
                pool.wait_ge(h_var, c + 1)
                pool.tensor_tensor(rstd[:, c % 2, :], ve[:, c % 2, :], mhalf[:, 0:CH], ALU.pow).then_inc(h_rstd, 1)

        @block.scalar
        def _(act):
            act.wait_ge(vec_ps, 1)
            act.activation(vec[:], bank(0)[:, 0:P], ACT.Copy).then_inc(vec_ready, 1)
            act.wait_ge(bo_ps, 1)
            act.activation(bo_eff[:], bank(1)[:, 0:1], ACT.Identity, bias=vec[:, R_BO:R_BO + 1])
            act.wait_ge(w_in, 16 * N_W)
            act.activation(w_qkv0[:, :, 3 * P], vec[:, R_BQ:R_BQ + PAIRS0], ACT.Copy)
            act.activation(w_qkv0[:, :, 3 * P + 1], vec[:, R_BK:R_BK + PAIRS0], ACT.Copy)
            act.sem_inc(a_xt, FREE)
            with act.Fori(0, NC) as c:
                act.wait_ge(a_tr, c + 1 + FREE)
                apart(act)
                act.activation(xT[:, bass.ds(c * CH * P, CH * P)], bank(0), ACT.Identity,
                               scale=vec[:, R_LN1W:R_LN1W + 1], bias=vec[:, R_LN1B:R_LN1B + 1]).then_inc(a_xt, 1)
            end_phase(act, 1)
            act.wait_ge(kz_zero, 1)

            def qk_evac(g, s):
                act.wait_ge(qk_ready, g + 1)
                act.activation(qT[s][:], bank(0)[:, 0:S], ACT.Identity, bias=wst[s][:, 3 * P:3 * P + 1])
                act.activation(kZ[s][0:64, 0, :], bank(0)[0:64, S:2 * S], ACT.Identity,
                               bias=wst[s][0:64, 3 * P + 1:3 * P + 2])
                act.activation(kZ[s][64:P, 1, :], bank(0)[64:P, S:2 * S], ACT.Identity,
                               bias=wst[s][64:P, 3 * P + 1:3 * P + 2]).then_inc(qk_sb, 1)

            def exps(g, s):
                act.wait_ge(negmax_ready, g + 1)
                for t in range(TB):
                    for h in range(2):
                        last = act.activation(pr[s][:, t, h, :], bank(2 + t)[:, h * S:(h + 1) * S], ACT.Exp,
                                              bias=nb[s][:, 2 * t + h:2 * t + h + 1], scale=DH ** -0.5,
                                              accum_out=sm[s][:, 2 * t + h:2 * t + h + 1])
                last.then_inc(exp_ready, 1)

            def pt_evac(g, s):
                act.wait_ge(pT_ready[0], g + 1)
                act.wait_ge(z_ready, g + FREE)
                act.activation(pt[0][:], bank(4), ACT.Copy).then_inc(pt_sb[0], 1)

            def z_evac(g, s):
                act.wait_ge(z_ready, g + 1 + FREE)
                apart(act)
                act.activation(zT[:, g, :], bank(6)[:, 0:S], ACT.Copy).then_inc(z_sb, 1)

            act.sem_inc(qk_sb, 2)
            act.sem_inc(z_sb, FREE)
            act.sem_inc(exp_ready, FREE)

            def slot(g, s):
                if not isinstance(g, int) or g >= 0:
                    pt_evac(g, s)
                if not isinstance(g, int) or 0 <= g + 1 < SLOTS:
                    exps(g + 1, 1 - s)
                if not isinstance(g, int) or g >= 0:
                    z_evac(g, s)
                if not isinstance(g, int) or g + 2 < SLOTS:
                    qk_evac(g + 2, s)

            run_slots(act, slot)
            end_phase(act, 2)
            act.sem_inc(c_oT, FREE)
            with act.Fori(0, NC) as c:
                act.wait_ge(c_o, c + 1)
                act.activation(oT[:], bank(0), ACT.Identity, bias=bo_eff[:]).then_inc(c_oT, 1)
                act.wait_ge(c_xtps, c + 1)
                act.activation(xt1c[:], bank(2), ACT.Copy)
                act.activation(xT[:, bass.ds(c * CH * P, CH * P)], bank(2), ACT.Copy).then_inc(c_xt, 1)
                act.wait_ge(c_sub, c + 1)
                act.activation(ex[:], lg[:], ACT.Exp).then_inc(c_exp, 1)
                act.wait_ge(c_ctps, c + 1)
                act.activation(combT[:], bank(4)[0:NE, :], ACT.Copy).then_inc(c_ct, 1)
            end_phase(act, 3)
            act.sem_inc(g_ready, 2)

            def gelu(n, u, e):
                if u % NC == 0:
                    act.activation(b1x[u // NC], vec[:, bass.ds(e * KE + R_B1, KE)], ACT.Copy)
                    act.drain()
                act.wait_ge(u_ready, n + 1)
                act.wait_ge(y_ready, n + 1)
                for kt in range(KE):
                    last = act.activation(gE[u % 2][:, kt, :], bank(2 * (u % 2) + kt), ACT.Gelu,
                                          bias=b1x[u // NC][:, kt:kt + 1])
                last.then_inc(g_ready, 1)

            with act.Fori(0, NE // 2) as i:
                for u in range(2 * NC):
                    gelu(i * 2 * NC + u, u, i * 2 + u // NC)
            end_phase(act, 4)
            with act.Fori(0, B // 2) as i:
                for s in range(2):
                    act.wait_ge(e_x2, i * 2 + s + 1)
                    for t in range(TB):
                        last = act.activation(sqj[s][:, t, :], x2[s][:, t, :], ACT.Square,
                                              accum_out=ssq[s][:, t:t + 1])
                    last.then_inc(e_ssq, 1)
                for s in range(2):
                    act.wait_ge(e_xnps, i * 2 + s + 1)
                    act.activation(xnT[s][:], bank(s), ACT.Copy).then_inc(e_xn, 1)
                for s in range(2):
                    act.wait_ge(e_sim, i * 2 + s + 1)
                    act.activation(rel[s][:], bank(2 + s), ACT.Relu).then_inc(e_rel, 1)
                for s in range(2):
                    act.wait_ge(e_ctr, i * 2 + s + 1)
                    act.activation(zb[s][:], bank(4 + s)[:, 0:S], ACT.Identity, bias=vec[:, R_CB1:R_CB1 + 1])
                act.drain()
                for s in range(2):
                    act.activation(az[s][:], zb[s][:], ACT.Abs)
                act.drain()
                for s in range(2):
                    act.activation(az[s][:], az[s][:], ACT.Exp, scale=-1.0)
                act.drain()
                for s in range(2):
                    act.activation(az[s][:], az[s][:], ACT.Ln, bias=onecol[:]).then_inc(e_log, 1)
                for s in range(2):
                    act.wait_ge(e_o, i * 2 + s + 1)
                    act.activation(oE[s][:], bank(6 + s)[:, 0:S], ACT.Copy).then_inc(e_osb, 1)
            end_phase(act, 5)
            act.wait_ge(f_zero, 1)

            def shift_in(m, s):
                act.wait_ge(f_xT, m + 1)
                if later(m - 1):
                    act.wait_ge(f_vps, m * 2 - 2)
                act.activation(hT[s][0:64, :], bank(5)[0:64, 0:S], ACT.Copy)
                act.activation(hT[s][64:P, 1:S], bank(5)[64:P, 0:S - 1], ACT.Copy).then_inc(f_hT, 1)

            def square(m, i):
                act.wait_ge(f_qk, m * 4 + i + 1)
                if later(m * 4 + i - 1):
                    act.wait_ge(f_rot, m * 4 + i - 1)
                act.activation(sq1[i % 2], bank(MBANK[i]), ACT.Square).then_inc(f_sq, 1)

            def value_out(m, s, t):
                act.wait_ge(f_vps, m * 2 + t + 1)
                if later(m * 4 - 4):
                    act.wait_ge(f_z, m * 4 - 4)
                act.activation(v1[s][:, t, :], bank(5), ACT.Copy).then_inc(f_v, 1)

            def turned_out(m, s, u):
                act.wait_ge(f_tr, m * 4 + u + 1)
                if later(m * 4 - 4):
                    act.wait_ge(f_s, m * 4 - 4)
                src = bank(RBANK[u]).rearrange("p (a n) -> p a n", a=2)
                a = 2 * (u % 2)
                if u < 2:
                    act.activation(q1T[s][:, a:a + 2, :], src, ACT.Copy).then_inc(f_trs, 1)
                else:
                    act.activation(k1Z[s][0:64, a:a + 2, 0, :], src[0:64], ACT.Copy)
                    act.activation(k1Z[s][64:P, a:a + 2, 1, :], src[64:P], ACT.Copy).then_inc(f_trs, 1)

            def expo(m, s, a):
                act.wait_ge(f_nb, m * 4 + a + 1)
                if later(m * 4 + a - 1):
                    act.wait_ge(f_t, m * 4 + a - 1)
                k = a % 2
                for t in range(TB):
                    for h in range(2):
                        if t == 0:
                            o, src = p0[k][:, h, :], bank(0)[:, h * P:(h + 1) * P]
                        else:
                            o, src = p1[k][:, h, WIN:S], bank(1)[:, h * 192:(h + 1) * 192]
                        last = act.activation(o, src, ACT.Exp, bias=nb1[k][:, t, h:h + 1],
                                              scale=rq8[s][:, t, 2 * a + h:2 * a + h + 1],
                                              accum_out=sm1[k][:, t, h:h + 1])
                last.then_inc(f_e, 1)

            def probs_out(m, a):
                act.wait_ge(f_t, m * 4 + a + 1)
                act.activation(pt1[0][:], bank(2)[:, 0:3 * P], ACT.Copy).then_inc(f_pt0, 1)

            def z_out(m, s, a):
                act.wait_ge(f_z, m * 4 + a + 1)
                if later(m - 1):
                    act.wait_ge(f_wo, m - 1)
                act.activation(oT1[s][:, a, :], bank(2)[:, 0:S], ACT.Copy).then_inc(f_zsb, 1)

            def normed_out(m):
                act.wait_ge(f_wf1, m + 1)
                act.wait_ge(f_h2ps, m + 1)
                act.activation(h2T[:], bank(6)[:, S:2 * S], ACT.Identity,
                               scale=lv[:, 0:1], bias=lv[:, 1:2]).then_inc(f_h2, 1)

            def gelu1(m, c):
                act.wait_ge(f_ga, m * 3 + c + 1)
                w = FCH[c][1]
                act.activation(gl[0:w, c, :], bank(GBANK[c])[0:w, 0:S], ACT.Gelu,
                               bias=lv[0:w, 5 + c:6 + c]).then_inc(f_gl, 1)

            def step(n, s):
                if live(n):
                    expo(n, s, 1)
                if live(n + 2):
                    square(n + 2, 0)
                if live(n):
                    probs_out(n, 0)
                if live(n + 1):
                    value_out(n + 1, 1 - s, 0)
                if live(n):
                    z_out(n, s, 0)
                if live(n + 2):
                    square(n + 2, 1)
                if live(n):
                    expo(n, s, 2)
                if live(n + 2):
                    square(n + 2, 2)
                if live(n):
                    probs_out(n, 1)
                    z_out(n, s, 1)
                if live(n + 2):
                    square(n + 2, 3)
                if live(n):
                    expo(n, s, 3)
                    probs_out(n, 2)
                if live(n - 1):
                    normed_out(n - 1)
                if live(n):
                    z_out(n, s, 2)
                if live(n + 1):
                    for u in range(4):
                        turned_out(n + 1, 1 - s, u)
                    expo(n + 1, 1 - s, 0)
                    value_out(n + 1, 1 - s, 1)
                if live(n):
                    probs_out(n, 3)
                if live(n - 1):
                    gelu1(n - 1, 0)
                if live(n):
                    z_out(n, s, 3)
                if live(n - 1):
                    gelu1(n - 1, 1)
                    gelu1(n - 1, 2)
                if live(n + 3):
                    shift_in(n + 3, 1 - s)

            run_steps(act, step)
            end_phase(act, 6)

        @block.tensor
        def _(pe):
            pe.wait_ge(const_ready, 1)
            pe.wait_ge(rows_in, 16 * N_ROWS)
            pe.transpose(bank(0)[:, 0:P], vrows[:], ident[:]).then_inc(vec_ps, 1)
            pe.wait_ge(vec_ready, 1)
            pe.wait_ge(w_in, 16 * N_W)
            for a in range(PAIRS0):
                mm = pe.matmul(bank(1)[:, 0:1], w_o0[:, a, :], vec[:, R_BV + a:R_BV + a + 1],
                               start=(a == 0), stop=(a == PAIRS0 - 1))
            mm.then_inc(bo_ps, 1)
            pe.sem_inc(a_tr, FREE)
            with pe.Fori(0, NC) as c:
                pe.wait_ge(a_xn, c + 1)
                pe.wait_ge(a_xt, c + FREE)
                for t in range(CH):
                    mm = pe.transpose(bank(0)[:, t * P:(t + 1) * P], xn[:, t, :], ident[:])
                mm.then_inc(a_tr, 1)
            end_phase(pe, 1)
            pe.wait_ge(s0_zero, 1)
            pe.sem_inc(v_ready, 2)
            pe.sem_inc(z_ready, FREE)

            def project(g, s, turn):
                pe.wait_ge(w_staged[s], (turn + 1) * 16)
                pe.wait_ge(x_staged[s], (turn + 1) * 16)
                pe.wait_ge(qk_sb, g + 1 + FREE)
                for j in range(2):
                    mm = pe.matmul(bank(0)[:, j * S:(j + 1) * S], wst[s][:, j * P:(j + 1) * P], xst[s][:],
                                   start=True, stop=True)
                mm.then_inc(qk_ready, 1)
                pe.wait_ge(v_sb, g + FREE)
                for t in range(TB):
                    mm = pe.matmul(bank(1)[:, t * P:(t + 1) * P], xst[s][:, t * P:(t + 1) * P],
                                   wst[s][:, 2 * P:3 * P], start=True, stop=True)
                mm.then_inc(v_ready, 1)

            def scores(g, s):
                pe.wait_ge(qk_sb, g + 1 + 2)
                pe.wait_ge(exp_ready, g + FREE)
                pe.matmul(bank(2).rearrange("p (h n) -> p h n", h=2)[:, :, 0:P], qT[s][:, 0:P],
                          kZ[s][:, :, 0:P], start=True, stop=True)
                pe.matmul(bank(3), qT[s][:, P:S], kZ[s][:].rearrange("p h n -> p (h n)"),
                          start=True, stop=True).then_inc(scores_ready, 1)

            def turn_probs(g, s):
                pe.wait_ge(probs_ready, g + 1)
                for h in range(2):
                    pe.wait_ge(pt_sb[h], g + FREE)
                    for kt in range(TB):
                        for t in range(TB):
                            mm = pe.transpose(bank(4 + h)[:, kt * S + t * P:kt * S + (t + 1) * P],
                                              pr[s][:, t, h, kt * P:(kt + 1) * P], ident[:])
                    mm.then_inc(pT_ready[h], 1)

            def values(g, s):
                pe.wait_ge(pt_sb[0], g + 1 + FREE)
                pe.wait_ge(pt_sb[1], g + 1 + FREE)
                pe.wait_ge(v_sb, g + 1 + FREE)
                pe.wait_ge(z_sb, g + FREE)
                for kt in range(TB):
                    for h in range(2):
                        mm = pe.matmul(bank(6)[h * 64:(h + 1) * 64, 0:S], vS[s][:, kt, h * 64:(h + 1) * 64],
                                       pt[h][:, kt * S:(kt + 1) * S], start=(kt == 0), stop=(kt == TB - 1))
                mm.then_inc(z_ready, 1)

            pe.wait_ge(phase_done, 4)

            def slot(g, s):
                full = not isinstance(g, int)
                if full or g >= 0:
                    turn_probs(g, s)
                if full or g + 2 < SLOTS:
                    project(g + 2, s, turn_of(g, s) + 1)
                if full or g >= 0:
                    values(g, s)
                if full or g + 2 < SLOTS:
                    scores(g + 2, s)

            def turn_of(g, s):
                return g // 2 if isinstance(g, int) else half[0]

            half = [None]
            for g in (-2, -1):
                slot(g, g % 2)
            with pe.Fori(0, SLOTS // 2 - 1) as i:
                half[0] = i
                for s in range(2):
                    slot(i * 2 + s, s)
            for g in (SLOTS - 2, SLOTS - 1):
                slot(g, g % 2)
            end_phase(pe, 2)
            zT4 = big[:, :].rearrange("p (b a n) -> p b a n", b=B, a=PAIRS0)
            pe.sem_inc(c_tr, FREE)
            with pe.Fori(0, NC) as c:
                pe.wait_ge(c_oT, c + FREE)
                for a in range(PAIRS0):
                    mm = pe.matmul(bank(0), w_o0[:, a, :], zT4[:, bass.ds(c * 2, 2), a, :],
                                   start=(a == 0), stop=(a == PAIRS0 - 1))
                mm.then_inc(c_o, 1)
                pe.wait_ge(c_oT, c + 1 + FREE)
                for t in range(CH):
                    mm = pe.transpose(bank(1)[:, t * P:(t + 1) * P], oT[:, t * P:(t + 1) * P], ident[:])
                mm.then_inc(c_tr, 1)
                pe.wait_ge(c_x1, c + 1)
                for t in range(CH):
                    mm = pe.transpose(bank(2)[:, t * P:(t + 1) * P], x1c[:, t, :], ident[:])
                mm.then_inc(c_xtps, 1)
                pe.wait_ge(c_xt, c + 1)
                for t in range(CH):
                    mm = pe.matmul(bank(3)[:, t * NE:(t + 1) * NE], xt1c[:, t * P:(t + 1) * P], w_r[:],
                                   start=True, stop=True)
                mm.then_inc(c_lg, 1)
                pe.wait_ge(c_comb, c + 1)
                for t in range(CH):
                    mm = pe.transpose(bank(4)[0:NE, t * P:(t + 1) * P], combc[:, t, :], ident[:])
                mm.then_inc(c_ctps, 1)
                pe.wait_ge(c_ct, c + 1)
                for t in range(CH):
                    mm = pe.matmul(bank(5)[:, t * P:(t + 1) * P], combT[:, t * P:(t + 1) * P], b2e[:],
                                   start=True, stop=True)
                mm.then_inc(c_yb, 1)
            end_phase(pe, 3)
            pe.sem_inc(y_ready, 2)

            def up(n, u, turn):
                if u % NC == 0:
                    pe.wait_ge(we_in[u // NC % 2], (turn + 1) * 32)
                pe.wait_ge(g_ready, n + 1)
                for kt in range(KE):
                    mm = pe.matmul(bank(2 * (u % 2) + kt), w1e[u // NC % 2][:, kt * P:(kt + 1) * P],
                                   xT[:, (u % NC) * CH * P:(u % NC + 1) * CH * P], start=True, stop=True)
                mm.then_inc(u_ready, 1)

            def down(n, u):
                pe.wait_ge(g_ready, n + 1 + 2)
                pe.wait_ge(acc_done, n + 1)
                for t in range(CH):
                    for kt in range(KE):
                        mm = pe.matmul(bank(4 + u % 2)[:, t * P:(t + 1) * P], gE[u % 2][:, kt, t * P:(t + 1) * P],
                                       w2e[u // NC][:, kt, :], start=(kt == 0), stop=(kt == KE - 1))
                mm.then_inc(y_ready, 1)

            up(0, 0, 0)
            with pe.Fori(0, NE // 2 - 1) as i:
                for u in range(2 * NC):
                    up(i * 2 * NC + u + 1, u + 1, i + (u + 1) // (2 * NC))
                    down(i * 2 * NC + u, u)
            for u in range(2 * NC):
                n = (NE // 2 - 1) * 2 * NC + u
                if u + 1 < 2 * NC:
                    up(n + 1, u + 1, NE // 2 - 1)
                down(n, u)
            end_phase(pe, 4)
            with pe.Fori(0, B // 2) as i:
                for s in range(2):
                    pe.wait_ge(e_nrm, i * 2 + s + 1)
                    for t in range(TB):
                        pe.transpose(bank(s)[:, t * P:(t + 1) * P], x2[s][:, t, :], ident[:])
                        mm = pe.transpose(bank(s)[:, S + t * P:S + (t + 1) * P], nrm[s][:, t, :], ident[:])
                    mm.then_inc(e_xnps, 1)
                for s in range(2):
                    pe.wait_ge(e_xn, i * 2 + s + 1)
                    for t in range(TB):
                        mm = pe.matmul(bank(2 + s)[:, t * S:(t + 1) * S], xnT[s][:, S + t * P:S + (t + 1) * P],
                                       xnT[s][:, S:2 * S], start=True, stop=True)
                    mm.then_inc(e_sim, 1)
                for s in range(2):
                    pe.wait_ge(e_rel, i * 2 + s + 1)
                    for t in range(TB):
                        mm = pe.matmul(bank(4 + s)[:, 0:S], w1c[:], rel[s][:, t * S:(t + 1) * S],
                                       start=(t == 0), stop=(t == TB - 1))
                    mm.then_inc(e_ctr, 1)
                for s in range(2):
                    pe.wait_ge(e_sp, i * 2 + s + 1)
                    pe.matmul(bank(6 + s)[:, 0:S], w2c[:, 0, :], xnT[s][:, 0:S], start=True, stop=False)
                    pe.matmul(bank(6 + s)[:, 0:S], w2c[:, 1, :], sp[s][:], start=False, stop=True).then_inc(e_o, 1)
                for s in range(2):
                    pe.wait_ge(e_osb, i * 2 + s + 1)
                    for t in range(TB):
                        mm = pe.transpose(bank(6 + s)[:, S + t * P:S + (t + 1) * P], oE[s][:, t * P:(t + 1) * P], ident[:])
                    mm.then_inc(e_oT, 1)
                pe.wait_ge(e_x3, i * 2 + 2)
            end_phase(pe, 5)
            pe.wait_ge(f_zero, 1)

            def turn_x(m):
                pe.wait_ge(f_xc, m + 1)
                if later(m):
                    pe.wait_ge(f_hT, m)
                    pe.wait_ge(f_rot, m * 4 - 1)
                if later(m - 1):
                    pe.wait_ge(f_v, m * 2 - 2)
                for t in range(TB):
                    mm = pe.transpose(bank(5)[:, t * P:(t + 1) * P], xc[:, t, :], ident[:])
                mm.then_inc(f_xT, 1)

            def project1(m, s, i):
                if i == 0:
                    pe.wait_ge(f_wqk, m + 1)
                    pe.wait_ge(f_hT, m + 1)
                    if later(m):
                        pe.wait_ge(f_rot, m * 4)
                    if later(m * 4 - 4):
                        pe.wait_ge(f_trs, m * 4 - 4)
                elif i == 2:
                    if later(m):
                        pe.wait_ge(f_v, m * 2 - 1)
                else:
                    pe.wait_ge(f_rot, m * 4 + (i + 1) // 2)
                j, t = 1 - i // 2, i % 2
                pe.matmul(bank(MBANK[i]), hT[s][:, t * P:(t + 1) * P], wqkv1[:, j * INNER:(j + 1) * INNER],
                          start=True, stop=True).then_inc(f_qk, 1)

            def project_v(m, s, t):
                if t == 0:
                    pe.wait_ge(f_wv, m + 1)
                    if live(m + 1):
                        pe.wait_ge(f_hT, m + 2)
                    elif later(m):
                        pe.wait_ge(f_v, m * 2)
                else:
                    pe.wait_ge(f_trs, m * 4 + 3)
                pe.matmul(bank(5), hT[s][:, t * P:(t + 1) * P], wqkv1[:, 2 * INNER:],
                          start=True, stop=True).then_inc(f_vps, 1)

            def turn_qk(m, s, u):
                if u == 0:
                    pe.wait_ge(f_kn, m + 1)
                    pe.wait_ge(f_add, m * 4 + 4)
                    pe.wait_ge(f_v, m * 2 + 1)
                if u < 2:
                    if live(m + 1):
                        pe.wait_ge(f_rot, m * 4 + 7 + u)
                    if u == 1 and later(m):
                        pe.wait_ge(f_trs, m * 4)
                else:
                    pe.wait_ge(f_trs, m * 4 + u - 1)
                j, a = u // 2, 2 * (u % 2)
                for b_ in range(2):
                    for t in range(TB):
                        o = j * INNER + (a + b_) * P
                        mm = pe.transpose(bank(RBANK[u])[:, b_ * S + t * P:b_ * S + (t + 1) * P],
                                          qk[s][t][:, o:o + P], ident[:])
                mm.then_inc(f_tr, 1)

            def scores1(m, s, a):
                if a == 0:
                    pe.wait_ge(f_trs, m * 4 + 4)
                if later(m * 4 + a):
                    pe.wait_ge(f_e, m * 4 + a)
                o = bank(0)[:, 0:2 * P].rearrange("p (h n) -> p h n", h=2)
                pe.matmul(o, q1T[s][:, a, 0:P], k1Z[s][:, a, :, 0:P], start=True, stop=False)
                pe.matmul(o, identb[:], band0[:], start=False, stop=True)
                o = bank(1)[:, 0:384].rearrange("p (h n) -> p h n", h=2)
                pe.matmul(o, q1T[s][:, a, P:S], k1Z[s][:, a, :, WIN:S], start=True, stop=False)
                pe.matmul(o, identb[:], band1[:], start=False, stop=True).then_inc(f_s, 1)

            def turn_probs1(m, a):
                pe.wait_ge(f_p, m * 4 + a + 1)
                if later(m * 4 + a):
                    pe.wait_ge(f_zsb, m * 4 + a)
                k = a % 2
                for h in range(2):
                    pe.transpose(bank(2 + h)[:, 0:P], p0[k][:, h, :], ident[:])
                    for kt in range(TB):
                        mm = pe.transpose(bank(2 + h)[:, (kt + 1) * P:(kt + 2) * P],
                                          p1[k][:, h, kt * P:(kt + 1) * P], ident[:])
                mm.then_inc(f_t, 1)

            def values1(m, s, a):
                pe.wait_ge(f_pt0, m * 4 + a + 1)
                pe.wait_ge(f_pt1, m * 4 + a + 1)
                if a == 0:
                    pe.wait_ge(f_v, m * 2 + 2)
                for h in range(2):
                    v = v1[s][:, :, (2 * a + h) * DH:(2 * a + h + 1) * DH]
                    o = bank(2)[h * 64:(h + 1) * 64]
                    pe.matmul(o[:, 0:S], v[:, 0, :], pt1[h][:, 0:S], start=True, stop=False,
                              skip_group_check=True)
                    mm = pe.matmul(o[:, P:S], v[:, 1, :], pt1[h][:, S:3 * P], start=False, stop=True,
                                   skip_group_check=True)
                mm.then_inc(f_z, 1)

            def attn_out(m, s):
                pe.wait_ge(f_wwo, m + 1)
                pe.wait_ge(f_zsb, m * 4 + 4)
                if later(m):
                    pe.wait_ge(f_hg, m * 3)
                for t in range(TB):
                    for a in range(PAIRS1):
                        mm = pe.matmul(bank(6)[:, t * P:(t + 1) * P], oT1[s][:, a, t * P:(t + 1) * P], wo1[:, a, :],
                                       start=(a == 0), stop=(a == PAIRS1 - 1))
                mm.then_inc(f_wo, 1)

            def shift_mid(m, s):
                pe.wait_ge(f_xm, m + 1)
                pe.wait_ge(f_x, m + B)
                o = bank(7)[:, 0:S].rearrange("p (t d) -> p t d", t=TB)
                pe.matmul(o[:, :, 0:64], ident[:], xm[s][:, :, 0:64], start=True, stop=True, skip_group_check=True)
                pe.matmul(o[:, :, 64:P], shift[:], xm[s][:, :, 64:P], start=True, stop=False, skip_group_check=True)
                pe.matmul(o[:, 1, 64:P], carry[:], xm[s][:, 0, 64:P], start=False, stop=True,
                          skip_group_check=True).then_inc(f_sh, 1)

            def turn_normed(m):
                pe.wait_ge(f_hn, m + 1)
                for t in range(TB):
                    mm = pe.transpose(bank(6)[:, S + t * P:S + (t + 1) * P], hn[:, t, :], ident[:])
                mm.then_inc(f_h2ps, 1)

            def hidden(m, c):
                o, w = FCH[c]
                if c == 0:
                    pe.wait_ge(f_wf1, m + 1)
                    pe.wait_ge(f_h2, m + 1)
                if c == 2:
                    pe.wait_ge(f_hg, m * 3 + 1)
                for half_ in range(2):
                    mm = pe.matmul(bank(GBANK[c])[0:w, half_ * S:(half_ + 1) * S],
                                   wf1[:, (1 - half_) * HID + o:(1 - half_) * HID + o + w], h2T[:],
                                   start=True, stop=True)
                mm.then_inc(f_ga, 1)

            def ffn_out(m):
                pe.wait_ge(f_wf2, m + 1)
                pe.wait_ge(f_hg, m * 3 + 3)
                for t in range(TB):
                    for c in range(3):
                        w = P if c < 2 else HID - 255
                        mm = pe.matmul(bank(7)[:, t * P:(t + 1) * P], hg[0:w, c, t * P:(t + 1) * P],
                                       wf2[0:w, c, :], start=(c == 0), stop=(c == 2))
                mm.then_inc(f_w2, 1)

            def step(n, s):
                if live(n):
                    scores1(n, s, 1)
                if live(n + 2):
                    project1(n + 2, s, 0)
                if live(n - 1):
                    attn_out(n - 1, 1 - s)
                if live(n - 2):
                    ffn_out(n - 2)
                if live(n):
                    turn_probs1(n, 0)
                if live(n + 1):
                    project_v(n + 1, 1 - s, 0)
                if live(n):
                    values1(n, s, 0)
                if live(n + 2):
                    project1(n + 2, s, 1)
                if live(n):
                    scores1(n, s, 2)
                if live(n + 2):
                    project1(n + 2, s, 2)
                if live(n):
                    turn_probs1(n, 1)
                if live(n - 1):
                    shift_mid(n - 1, 1 - s)
                if live(n):
                    values1(n, s, 1)
                if live(n + 2):
                    project1(n + 2, s, 3)
                if live(n):
                    scores1(n, s, 3)
                    turn_probs1(n, 2)
                if live(n - 1):
                    turn_normed(n - 1)
                if live(n):
                    values1(n, s, 2)
                if live(n + 1):
                    for u in range(4):
                        turn_qk(n + 1, 1 - s, u)
                    scores1(n + 1, 1 - s, 0)
                    project_v(n + 1, 1 - s, 1)
                if live(n - 1):
                    hidden(n - 1, 0)
                if live(n):
                    turn_probs1(n, 3)
                if live(n - 1):
                    hidden(n - 1, 1)
                if live(n):
                    values1(n, s, 3)
                if live(n - 1):
                    hidden(n - 1, 2)
                if live(n + 3):
                    turn_x(n + 3)

            run_steps(pe, step)
            end_phase(pe, 6)

        @block.vector
        def _(dve):
            def ln_stats(src, n, k, ready):
                for t in range(n):
                    dve.bn_stats(st[:, k, t, :], src(t))
                dve.drain()
                for t in range(n):
                    dve.bn_aggr(mv[:, k, t, :], st[:, k, t, :])
                dve.drain()
                dve.tensor_scalar(ve[:, k, 0:n], mv[:, k, 0:n, 1], EPS, None, ALU.add).then_inc(ready, 1)

            def ln_apply(dst, src, n, k):
                for t in range(n):
                    last = dve.tensor_scalar(dst(t), src(t), mv[:, k, t, 0:1], rstd[:, k, t:t + 1],
                                             ALU.subtract, ALU.mult)
                return last

            dve.memset(vrows[:], 0.0).then_inc(rows_zero, 1)
            dve.wait_ge(w_in, 16 * N_W)
            for la in range(LAYERS):
                for j in range(2):
                    for t in range(TB):
                        dve.tensor_tensor(rot[:, la, 2 * j, t, :], tab[:, 2 * j, t, :], qks[:, j, la, :], ALU.mult)
                        for a, b_ in ((0, 32), (32, 0)):
                            dve.tensor_tensor(rot[:, la, 2 * j + 1, t, a:a + 32], tab[:, 2 * j + 1, t, a:a + 32],
                                              qks[:, j, la, b_:b_ + 32], ALU.mult)
            dve.wait_ge(x_in, 16)
            with dve.Fori(0, NC) as c:
                ln_stats(lambda t: x0[:, c * CH + t, :], CH, 0, a_var)
                dve.wait_ge(a_rstd, c + 1)
                dve.wait_ge(a_tr, c + FREE)
                ln_apply(lambda t: xn[:, t, :], lambda t: x0[:, c * CH + t, :], CH, 0).then_inc(a_xn, 1)
            end_phase(dve, 1)
            dve.memset(bank(2).rearrange("p (h n) -> p h n", h=2)[:, :, P:S], 0.0).then_inc(s0_zero, 1)
            dve.sem_inc(v_sb, FREE)
            dve.sem_inc(pt_sb[0], FREE)
            dve.sem_inc(pt_sb[1], FREE)
            mask = causal[:].unsqueeze(1).to_broadcast([P, 2, P])

            def negmax(g, s):
                dve.wait_ge(scores_ready, g + 1)
                for t in range(TB):
                    d = bank(2 + t).rearrange("p (h n) -> p h n", h=2)[:, :, t * P:(t + 1) * P]
                    dve.tensor_tensor(d, d, mask, ALU.mult)
                dve.drain()
                dve.tensor_reduce(mx[:, 0:2], bank(2).rearrange("p (h n) -> p h n", h=2)[:, :, 0:P], AX.X, ALU.max)
                dve.tensor_reduce(mx[:, 2:4], bank(3).rearrange("p (h n) -> p h n", h=2), AX.X, ALU.max)
                dve.drain()
                dve.tensor_scalar(nb[s][:, 0:2], mx[:, 0:2], -DH ** -0.5, 0.0, ALU.mult, ALU.min)
                dve.tensor_scalar(nb[s][:, 2:4], mx[:, 2:4], -DH ** -0.5, None, ALU.mult).then_inc(negmax_ready, 1)

            def normalise(g, s):
                dve.wait_ge(exp_ready, g + 1 + FREE)
                dve.reciprocal(rs[:], sm[s][:])
                dve.drain()
                for t in range(TB):
                    for h in range(2):
                        last = dve.tensor_scalar(pr[s][:, t, h, :], pr[s][:, t, h, :], rs[:, 2 * t + h:2 * t + h + 1],
                                                 None, ALU.mult)
                last.then_inc(probs_ready, 1)

            def pt_evac(g, s):
                dve.wait_ge(pT_ready[1], g + 1)
                dve.wait_ge(z_ready, g + FREE)
                dve.tensor_copy(pt[1][:], bank(5)).then_inc(pt_sb[1], 1)

            def v_evac(g, s):
                dve.wait_ge(v_ready, g + 1 + 2)
                if not isinstance(g, int) or g >= 2:
                    dve.wait_ge(z_ready, g - 1 + FREE)
                dve.tensor_copy(vS[s][:].rearrange("p t n -> p (t n)"), bank(1)[:, 0:S]).then_inc(v_sb, 1)

            def slot(g, s):
                full = not isinstance(g, int)
                if full or 0 <= g + 1 < SLOTS:
                    negmax(g + 1, 1 - s)
                if full or g >= 0:
                    pt_evac(g, s)
                if full or 0 <= g + 1 < SLOTS:
                    normalise(g + 1, 1 - s)
                if full or g + 2 < SLOTS:
                    v_evac(g + 2, s)

            run_slots(dve, slot)
            end_phase(dve, 2)
            bc = lambda v, n: v.unsqueeze(2).to_broadcast([P, CH, n])
            with dve.Fori(0, NC) as c:
                x0c = x0[:, bass.ds(c * CH, CH), :]
                dve.wait_ge(c_tr, c + 1 + FREE)
                dve.tensor_tensor(mid[:], bank(1).rearrange("p (t d) -> p t d", t=CH), x0c, ALU.add)
                dve.drain().then_inc(c_mid, 1)
                ln_stats(lambda t: mid[:, t, :], CH, 0, c_var)
                dve.wait_ge(c_rstd, c * 2 + 1)
                ln_apply(lambda t: x1c[:, t, :], lambda t: mid[:, t, :], CH, 0)
                dve.drain()
                dve.tensor_tensor(x1c[:], x1c[:], ln2w[:].unsqueeze(1).to_broadcast([P, CH, D]), ALU.mult)
                dve.drain()
                dve.wait_ge(c_u, c + 1)
                dve.tensor_tensor(x1c[:], x1c[:], uC[:], ALU.add)
                dve.drain()
                ln_stats(lambda t: x1c[:, t, :], CH, 1, c_var)
                dve.wait_ge(c_rstd, c * 2 + 2)
                ln_apply(lambda t: x1c[:, t, :], lambda t: x1c[:, t, :], CH, 1).then_inc(c_x1, 1)
                dve.wait_ge(c_lg, c + 1)
                dve.tensor_tensor(lg[:], bank(3)[:, 0:CH * NE].rearrange("p (t e) -> p t e", t=CH),
                                  br[:].unsqueeze(1).to_broadcast([P, CH, NE]), ALU.add)
                dve.drain()
                dve.tensor_reduce(r4[:], lg[:], AX.X, ALU.max)
                dve.drain()
                dve.tensor_tensor(lg[:], lg[:], bc(r4[:], NE), ALU.subtract).then_inc(c_sub, 1)
                dve.wait_ge(c_exp, c + 1)
                dve.tensor_reduce(r4[:], ex[:], AX.X, ALU.add)
                dve.drain()
                dve.reciprocal(r4[:], r4[:])
                dve.drain()
                dve.tensor_tensor(ex[:], ex[:], bc(r4[:], NE), ALU.mult)
                dve.drain()
                for t in range(CH):
                    dve.max(m8[:, t, :], ex[:, t, :])
                dve.drain()
                dve.tensor_copy(top2[:, :, 0:2], m8[:, :, 0:2])
                dve.tensor_tensor(r4[:], m8[:, :, 0], m8[:, :, 1], ALU.add)
                dve.drain()
                dve.tensor_scalar(r4[:], r4[:], 1e-9, None, ALU.max)
                for t in range(CH):
                    dve.match_replace(rest[:, t, :], top2[:, t, :], ex[:, t, :], 0.0)
                dve.drain()
                dve.reciprocal(r4[:], r4[:])
                dve.tensor_tensor(rest[:], ex[:], rest[:], ALU.subtract)
                dve.drain()
                dve.tensor_tensor(combc[:], rest[:], bc(r4[:], NE), ALU.mult)
                dve.tensor_tensor(comb[:, bass.ds(c * CH, CH), :], rest[:], bc(r4[:], NE), ALU.mult).then_inc(c_comb, 1)
                dve.wait_ge(c_yb, c + 1)
                dve.scalar_tensor_tensor(acc[:, bass.ds(c * CH, CH), :].rearrange("p t d -> p (t d)"),
                                         x1c[:].rearrange("p t d -> p (t d)"), 2.0, bank(5),
                                         ALU.mult, ALU.add).then_inc(c_acc, 1)
                dve.drain()
            end_phase(dve, 3)
            dve.sem_inc(acc_done, 2)
            with dve.Fori(0, NE // 2) as i:
                for u in range(2 * NC):
                    dve.wait_ge(y_ready, i * 2 * NC + u + 1 + 2)
                    for t in range(CH):
                        tt = (u % NC) * CH + t
                        last = dve.scalar_tensor_tensor(
                            acc[:, tt, :], bank(4 + u % 2)[:, t * P:(t + 1) * P],
                            comb[:, tt, bass.ds(i * 2 + u // NC, 1)], acc[:, tt, :], ALU.mult, ALU.add)
                    dve.drain().then_inc(acc_done, 1)
            end_phase(dve, 4)
            with dve.Fori(0, B // 2) as i:
                b0 = i * 4
                for s in range(2):
                    ln_stats(lambda t: acc[:, b0 + (2 * s + t), :], TB, s, e_var)
                for s in range(2):
                    dve.wait_ge(e_rstd, i * 4 + s + 1)
                    ln_apply(lambda t: x2[s][:, t, :], lambda t: acc[:, b0 + (2 * s + t), :], TB, s).then_inc(e_x2, 1)
                for s in range(2):
                    dve.wait_ge(e_ssq, i * 2 + s + 1)
                    dve.tensor_scalar(mq[s][:], ssq[s][:], 1e-12, None, ALU.max).then_inc(e_mq, 1)
                dve.drain()
                for s in range(2):
                    dve.wait_ge(e_rn, i * 2 + s + 1)
                    for t in range(TB):
                        last = dve.tensor_scalar(nrm[s][:, t, :], x2[s][:, t, :], rn[s][:, t:t + 1], None, ALU.mult)
                    last.then_inc(e_nrm, 1)
                for s in range(2):
                    dve.wait_ge(e_log, i * 2 + s + 1)
                    dve.scalar_tensor_tensor(sp[s][:], zb[s][:], 0.0, az[s][:], ALU.max, ALU.add).then_inc(e_sp, 1)
                for s in range(2):
                    dve.wait_ge(e_oT, i * 2 + s + 1)
                    dve.tensor_tensor(x2[s][:], x2[s][:], bank(6 + s)[:, S:2 * S].rearrange("p (t d) -> p t d", t=TB), ALU.add)
                    dve.drain()
                    ln_stats(lambda t: x2[s][:, t, :], TB, s, e_var)
                for s in range(2):
                    dve.wait_ge(e_rstd, i * 4 + s + 3)
                    ln_apply(lambda t: x3[:, b0 + (2 * s + t), :], lambda t: x2[s][:, t, :], TB, s).then_inc(e_x3, 1)
                dve.drain()
            end_phase(dve, 5)
            dve.wait_ge(f_zero, 1)
            dve.sem_inc(f_x, B)

            def rotate(m, i):
                j, t = 1 - i // 2, i % 2
                dve.wait_ge(f_sq, m * 4 + i + 1)
                if i % 2 == 0 and later(m):
                    dve.wait_ge((f_rk, f_rq)[i // 2], m)
                o3 = lambda v: v.rearrange("p (h k) -> p h k", k=DH)
                dve.tensor_reduce(ss[:, t, j * H1:(j + 1) * H1], o3(sq1[i % 2]), AX.X, ALU.add)
                if later(m * 4 + i - 1):
                    dve.wait_ge(f_add, m * 4 + i - 1)
                src = o3(bank(MBANK[i]))
                o1, o2 = o3(t1[i % 2]), o3(t2[i % 2])
                ca = rotc[:, 2 * j, t, :].unsqueeze(1).to_broadcast([P, H1, DH])
                cb = rotc[:, 2 * j + 1, t, :].unsqueeze(1).to_broadcast([P, H1, DH])
                dve.tensor_tensor(o1, src, ca, ALU.mult)
                dve.tensor_tensor(o2[:, :, 0:32], src[:, :, 32:64], cb[:, :, 0:32], ALU.mult)
                dve.tensor_tensor(o2[:, :, 32:64], src[:, :, 0:32], cb[:, :, 32:64], ALU.mult).then_inc(f_rot, 1)
                if i % 2 == 1:
                    dve.drain()
                    dve.tensor_scalar(ss[:, :, j * H1:(j + 1) * H1], ss[:, :, j * H1:(j + 1) * H1], 1e-24, None,
                                      ALU.max).then_inc(f_ss, 1)

            def query_scales(m, s):
                dve.wait_ge(f_rq, m + 1)
                dve.tensor_scalar(rq8[s][:], rqk[:, :, 0:H1], 8.0, None, ALU.mult)
                dve.tensor_scalar(nrq8[s][:], rqk[:, :, 0:H1], -8.0, None, ALU.mult).then_inc(f_rq8, 1)

            def neg_max(m, s, a):
                k = a % 2
                dve.wait_ge(f_s, m * 4 + a + 1)
                dve.tensor_reduce(mx1[k][:, 0, :], bank(0)[:, 0:2 * P].rearrange("p (h n) -> p h n", h=2), AX.X, ALU.max)
                dve.tensor_reduce(mx1[k][:, 1, :], bank(1)[:, 0:384].rearrange("p (h n) -> p h n", h=2), AX.X, ALU.max)
                dve.drain()
                dve.tensor_tensor(nb1[k][:], mx1[k][:], nrq8[s][:, :, 2 * a:2 * a + 2], ALU.mult).then_inc(f_nb, 1)

            def normalise1(m, a):
                k = a % 2
                dve.wait_ge(f_e, m * 4 + a + 1)
                dve.reciprocal(rs1[k][:], sm1[k][:])
                dve.drain()
                for h in range(2):
                    dve.tensor_scalar(p0[k][:, h, :], p0[k][:, h, :], rs1[k][:, 0, h:h + 1], None, ALU.mult)
                    last = dve.tensor_scalar(p1[k][:, h, WIN:S], p1[k][:, h, WIN:S], rs1[k][:, 1, h:h + 1], None, ALU.mult)
                last.then_inc(f_p, 1)

            def probs_out(m, a):
                dve.wait_ge(f_t, m * 4 + a + 1)
                dve.tensor_copy(pt1[1][:], bank(3)[:, 0:3 * P]).then_inc(f_pt1, 1)

            def residual_mid(m, s):
                dve.wait_ge(f_wo, m + 1)
                dve.tensor_tensor(xm[s][:], stream[:, bass.ds(m * TB, TB), :],
                                  bank(6)[:, 0:S].rearrange("p (t d) -> p t d", t=TB), ALU.add).then_inc(f_xm, 1)

            def residual_out(m, s):
                dve.wait_ge(f_w2, m + 1)
                dve.tensor_tensor(stream[:, bass.ds(m * TB + NT, TB), :], xm[s][:],
                                  bank(7)[:, 0:S].rearrange("p (t d) -> p t d", t=TB), ALU.add).then_inc(f_x, 1)

            def stats_mid(m):
                dve.wait_ge(f_sh, m + 1)
                ln_stats(lambda t: bank(7)[:, t * P:(t + 1) * P], TB, 0, f_var)

            def normed_mid(m):
                dve.wait_ge(f_rstd, m + 1)
                ln_apply(lambda t: hn[:, t, :], lambda t: bank(7)[:, t * P:(t + 1) * P], TB, 0).then_inc(f_hn, 1)

            def gate(m, c):
                w = FCH[c][1]
                dve.wait_ge(f_gl, m * 3 + c + 1)
                dve.scalar_tensor_tensor(hg[0:w, c, :], bank(GBANK[c])[0:w, S:2 * S], lv[0:w, 2 + c:3 + c],
                                         gl[0:w, c, :], ALU.add, ALU.mult).then_inc(f_hg, 1)

            def step(n, s):
                if live(n):
                    normalise1(n, 0)
                    neg_max(n, s, 1)
                if live(n + 2):
                    rotate(n + 2, 0)
                if live(n):
                    probs_out(n, 0)
                if live(n - 1):
                    residual_mid(n - 1, 1 - s)
                if live(n - 2):
                    residual_out(n - 2, s)
                if live(n):
                    normalise1(n, 1)
                    neg_max(n, s, 2)
                if live(n + 2):
                    rotate(n + 2, 1)
                if live(n):
                    probs_out(n, 1)
                if live(n - 1):
                    stats_mid(n - 1)
                if live(n + 2):
                    rotate(n + 2, 2)
                if live(n):
                    normalise1(n, 2)
                    neg_max(n, s, 3)
                if live(n - 1):
                    normed_mid(n - 1)
                if live(n):
                    probs_out(n, 2)
                if live(n + 2):
                    rotate(n + 2, 3)
                if live(n + 1):
                    query_scales(n + 1, 1 - s)
                if live(n):
                    normalise1(n, 3)
                if live(n + 1):
                    neg_max(n + 1, 1 - s, 0)
                if live(n):
                    probs_out(n, 3)
                if live(n - 1):
                    for c in range(3):
                        gate(n - 1, c)

            run_steps(dve, step)
            end_phase(dve, 6)
            for c in range(NC):
                x5c = x5[:, c * CH:(c + 1) * CH, :]
                dve.tensor_tensor(x5c, x5c, x3[:, c * CH:(c + 1) * CH, :], ALU.add)
            dve.drain()
            for c in range(NC + 1):
                if c < NC:
                    ln_stats(lambda t: x5[:, c * CH + t, :], CH, c % 2, h_var)
                if c > 0:
                    dve.wait_ge(h_rstd, c)
                    ln_apply(lambda t: x5[:, (c - 1) * CH + t, :], lambda t: x5[:, (c - 1) * CH + t, :], CH,
                             (c - 1) % 2).then_inc(h_out, 1)


N_W = 24


_INS = ['L0_attn_resid_pre', 'L0_attn_W_Q', 'L0_attn_b_Q', 'L0_attn_W_K', 'L0_attn_b_K', 'L0_attn_W_V',
        'L0_attn_b_V', 'L0_attn_W_O', 'L0_attn_b_O', 'L0_attn_ln1_w', 'L0_attn_ln1_b', 'L0_attn_ln2_w',
        'L0_attn_ln2_b', 'L0_ffn_Wr', 'L0_ffn_br', 'L0_ffn_W1', 'L0_ffn_b1', 'L0_ffn_W2', 'L0_ffn_b2',
        'L1_attn_W1', 'L1_attn_b1', 'L1_attn_W2', 'L1_ffn_wqkv', 'L1_ffn_q_scale', 'L1_ffn_k_scale',
        'L1_ffn_wo', 'L1_ffn_ln_g', 'L1_ffn_ln_b', 'L1_ffn_w1', 'L1_ffn_b1', 'L1_ffn_w2', 'L1_ffn_b2']


def rotary_tables():
    import numpy as np
    half = np.arange(0, DH, 2, dtype=np.float32)
    inv = (1.0 / np.float32(10000.0) ** (half / np.float32(DH))).astype(np.float32)
    t = np.arange(S, dtype=np.float32)
    freqs = t[:, None] * inv[None, :]
    base = ((half + np.float32(0.4 * DH)) / np.float32(1.4 * DH)).astype(np.float32)
    power = ((t - S // 2) / np.float32(WIN // 2)).astype(np.float32)
    scale = (base[None, :] ** power[:, None]).astype(np.float32)
    cos, sin = np.cos(freqs), np.sin(freqs)
    return np.stack([np.concatenate([cos * scale, cos * scale], -1),
                     np.concatenate([-sin * scale, sin * scale], -1),
                     np.concatenate([cos / scale, cos / scale], -1),
                     np.concatenate([-sin / scale, sin / scale], -1)]).astype(np.float32)


def kernel(**inputs):
    import numpy as np
    import concourse.bacc as bacc
    from concourse.bass_utils import run_bass_kernel_spmd

    nc = bacc.Bacc("TRN2", target_bir_lowering=False, num_devices=1)
    arrays, A = {}, {}
    for name in _INS + ["tables"]:
        a = rotary_tables() if name == "tables" else np.ascontiguousarray(inputs[name])
        arrays[f"in_{name}"] = a
        A[name] = nc.dram_tensor(f"in_{name}", a.shape, mybir.dt.from_np(a.dtype), kind="ExternalInput").ap()
    out = nc.dram_tensor("out_0", (B, S, D), F32, kind="ExternalOutput").ap()
    build_program(nc, A, out)
    r = run_bass_kernel_spmd(nc, [arrays], core_ids=[0])
    return r.results[0]["out_0"]
```

```python
import concourse.bass as bass
from concourse import mybir
from contextlib import ExitStack

F32 = mybir.dt.float32
BF16 = mybir.dt.bfloat16
I32 = mybir.dt.int32
ALU = mybir.AluOpType
ACT = mybir.ActivationFunctionType
AX = mybir.AxisListType

P = 128
D = 128
B, S = 8, 256
TB = S // P
NT = B * TB
CH = 4
NC = NT // CH
EPS = 1e-5

H0, DH = 16, 64
PAIRS0 = H0 // 2
SLOTS = B * PAIRS0
WCOLS = 3 * P + 2

NE, HE = 16, 256
KE = HE // P

LAYERS, H1, WIN = 2, 8, 64
INNER = H1 * DH
PAIRS1 = H1 // 2
HID = 341
FCH = [(0, 128), (128, 128), (256, HID - 256)]
SCRATCH = 11264
NEG = -1e30

R_BQ, R_BK, R_BV, R_BO, R_LN1W, R_LN1B, R_CB1 = 0, 8, 16, 24, 25, 26, 27
R_B1, R_LV = 28, 60
LV = 8
FREE = 1


def build_program(nc, A, out):
    with ExitStack() as ctx:
        def sb(name, shape, dt=F32):
            return ctx.enter_context(nc.sbuf_tensor(name, shape, dt))

        def sem(name):
            return ctx.enter_context(nc.semaphore(name))

        psum = ctx.enter_context(nc.psum_tensor("psum", [P, 8, 512], F32))

        def bank(k):
            return psum[:, k, :]

        ident = sb("ident", [P, P])
        identb = sb("identb", [P, P], BF16)
        causal = sb("causal", [P, P])
        band0 = sb("band0", [P, 2, P], BF16)
        band1 = sb("band1", [P, 2, 192], BF16)
        shift = sb("shift", [P, P])
        carry = sb("carry", [P, P])
        mhalf = sb("mhalf", [P, TB * H1])
        onecol = sb("onecol", [P, 1])
        zrow = sb("zrow", [P, 1])
        vrows = sb("vrows", [P, P])
        vec = sb("vec", [P, P])
        bo_all = sb("bo_all", [P, D])
        w_qkv0 = sb("w_qkv0", [P, PAIRS0, WCOLS])
        w_o0 = sb("w_o0", [P, PAIRS0, D])
        ln2w = sb("ln2w", [P, D])
        ln2b = sb("ln2b", [P, D])
        w_r = sb("w_r", [P, NE])
        br = sb("br", [P, NE])
        b2e = sb("b2e", [NE, D])
        w1c = sb("w1c", [P, D])
        w2c = sb("w2c", [P, 2, D])
        wqkv1 = sb("wqkv1", [P, 3 * INNER])
        wo1 = sb("wo1", [P, PAIRS1, D])
        wf1 = sb("wf1", [P, 2 * HID])
        wf2 = sb("wf2", [P, 3, D])
        lv = sb("lv", [P, LV])
        rotc = sb("rotc", [P, 4, TB, DH])
        tab = sb("tab", [P, 4, TB, DH])
        qks = sb("qks", [P, 2, LAYERS, DH])
        rot = sb("rot", [P, LAYERS, 4, TB, DH])

        stream = sb("stream", [P, 3 * NT, D])
        x3 = stream[:, 0:NT, :]
        acc = stream[:, NT:2 * NT, :]
        x0 = stream[:, 2 * NT:3 * NT, :]
        x5 = x0
        big = sb("big", [P, SLOTS * S])
        zT = big[:, :].rearrange("p (g n) -> p g n", n=S)
        scratch = sb("scratch", [P, SCRATCH])
        at = [0, 0]

        def shaped(v, dims):
            if len(dims) == 1:
                return v
            names = "abcd"[:len(dims)]
            return v.rearrange(f"p ({' '.join(names)}) -> p {' '.join(names)}", **dict(zip(names, dims)))

        def carve(which, dims, dt=F32):
            n = 1
            for d in dims:
                n *= d
            a = at[which]
            at[which] = a + n
            assert at[which] <= (SLOTS * S, SCRATCH)[which], (which, at)
            return shaped((big, scratch)[which][:, a:a + n], dims)

        def from_big(*dims):
            return carve(0, dims)

        def from_scratch(*dims):
            return carve(1, dims)
        xT = sb("xT", [P, NT * P])
        comb = sb("comb", [P, NT, NE])

        st = sb("st", [P, 4, CH, 6])
        mv = sb("mv", [P, 4, CH, 2])
        ve = sb("ve", [P, 4, CH])
        rstd = sb("rstd", [P, 4, CH])

        x_in = sem("x_in")
        w_in = sem("w_in")
        rows_zero = sem("rows_zero")
        rows_in = sem("rows_in")
        const_ready = sem("const_ready")
        vec_ps = sem("vec_ps")
        vec_ready = sem("vec_ready")
        bo_ps = sem("bo_ps")
        phase_done = sem("phase_done")

        def apart(eng):
            eng.wait_ge(const_ready, 1)

        def c_count(c, which):
            return min(2 * c + 3, 2 * NC) if which else max(2 * c, 1)

        def end_phase(eng, n):
            eng.drain().then_inc(phase_done, 1)
            eng.wait_ge(phase_done, 4 * n)

        a_var, a_rstd, a_xn, a_tr, a_xt = (sem(f"a_{n}") for n in ("var", "rstd", "xn", "tr", "xt"))
        xn = sb("xn", [P, CH, D])
        bv_wide = xn[:]
        bv_ready = sem("bv_ready")
        bo_ready = sem("bo_ready")

        wst = [from_scratch(WCOLS) for i in range(2)]
        xst = [from_scratch(S) for i in range(2)]
        qT = [from_scratch(S) for i in range(2)]
        kZ = [from_scratch(2, S) for i in range(2)]
        vS = [from_scratch(TB, P) for i in range(2)]
        pr = [from_scratch(TB, 2, S) for i in range(2)]
        pt = [from_scratch(TB * S) for i in range(2)]
        mx = from_scratch(4)
        nb = [from_scratch(4) for i in range(2)]
        sm = [from_scratch(4) for i in range(2)]
        rs = from_scratch(4)
        staged = [sem(f"b_staged{i}") for i in range(2)]
        (b_zero, b_qk, b_qksb, b_v, b_vsb, b_s, b_nb, b_e, b_p, b_t0, b_t1, b_pt0, b_pt1, b_z, b_zsb) = (
            sem(f"b_{n}") for n in ("zero", "qk", "qksb", "v", "vsb", "s", "nb", "e", "p", "t0", "t1",
                                    "pt0", "pt1", "z", "zsb"))

        def score_bank(s, t):
            return bank(2 * s + t)

        def slot_live(g):
            return not isinstance(g, int) or 0 <= g < SLOTS

        def later(count):
            return not isinstance(count, int) or count > 0

        def run_slots(eng, slot):
            full = (2, SLOTS - 4)
            for g in range(-3, full[0]):
                slot(g, g % 2, g // 2)
            with eng.Fori(0, (full[1] - full[0]) // 2) as i:
                for s in range(2):
                    slot(i * 2 + (full[0] + s), s, i + full[0] // 2)
            for g in range(full[1], SLOTS):
                slot(g, g % 2, g // 2)

        at[1] = 0
        mid = [from_scratch(CH, D) for i in range(2)]
        uC = [from_scratch(CH, D) for i in range(2)]
        lg = from_scratch(NT, NE)
        ex = from_scratch(NT, NE)
        rmax = from_scratch(NT)
        rsum = from_scratch(NT)
        m8 = from_scratch(NT, 8)
        top2 = from_scratch(NT, 8)
        rest = from_scratch(NT, NE)
        combT = [from_scratch(CH * P)[0:NE] for i in range(2)]
        (c_x0, c_top, c_o, c_mid, c_u, c_var, c_rstd, c_x1, c_xtps, c_xt, c_lg, c_sub, c_exp, c_comb,
         c_ctps, c_ct, c_yb, c_acc) = (sem(f"c_{n}") for n in (
             "x0", "top", "o", "mid", "u", "var", "rstd", "x1", "xtps", "xt", "lg", "sub", "exp",
             "comb", "ctps", "ct", "yb", "acc"))

        at[0] = 0
        w1e = [sb(f"w1e{i}", [P, HE]) for i in range(2)]
        w2e = [sb(f"w2e{i}", [P, KE, D]) for i in range(2)]
        gE = [from_scratch(KE, CH * P) for i in range(2)]
        b1x = [from_scratch(KE) for i in range(2)]
        we_in = [sem(f"we_in{i}") for i in range(2)]
        u_ready, g_ready, y_ready, acc_done = (sem(n) for n in ("u_ready", "g_ready", "y_ready", "acc_done"))

        at[0] = 0

        def two(make, *dims):
            return [make(*dims) for _ in range(2)]

        x2 = [from_big(TB, D) for _ in range(4)]
        sqj = two(from_big, TB, D)
        ssq = two(from_big, TB)
        mq = two(from_big, TB)
        rn = two(from_big, TB)
        nrm = two(from_big, TB, D)
        xnT = two(from_big, 2 * S)
        rel = two(from_big, TB * S)
        zb = two(from_big, S)
        az = two(from_big, S)
        sp = two(from_big, S)
        (e_var, e_rstd, e_x2, e_ssq, e_mq, e_rn, e_nrm, e_xnps, e_xn, e_sim, e_rel, e_ctr, e_zb, e_log, e_sp,
         e_o, e_y, e_yvar, e_yrstd, e_x3) = (sem(f"e_{n}") for n in (
             "var", "rstd", "x2", "ssq", "mq", "rn", "nrm", "xnps", "xn", "sim", "rel", "ctr", "zb", "log",
             "sp", "o", "y", "yvar", "yrstd", "x3"))

        def batch_live(b):
            return 0 <= b < B

        def run_batches(eng, batch):
            for b in range(-2, B):
                batch(b)

        at[0], at[1] = 0, 0
        v1 = two(from_big, TB, INNER)
        sq1 = two(from_big, INNER)
        t1 = two(from_big, INNER)
        t2 = two(from_big, INNER)
        qk = [two(from_big, 2 * INNER) for _ in range(2)]
        q1T = two(from_big, PAIRS1, S)
        k1Z = two(from_big, PAIRS1, 2, S)
        xc = from_scratch(TB, D)
        hT = two(from_scratch, S)
        p0 = two(from_scratch, 2, P)
        p1 = two(from_scratch, 2, S)
        pt1 = two(from_scratch, 3 * P)
        ss = from_scratch(TB, 2 * H1)
        rqk = from_scratch(TB, 2 * H1)
        rq8 = two(from_scratch, TB, H1)
        nrq8 = two(from_scratch, TB, H1)
        mx1 = two(from_scratch, TB, 2)
        nb1 = two(from_scratch, TB, 2)
        sm1 = two(from_scratch, TB, 2)
        rs1 = two(from_scratch, TB, 2)
        oT1 = two(from_scratch, PAIRS1, S)
        xm = two(from_scratch, TB, D)
        hn = from_scratch(TB, D)
        h2T = from_scratch(S)
        gl = from_scratch(3, S)
        hg = from_scratch(3, S)
        UNITS = LAYERS * B
        (f_xc, f_xT, f_hT, f_qk, f_sq, f_rot, f_add, f_ss, f_rk, f_kn, f_rq, f_rq8, f_vps, f_v, f_tr, f_trs,
         f_s, f_nb, f_e, f_p, f_t, f_pt0, f_pt1, f_z, f_zsb, f_wo, f_xm, f_sh, f_var, f_rstd, f_hn,
         f_h2ps, f_h2, f_g, f_a, f_gl, f_hg, f_w2, f_x, f_zero, f_wqk, f_wv, f_wwo, f_wf1, f_wf2) = (
             sem(f"f_{n}") for n in (
                 "xc", "xT", "hT", "qk", "sq", "rot", "add", "ss", "rk", "kn", "rq", "rq8", "vps", "v", "tr",
                 "trs", "s", "nb", "e", "p", "t", "pt0", "pt1", "z", "zsb", "wo", "xm", "sh", "var", "rstd",
                 "hn", "h2ps", "h2", "g", "a", "gl", "hg", "w2", "x", "zero", "wqk", "wv", "wwo", "wf1", "wf2"))
        layer_in = sem("layer_in")
        h_var, h_rstd, h_out = sem("h_var"), sem("h_rstd"), sem("h_out")

        def live(m):
            return not isinstance(m, int) or 0 <= m < UNITS

        def hidden_bank(half_, c):
            return bank(7)[0:FCH[c][1], c * S:(c + 1) * S] if c < 2 else bank(6)[0:FCH[c][1], half_ * S:(half_ + 1) * S]

        def run_steps(eng, step):
            full = (2, 12)
            for n in range(-3, full[0]):
                step(n, n % 2)
            with eng.Fori(0, (full[1] - full[0]) // 2) as i:
                for s in range(2):
                    step(i * 2 + (full[0] + s), s)
            for n in range(full[1], UNITS + 2):
                step(n, n % 2)

        out_sem = sem("out_sem")

        N_ROWS = 23
        block = ctx.enter_context(nc.Block())

        @block.sync
        def _(sp_):
            sp_.dma_start(x0[:], A["L0_attn_resid_pre"].rearrange("b (t p) d -> p (b t) d", p=P)).then_inc(x_in, 16)
            sp_.wait_ge(rows_zero, 1)

            def rows(r, n, src, w=P):
                sp_.dma_start(vrows[r:r + n, 0:w], src).then_inc(rows_in, 16)

            one = lambda name: A[name].rearrange("(a d) -> a d", a=1)
            rows(R_LN1W, 1, one("L0_attn_ln1_w"))
            rows(R_LN1B, 1, one("L0_attn_ln1_b"))
            for r, name in ((R_BQ, "Q"), (R_BK, "K"), (R_BV, "V")):
                rows(r, PAIRS0, A[f"L0_attn_b_{name}"].rearrange("(a two) k -> a (two k)", two=2))
            rows(R_CB1, 1, one("L1_attn_b1"))
            rows(R_B1, NE * KE, A["L0_ffn_b1"].rearrange("e (k p) -> (e k) p", p=P))
            for la in range(LAYERS):
                rows(R_LV + LV * la, 1, A["L1_ffn_ln_g"][la:la + 1, :])
                rows(R_LV + LV * la + 1, 1, A["L1_ffn_ln_b"][la:la + 1, :])
                for half in range(2):
                    for c, (o, w) in enumerate(FCH):
                        rows(R_LV + LV * la + 2 + 3 * half + c, 1,
                             A["L1_ffn_b1"][la:la + 1, half * HID + o:half * HID + o + w], w)
            n = [0]

            def layer1_load(load, la, parts):
                if "qk" in parts:
                    load(wqkv1[:, 0:2 * INNER], A["L1_ffn_wqkv"][la, :, 0:2 * INNER])
                if "v" in parts:
                    load(wqkv1[:, 2 * INNER:], A["L1_ffn_wqkv"][la, :, 2 * INNER:])
                if "o" in parts:
                    load(wo1[:], A["L1_ffn_wo"][la].rearrange("(a p) d -> p a d", p=P))
                if "f1" in parts:
                    load(wf1[:], A["L1_ffn_w1"][la])
                if "f2" in parts:
                    load(wf2[:, 0:2, :], A["L1_ffn_w2"][la, 0:256, :].rearrange("(c p) d -> p c d", p=P))
                    load(wf2[0:HID - 256, 2, :], A["L1_ffn_w2"][la, 256:HID, :])
                    load(wf2[HID - 256:HID - 255, 2, :], A["L1_ffn_b2"][la:la + 1, :])

            def load(dst, src):
                sp_.dma_start(dst, src).then_inc(w_in, 16)
                n[0] += 1

            for j, name in enumerate("QKV"):
                for h in range(2):
                    o = j * P + h * DH
                    load(w_qkv0[:, :, o:o + DH],
                         A[f"L0_attn_W_{name}"].rearrange("(a two) d k -> two d a k", two=2)[h])
            load(w_o0[:], A["L0_attn_W_O"].rearrange("h k d -> (h k) d").rearrange("(a p) d -> p a d", p=P))
            load(bo_all[:], A["L0_attn_b_O"].partition_broadcast(P))
            load(ln2w[:], A["L0_attn_ln2_w"].partition_broadcast(P))
            load(ln2b[:], A["L0_attn_ln2_b"].partition_broadcast(P))
            load(w_r[:], A["L0_ffn_Wr"])
            load(br[:], A["L0_ffn_br"].partition_broadcast(P))
            load(b2e[:], A["L0_ffn_b2"])
            load(w1c[:], A["L1_attn_W1"].rearrange("a d -> (a d)").partition_broadcast(P))
            load(w2c[:], A["L1_attn_W2"].rearrange("(a p) d -> p a d", p=P))
            load(tab[:], A["tables"].rearrange("j (t p) k -> p j t k", p=P))
            for j, name in enumerate(("q", "k")):
                load(qks[:, j], A[f"L1_ffn_{name}_scale"].rearrange("a b -> (a b)").partition_broadcast(P)
                     .rearrange("p (a b) -> p a b", a=LAYERS))
            layer1_load(load, 0, ("qk", "v", "o", "f1", "f2"))
            assert n[0] == N_W
            for e in range(2):
                sp_.dma_start(w1e[e][:], A["L0_ffn_W1"][e]).then_inc(we_in[e], 16)
                sp_.dma_start(w2e[e][:], A["L0_ffn_W2"][e].rearrange("(k p) d -> p k d", p=P)).then_inc(we_in[e], 16)
            sp_.wait_ge(phase_done, 4)

            def stage(b, a, g, s):
                if later(g - 1):
                    sp_.wait_ge(b_v, g - 1)
                    sp_.wait_ge(b_qksb, g - 1)
                sp_.dma_start(wst[s][:], w_qkv0[:, a, :]).then_inc(staged[s], 16)
                sp_.dma_start(xst[s][:], xT[:, bass.ds(b * S, S)]).then_inc(staged[s], 16)

            for a in range(PAIRS0):
                stage(0, a, a, a % 2)
            with sp_.Fori(1, B) as b:
                with sp_.Fori(0, PAIRS0 // 2) as pp:
                    for s in range(2):
                        stage(b, pp * 2 + s, b * PAIRS0 + pp * 2 + s, s)
            with sp_.Fori(1, NE // 2) as i:
                for e in range(2):
                    sp_.wait_ge(y_ready, i * (2 * NC) + ((e - 1) * NC + 2))
                    sp_.dma_start(w1e[e][:], A["L0_ffn_W1"][i * 2 + e]).then_inc(we_in[e], 16)
                    sp_.dma_start(w2e[e][:], A["L0_ffn_W2"][i * 2 + e].rearrange("(k p) d -> p k d", p=P)).then_inc(we_in[e], 16)
            sp_.wait_ge(phase_done, 16)
            sp_.dma_start(lv[:], vec[:, R_LV:R_LV + LV]).then_inc(layer_in, 16)
            sp_.dma_start(rotc[:], rot[:, 0]).then_inc(layer_in, 16)
            sp_.wait_ge(layer_in, 32)
            n_in = [32]

            def second(dst, src_):
                sp_.dma_start(dst, src_).then_inc(layer_in, 16)
                n_in[0] += 16

            for ready in (f_wqk, f_wv, f_wwo, f_wf1, f_wf2):
                sp_.sem_inc(ready, B)
            sp_.wait_ge(f_rot, 4 * B)
            second(rotc[:], rot[:, 1])
            layer1_load(second, 1, ("qk",))
            sp_.wait_ge(layer_in, n_in[0])
            sp_.sem_inc(f_wqk, B)
            sp_.wait_ge(f_vps, 2 * B)
            layer1_load(second, 1, ("v",))
            sp_.wait_ge(layer_in, n_in[0])
            sp_.sem_inc(f_wv, B)
            sp_.wait_ge(f_wo, B)
            layer1_load(second, 1, ("o",))
            sp_.wait_ge(layer_in, n_in[0])
            sp_.sem_inc(f_wwo, B)
            sp_.wait_ge(f_hg, B)
            second(lv[:], vec[:, R_LV + LV:R_LV + 2 * LV])
            layer1_load(second, 1, ("f1",))
            sp_.wait_ge(layer_in, n_in[0])
            sp_.sem_inc(f_wf1, B)
            sp_.wait_ge(f_w2, B)
            layer1_load(second, 1, ("f2",))
            sp_.wait_ge(layer_in, n_in[0])
            sp_.sem_inc(f_wf2, B)
            outc = out.rearrange("b (t p) d -> p (b t) d", p=P)
            for c in range(NC):
                sp_.wait_ge(h_out, c + 1)
                sp_.dma_start(outc[:, c * CH:(c + 1) * CH, :], x5[:, c * CH:(c + 1) * CH, :]).then_inc(out_sem, 16)
            sp_.wait_ge(out_sem, 16 * NC)

        @block.gpsimd
        def _(pool):
            pool.memset(mhalf[:], -0.5)
            pool.memset(onecol[:], 1.0)
            pool.memset(ident[:], 0.0)
            pool.memset(causal[:], 1.0)
            pool.memset(band0[:], 0.0)
            pool.memset(band1[:], 0.0)
            pool.memset(shift[:], 0.0)
            pool.memset(carry[:], 0.0)
            pool.drain()
            pool.affine_select(out=ident[:], in_=ident[:], compare_op=ALU.not_equal, fill=1.0, base=0,
                               pattern=[[-1, P]], channel_multiplier=1)
            pool.affine_select(out=causal[:], in_=causal[:], compare_op=ALU.is_ge, fill=0.0, base=0,
                               pattern=[[-1, P]], channel_multiplier=1)
            pool.affine_select(out=band0[:], in_=band0[:], compare_op=ALU.is_ge, fill=NEG, base=0,
                               pattern=[[0, 2], [-1, P]], channel_multiplier=1)
            pool.affine_select(out=band1[:], in_=band1[:], compare_op=ALU.is_ge, fill=NEG, base=WIN,
                               pattern=[[0, 2], [-1, 192]], channel_multiplier=1)
            pool.affine_select(out=shift[:], in_=shift[:], compare_op=ALU.not_equal, fill=1.0, base=1,
                               pattern=[[-1, P]], channel_multiplier=1)
            pool.affine_select(out=carry[:], in_=carry[:], compare_op=ALU.not_equal, fill=1.0,
                               base=-(P - 1), pattern=[[-1, P]], channel_multiplier=1)
            pool.drain()
            pool.affine_select(out=band0[:], in_=band0[:], compare_op=ALU.is_ge, fill=NEG, base=WIN,
                               pattern=[[0, 2], [1, P]], channel_multiplier=-1)
            pool.affine_select(out=band1[:], in_=band1[:], compare_op=ALU.is_ge, fill=NEG, base=0,
                               pattern=[[0, 2], [1, 192]], channel_multiplier=-1)
            pool.tensor_copy(identb[:], ident[:])
            pool.drain().then_inc(const_ready, 1)
            with pool.Fori(0, NC) as c:
                pool.wait_ge(a_var, c + 1)
                pool.tensor_tensor(rstd[:, 0, :], ve[:, 0, :], mhalf[:, 0:CH], ALU.pow).then_inc(a_rstd, 1)
            end_phase(pool, 1)
            for s in range(2):
                pool.memset(kZ[s][64:P, 0, :], 0.0)
                pool.memset(kZ[s][0:64, 1, :], 0.0)
            pool.drain().then_inc(b_zero, 1)
            pool.wait_ge(bo_ready, 1)
            pool.tensor_tensor(x3, x0, bo_all[:].unsqueeze(1).to_broadcast([P, NT, D]), ALU.add)
            pool.drain()
            pool.tensor_tensor(x0, x0, ln2b[:].unsqueeze(1).to_broadcast([P, NT, D]), ALU.add)
            pool.drain().then_inc(c_x0, 1)
            end_phase(pool, 2)
            pool.memset(top2[:], -1.0)
            pool.drain().then_inc(c_top, 1)

            def ln_rstd(c, which):
                k = 2 * (c % 2) + which
                pool.tensor_tensor(rstd[:, k, :], ve[:, k, :], mhalf[:, 0:CH], ALU.pow).then_inc(c_rstd, 1)

            for q in range(NC + 1):
                if q < NC:
                    pool.wait_ge(c_mid, q + 1)
                    pool.tensor_tensor(uC[q % 2], mid[q % 2], x0[:, q * CH:(q + 1) * CH, :], ALU.add).then_inc(c_u, 1)
                    pool.wait_ge(c_var, c_count(q, 0))
                    ln_rstd(q, 0)
                if q >= 1:
                    pool.wait_ge(c_var, c_count(q - 1, 1))
                    ln_rstd(q - 1, 1)
            end_phase(pool, 3)
            def norm_rstd(b):
                pool.wait_ge(e_var, b + 1)
                pool.tensor_tensor(rstd[:, b % 2, 0:TB], ve[:, b % 2, 0:TB], mhalf[:, 0:TB], ALU.pow).then_inc(e_rstd, 1)

            def inverse_norm0(b):
                pool.wait_ge(e_mq, b + 1)
                pool.tensor_tensor(rn[b % 2][:], mq[b % 2][:], mhalf[:, 0:TB], ALU.pow).then_inc(e_rn, 1)

            def end_rstd(b):
                pool.wait_ge(e_yvar, b + 1)
                pool.tensor_tensor(rstd[:, 2 + b % 2, 0:TB], ve[:, 2 + b % 2, 0:TB], mhalf[:, 0:TB],
                                   ALU.pow).then_inc(e_yrstd, 1)

            def batch(b):
                if batch_live(b + 2): norm_rstd(b + 2)
                if batch_live(b): end_rstd(b)
                if batch_live(b + 2): inverse_norm0(b + 2)

            run_batches(pool, batch)
            end_phase(pool, 4)
            for s in range(2):
                pool.memset(k1Z[s][64:P, :, 0, :], 0.0)
                pool.drain()
                pool.memset(k1Z[s][0:64, :, 1, :], 0.0)
                pool.drain()
                pool.memset(p1[s][:, :, 0:WIN], 0.0)
                pool.drain()
                pool.memset(hT[s][64:P, 0:1], 0.0)
                pool.drain()
            pool.memset(hg[64:P, 2, :], 1.0)
            pool.drain().then_inc(f_zero, 1)
            half = mhalf[:].rearrange("p (t h) -> p t h", t=TB)

            def copy_x(m):
                pool.wait_ge(f_x, m + 1)
                if later(m):
                    pool.wait_ge(f_xT, m)
                apart(pool)
                pool.tensor_copy(xc[:], stream[:, bass.ds(m * TB, TB), :]).then_inc(f_xc, 1)

            def add_rot(m, s, i):
                j, t = 1 - i // 2, i % 2
                if later(m * 4 - 4):
                    pool.wait_ge(f_tr, m * 4 - 4)
                pool.wait_ge(f_rot, m * 4 + i + 1)
                pool.tensor_tensor(qk[s][t][:, j * INNER:(j + 1) * INNER], t1[i % 2], t2[i % 2],
                                   ALU.add).then_inc(f_add, 1)

            def inverse_norm(m, j):
                pool.wait_ge(f_ss, m * 2 + 2 - j)
                if j == 0 and later(m):
                    pool.wait_ge(f_rq8, m)
                o = rqk[:, :, j * H1:(j + 1) * H1]
                pool.tensor_tensor(o, ss[:, :, j * H1:(j + 1) * H1], half, ALU.pow).then_inc((f_rq, f_rk)[j], 1)

            def scale_keys(m, s):
                pool.drain()
                for t in range(TB):
                    kk = qk[s][t][:, INNER:].rearrange("p (h k) -> p h k", h=H1)
                    last = pool.tensor_tensor(kk, kk, rqk[:, t, H1:].unsqueeze(2).to_broadcast([P, H1, DH]), ALU.mult)
                last.then_inc(f_kn, 1)

            def ln_rstd(m):
                pool.wait_ge(f_var, m + 1)
                pool.tensor_tensor(rstd[:, 0, 0:TB], ve[:, 0, 0:TB], mhalf[:, 0:TB], ALU.pow).then_inc(f_rstd, 1)

            def step(n, s):
                if live(n + 2): add_rot(n + 2, s, 0)
                if live(n + 3): copy_x(n + 3)
                if live(n - 1): ln_rstd(n - 1)
                if live(n + 2): add_rot(n + 2, s, 1)
                if live(n + 2): add_rot(n + 2, s, 2)
                if live(n + 2): inverse_norm(n + 2, 1)
                if live(n + 2): scale_keys(n + 2, s)
                if live(n + 2): add_rot(n + 2, s, 3)
                if live(n + 2): inverse_norm(n + 2, 0)

            run_steps(pool, step)
            end_phase(pool, 5)
            for c in range(NC):
                pool.wait_ge(h_var, c + 1)
                pool.tensor_tensor(rstd[:, c % 2, :], ve[:, c % 2, :], mhalf[:, 0:CH], ALU.pow).then_inc(h_rstd, 1)

        @block.scalar
        def _(act):
            act.wait_ge(vec_ps, 1)
            act.activation(vec[:], bank(0)[:, 0:P], ACT.Copy).then_inc(vec_ready, 1)
            act.drain()
            for q in range(2):
                if q:
                    act.wait_ge(bo_ps, 1)
                act.activation(bv_wide, vec[:, R_BV + 4 * q:R_BV + 4 * q + 4].unsqueeze(2).to_broadcast([P, 4, P]),
                               ACT.Copy).then_inc(bv_ready, 1)
            act.wait_ge(w_in, 16 * N_W)
            act.activation(w_qkv0[:, :, 3 * P], vec[:, R_BQ:R_BQ + PAIRS0], ACT.Copy)
            act.activation(w_qkv0[:, :, 3 * P + 1], vec[:, R_BK:R_BK + PAIRS0], ACT.Copy)
            act.sem_inc(a_xt, FREE)
            with act.Fori(0, NC) as c:
                act.wait_ge(a_tr, c + 1 + FREE)
                apart(act)
                act.activation(xT[:, bass.ds(c * CH * P, CH * P)], bank(0), ACT.Identity,
                               scale=vec[:, R_LN1W:R_LN1W + 1], bias=vec[:, R_LN1B:R_LN1B + 1]).then_inc(a_xt, 1)
            end_phase(act, 1)
            act.wait_ge(b_zero, 2)

            def qk_out(g, s):
                act.wait_ge(b_qk, g + 1)
                if later(g - 1):
                    act.wait_ge(b_s, g - 1)
                act.activation(qT[s][:], bank(6)[:, 0:S], ACT.Identity, bias=wst[s][:, 3 * P:3 * P + 1])
                act.activation(kZ[s][0:64, 0, :], bank(6)[0:64, S:2 * S], ACT.Identity,
                               bias=wst[s][0:64, 3 * P + 1:3 * P + 2])
                act.activation(kZ[s][64:P, 1, :], bank(6)[64:P, S:2 * S], ACT.Identity,
                               bias=wst[s][64:P, 3 * P + 1:3 * P + 2]).then_inc(b_qksb, 1)

            def expo(g, s, t):
                act.wait_ge(b_nb, g + 1)
                if later(g - 1):
                    act.wait_ge(b_t1, g - 1)
                for h in range(2):
                    last = act.activation(pr[s][:, t, h, :], score_bank(s, t)[:, h * S:(h + 1) * S], ACT.Exp,
                                          bias=nb[s][:, 2 * t + h:2 * t + h + 1], scale=DH ** -0.5,
                                          accum_out=sm[s][:, 2 * t + h:2 * t + h + 1])
                last.then_inc(b_e, 1)

            def probs_out(g):
                act.wait_ge(b_t0, g + 1)
                if later(g):
                    act.wait_ge(b_z, g)
                act.activation(pt[0][:], bank(4), ACT.Copy).then_inc(b_pt0, 1)

            def z_out(g):
                act.wait_ge(b_z, g + 1)
                apart(act)
                act.activation(zT[:, g, :], bank(4)[:, 0:S], ACT.Copy).then_inc(b_zsb, 1)

            def slot(g, s, h):
                if slot_live(g): probs_out(g)
                if slot_live(g + 1): expo(g + 1, 1 - s, 0)
                if slot_live(g + 1): expo(g + 1, 1 - s, 1)
                if slot_live(g): z_out(g)
                if slot_live(g + 3): qk_out(g + 3, 1 - s)

            run_slots(act, slot)
            end_phase(act, 2)
            act.sem_inc(g_ready, 2)
            for c in range(NC):
                act.wait_ge(c_xtps, c + 1)
                act.activation(xT[:, c * CH * P:(c + 1) * CH * P], bank(4 + c % 2), ACT.Copy).then_inc(c_xt, 1)
            act.wait_ge(c_sub, 1)
            act.activation(ex[:], lg[:], ACT.Exp).then_inc(c_exp, 1)
            for c in range(NC):
                act.wait_ge(c_ctps, c + 1)
                if c >= 2:
                    act.wait_ge(c_yb, c - 1)
                act.activation(combT[c % 2], bank(6 + c % 2)[0:NE, :], ACT.Copy).then_inc(c_ct, 1)
            def gelu(n, u, e):
                if u % NC == 0:
                    act.activation(b1x[u // NC], vec[:, bass.ds(e * KE + R_B1, KE)], ACT.Copy)
                    act.drain()
                act.wait_ge(u_ready, n + 1)
                act.wait_ge(y_ready, n + 1)
                for kt in range(KE):
                    last = act.activation(gE[u % 2][:, kt, :], bank(2 * (u % 2) + kt), ACT.Gelu,
                                          bias=b1x[u // NC][:, kt:kt + 1])
                last.then_inc(g_ready, 1)

            with act.Fori(0, NE // 2) as i:
                for u in range(2 * NC):
                    gelu(i * 2 * NC + u, u, i * 2 + u // NC)
            end_phase(act, 3)
            act.preload_act_table_set("natural_log_exp_and_others")

            def squares(b):
                act.wait_ge(e_x2, b + 1)
                for t in range(TB):
                    last = act.activation(sqj[b % 2][:, t, :], x2[b % 4][:, t, :], ACT.Square,
                                          accum_out=ssq[b % 2][:, t:t + 1])
                last.then_inc(e_ssq, 1)

            def turned_out0(b):
                act.wait_ge(e_xnps, b + 1)
                if b >= 2:
                    act.wait_ge(e_o, b - 1)
                act.activation(xnT[b % 2][:], bank(b % 2), ACT.Copy).then_inc(e_xn, 1)

            def positive(b):
                act.wait_ge(e_sim, b + 1)
                act.activation(rel[b % 2][:], bank(2 + b % 2), ACT.Relu).then_inc(e_rel, 1)

            def counter_out(b):
                act.wait_ge(e_ctr, b + 1)
                z, a = zb[b % 2][:], az[b % 2][:]
                if b >= 2:
                    act.wait_ge(e_sp, b - 1)
                act.activation(z, bank(4 + b % 2)[:, 0:S], ACT.Identity, bias=vec[:, R_CB1:R_CB1 + 1])
                act.drain()
                act.activation(a, z, ACT.Abs)
                act.drain()
                act.activation(a, a, ACT.Exp, scale=-1.0)
                act.drain()
                act.activation(a, a, ACT.Ln, bias=onecol[:]).then_inc(e_log, 1)

            def batch(b):
                if batch_live(b + 1): positive(b + 1)
                if batch_live(b + 2): squares(b + 2)
                if batch_live(b + 1): counter_out(b + 1)
                if batch_live(b + 2): turned_out0(b + 2)

            run_batches(act, batch)
            end_phase(act, 4)
            act.wait_ge(f_zero, 1)

            def shift_in(m, s):
                act.wait_ge(f_xT, m + 1)
                if later(m - 1):
                    act.wait_ge(f_vps, m * 2 - 2)
                act.activation(hT[s][0:64, :], bank(5)[0:64, 0:S], ACT.Copy)
                act.activation(hT[s][64:P, 1:S], bank(5)[64:P, 0:S - 1], ACT.Copy).then_inc(f_hT, 1)

            def square(m, i):
                act.wait_ge(f_qk, m * 4 + i + 1)
                if later(m * 4 + i - 1):
                    act.wait_ge(f_rot, m * 4 + i - 1)
                act.activation(sq1[i % 2], bank(4), ACT.Square).then_inc(f_sq, 1)

            def value_out(m, s, t):
                act.wait_ge(f_vps, m * 2 + t + 1)
                if later(m * 4 - 4):
                    act.wait_ge(f_z, m * 4 - 4)
                act.activation(v1[s][:, t, :], bank(4 + t), ACT.Copy).then_inc(f_v, 1)

            def turned_out(m, s, u):
                act.wait_ge(f_tr, m * 4 + u + 1)
                if later(m * 4 - 4):
                    act.wait_ge(f_s, m * 4 - 4)
                src = bank(5).rearrange("p (a n) -> p a n", a=2)
                a = 2 * (u // 2)
                if u % 2:
                    act.activation(q1T[s][:, a:a + 2, :], src, ACT.Copy).then_inc(f_trs, 1)
                else:
                    act.activation(k1Z[s][0:64, a:a + 2, 0, :], src[0:64], ACT.Copy)
                    act.activation(k1Z[s][64:P, a:a + 2, 1, :], src[64:P], ACT.Copy).then_inc(f_trs, 1)

            def expo(m, s, a):
                act.wait_ge(f_nb, m * 4 + a + 1)
                if later(m * 4 + a - 1):
                    act.wait_ge(f_t, m * 4 + a - 1)
                k = a % 2
                for t in range(TB):
                    for h in range(2):
                        if t == 0:
                            o, src = p0[k][:, h, :], bank(0)[:, h * P:(h + 1) * P]
                        else:
                            o, src = p1[k][:, h, WIN:S], bank(1)[:, h * 192:(h + 1) * 192]
                        last = act.activation(o, src, ACT.Exp, bias=nb1[k][:, t, h:h + 1],
                                              scale=rq8[s][:, t, 2 * a + h:2 * a + h + 1],
                                              accum_out=sm1[k][:, t, h:h + 1])
                last.then_inc(f_e, 1)

            def probs_out(m, a):
                act.wait_ge(f_t, m * 4 + a + 1)
                act.activation(pt1[0][:], bank(2)[:, 0:3 * P], ACT.Copy).then_inc(f_pt0, 1)

            def z_out(m, s, a):
                act.wait_ge(f_z, m * 4 + a + 1)
                if later(m - 1):
                    act.wait_ge(f_wo, m - 1)
                act.activation(oT1[s][:, a, :], bank(2)[:, 0:S], ACT.Copy).then_inc(f_zsb, 1)

            def normed_out(m):
                act.wait_ge(f_wf1, m + 1)
                act.wait_ge(f_h2ps, m + 1)
                act.activation(h2T[:], bank(6)[:, 0:S], ACT.Identity,
                               scale=lv[:, 0:1], bias=lv[:, 1:2]).then_inc(f_h2, 1)

            def gelus(m):
                act.wait_ge(f_g, m + 1)
                if later(m):
                    act.wait_ge(f_hg, m)
                for c, (o, w) in enumerate(FCH):
                    last = act.activation(gl[0:w, c, :], hidden_bank(1, c), ACT.Gelu, bias=lv[0:w, 5 + c:6 + c])
                last.then_inc(f_gl, 1)

            def step(n, s):
                if live(n + 2): square(n + 2, 0)
                if live(n + 1): turned_out(n + 1, 1 - s, 0)
                if live(n): expo(n, s, 1)
                if live(n): probs_out(n, 0)
                if live(n): z_out(n, s, 0)
                if live(n + 2): square(n + 2, 1)
                if live(n + 1): turned_out(n + 1, 1 - s, 1)
                if live(n): expo(n, s, 2)
                if live(n): probs_out(n, 1)
                if live(n + 2): square(n + 2, 2)
                if live(n): z_out(n, s, 1)
                if live(n + 1): turned_out(n + 1, 1 - s, 2)
                if live(n): expo(n, s, 3)
                if live(n): probs_out(n, 2)
                if live(n - 1): normed_out(n - 1)
                if live(n + 1): value_out(n + 1, 1 - s, 0)
                if live(n): z_out(n, s, 2)
                if live(n + 1): value_out(n + 1, 1 - s, 1)
                if live(n + 2): square(n + 2, 3)
                if live(n + 1): expo(n + 1, 1 - s, 0)
                if live(n + 1): turned_out(n + 1, 1 - s, 3)
                if live(n): probs_out(n, 3)
                if live(n - 1): gelus(n - 1)
                if live(n): z_out(n, s, 3)
                if live(n + 3): shift_in(n + 3, 1 - s)

            run_steps(act, step)
            end_phase(act, 5)

        @block.tensor
        def _(pe):
            pe.wait_ge(const_ready, 1)
            pe.wait_ge(rows_in, 16 * N_ROWS)
            pe.transpose(bank(0)[:, 0:P], vrows[:], ident[:]).then_inc(vec_ps, 1)
            pe.wait_ge(w_in, 16 * N_W)
            for a in range(PAIRS0):
                if a % 4 == 0:
                    pe.wait_ge(bv_ready, a // 4 + 1)
                mm = pe.matmul(bank(1)[:, 0:D], bv_wide[:, a % 4, :], w_o0[:, a, :],
                               start=(a == 0), stop=(a == PAIRS0 - 1))
                if a % 4 == 3:
                    mm.then_inc(bo_ps, 1)
            pe.sem_inc(a_tr, FREE)
            with pe.Fori(0, NC) as c:
                pe.wait_ge(a_xn, c + 1)
                pe.wait_ge(a_xt, c + FREE)
                for t in range(CH):
                    mm = pe.transpose(bank(0)[:, t * P:(t + 1) * P], xn[:, t, :], ident[:])
                mm.then_inc(a_tr, 1)
            end_phase(pe, 1)
            pe.wait_ge(b_zero, 2)

            def project(g, s, turn):
                pe.wait_ge(staged[s], (turn + 1) * 32)
                if later(g):
                    pe.wait_ge(b_qksb, g)
                for j in range(2):
                    mm = pe.matmul(bank(6)[:, j * S:(j + 1) * S], wst[s][:, j * P:(j + 1) * P], xst[s][:],
                                   start=True, stop=True)
                mm.then_inc(b_qk, 1)

            def project_v(g, s):
                if later(g):
                    pe.wait_ge(b_vsb, g)
                for t in range(TB):
                    mm = pe.matmul(bank(7)[:, t * P:(t + 1) * P], xst[s][:, t * P:(t + 1) * P],
                                   wst[s][:, 2 * P:3 * P], start=True, stop=True)
                mm.then_inc(b_v, 1)

            def scores(g, s):
                pe.wait_ge(b_qksb, g + 1)
                if later(g - 1):
                    pe.wait_ge(b_e, g * 2 - 2)
                pe.matmul(score_bank(s, 0).rearrange("p (h n) -> p h n", h=2)[:, :, 0:P], qT[s][:, 0:P],
                          kZ[s][:, :, 0:P], start=True, stop=True)
                pe.matmul(score_bank(s, 1), qT[s][:, P:S], kZ[s][:].rearrange("p h n -> p (h n)"),
                          start=True, stop=True).then_inc(b_s, 1)

            def turn_probs(g, s, h):
                pe.wait_ge(b_p, g + 1)
                if later(g):
                    pe.wait_ge(b_zsb, g)
                for kt in range(TB):
                    for t in range(TB):
                        mm = pe.transpose(bank(4 + h)[:, kt * S + t * P:kt * S + (t + 1) * P],
                                          pr[s][:, t, h, kt * P:(kt + 1) * P], ident[:])
                mm.then_inc((b_t0, b_t1)[h], 1)

            def values(g, s):
                pe.wait_ge(b_pt0, g + 1)
                pe.wait_ge(b_pt1, g + 1)
                pe.wait_ge(b_vsb, g + 1)
                for kt in range(TB):
                    for h in range(2):
                        mm = pe.matmul(bank(4)[h * 64:(h + 1) * 64, 0:S], vS[s][:, kt, h * 64:(h + 1) * 64],
                                       pt[h][:, kt * S:(kt + 1) * S], start=(kt == 0), stop=(kt == TB - 1))
                mm.then_inc(b_z, 1)

            def slot(g, s, h):
                if slot_live(g): turn_probs(g, s, 0)
                if slot_live(g): turn_probs(g, s, 1)
                if slot_live(g + 2): scores(g + 2, s)
                if slot_live(g): values(g, s)
                if slot_live(g + 3): project(g + 3, 1 - s, h + (3 + s) // 2)
                if slot_live(g + 2): project_v(g + 2, s)

            run_slots(pe, slot)
            end_phase(pe, 2)
            def attn_out0(c):
                if c >= 2:
                    pe.wait_ge(c_mid, c - 1)
                for t in range(CH):
                    b, o = (c * CH + t) // TB, (t % TB) * P
                    for a in range(PAIRS0):
                        mm = pe.matmul(bank(6 + c % 2)[:, t * P:(t + 1) * P], zT[:, b * PAIRS0 + a, o:o + P],
                                       w_o0[:, a, :], start=(a == 0), stop=(a == PAIRS0 - 1))
                mm.then_inc(c_o, 1)

            def turn_x1(c):
                pe.wait_ge(c_x1, c + 1)
                if c >= 2:
                    pe.wait_ge(c_xt, c - 1)
                for t in range(CH):
                    mm = pe.transpose(bank(4 + c % 2)[:, t * P:(t + 1) * P], acc[:, c * CH + t, :], ident[:])
                mm.then_inc(c_xtps, 1)

            for c in range(NC):
                attn_out0(c)
                if c >= 2:
                    turn_x1(c - 2)
            turn_x1(NC - 2)
            turn_x1(NC - 1)
            pe.wait_ge(c_xt, NC)
            pe.wait_ge(c_mid, NC)
            for t in range(NT):
                mm = pe.matmul(bank(6)[:, t * NE:(t + 1) * NE], xT[:, t * P:(t + 1) * P], w_r[:],
                               start=True, stop=True)
            mm.then_inc(c_lg, 1)

            def turn_comb(c):
                if c == 0:
                    pe.wait_ge(c_comb, 1)
                if c >= 2:
                    pe.wait_ge(c_ct, c - 1)
                for t in range(CH):
                    mm = pe.transpose(bank(6 + c % 2)[0:NE, t * P:(t + 1) * P], comb[:, c * CH + t, :], ident[:])
                mm.then_inc(c_ctps, 1)

            def bias_out(c):
                pe.wait_ge(c_ct, c + 1)
                if c >= 2:
                    pe.wait_ge(c_acc, c - 1)
                for t in range(CH):
                    mm = pe.matmul(bank(4 + c % 2)[:, t * P:(t + 1) * P], combT[c % 2][:, t * P:(t + 1) * P],
                                   b2e[:], start=True, stop=True)
                mm.then_inc(c_yb, 1)

            pe.sem_inc(y_ready, 2)

            def up(n, u, turn):
                if u % NC == 0:
                    pe.wait_ge(we_in[u // NC % 2], (turn + 1) * 32)
                pe.wait_ge(g_ready, n + 1)
                for kt in range(KE):
                    mm = pe.matmul(bank(2 * (u % 2) + kt), w1e[u // NC % 2][:, kt * P:(kt + 1) * P],
                                   xT[:, (u % NC) * CH * P:(u % NC + 1) * CH * P], start=True, stop=True)
                mm.then_inc(u_ready, 1)

            def down(n, u):
                pe.wait_ge(g_ready, n + 1 + 2)
                pe.wait_ge(acc_done, n + 1)
                for t in range(CH):
                    for kt in range(KE):
                        mm = pe.matmul(bank(4 + u % 2)[:, t * P:(t + 1) * P], gE[u % 2][:, kt, t * P:(t + 1) * P],
                                       w2e[u // NC][:, kt, :], start=(kt == 0), stop=(kt == KE - 1))
                mm.then_inc(y_ready, 1)

            up(0, 0, 0)
            for c in range(NC):
                turn_comb(c)
                if c >= 1:
                    bias_out(c - 1)
            bias_out(NC - 1)
            pe.wait_ge(c_acc, NC)
            with pe.Fori(0, NE // 2 - 1) as i:
                for u in range(2 * NC):
                    up(i * 2 * NC + u + 1, u + 1, i + (u + 1) // (2 * NC))
                    down(i * 2 * NC + u, u)
            for u in range(2 * NC):
                n = (NE // 2 - 1) * 2 * NC + u
                if u + 1 < 2 * NC:
                    up(n + 1, u + 1, NE // 2 - 1)
                down(n, u)
            end_phase(pe, 3)
            def turn0(b):
                pe.wait_ge(e_nrm, b + 1)
                if b >= 2:
                    pe.wait_ge(e_xn, b - 1)
                for t in range(TB):
                    pe.transpose(bank(b % 2)[:, t * P:(t + 1) * P], x2[b % 4][:, t, :], ident[:])
                    mm = pe.transpose(bank(b % 2)[:, S + t * P:S + (t + 1) * P], nrm[b % 2][:, t, :], ident[:])
                mm.then_inc(e_xnps, 1)

            def similarities(b):
                pe.wait_ge(e_xn, b + 1)
                if b >= 2:
                    pe.wait_ge(e_rel, b - 1)
                for t in range(TB):
                    mm = pe.matmul(bank(2 + b % 2)[:, t * S:(t + 1) * S], xnT[b % 2][:, S + t * P:S + (t + 1) * P],
                                   xnT[b % 2][:, S:2 * S], start=True, stop=True)
                mm.then_inc(e_sim, 1)

            def counter(b):
                pe.wait_ge(e_rel, b + 1)
                if b >= 2:
                    pe.wait_ge(e_log, b - 1)
                for t in range(TB):
                    mm = pe.matmul(bank(4 + b % 2)[:, 0:S], w1c[:], rel[b % 2][:, t * S:(t + 1) * S],
                                   start=(t == 0), stop=(t == TB - 1))
                mm.then_inc(e_ctr, 1)

            def out0(b):
                pe.wait_ge(e_sp, b + 1)
                if b >= 2:
                    pe.wait_ge(e_y, b - 1)
                for t in range(TB):
                    o = bank(6 + b % 2)[:, t * P:(t + 1) * P]
                    pe.matmul(o, xnT[b % 2][:, t * P:(t + 1) * P], w2c[:, 0, :], start=True, stop=False)
                    mm = pe.matmul(o, sp[b % 2][:, t * P:(t + 1) * P], w2c[:, 1, :], start=False, stop=True)
                mm.then_inc(e_o, 1)

            def batch(b):
                if batch_live(b + 1): similarities(b + 1)
                if batch_live(b): out0(b)
                if batch_live(b + 1): counter(b + 1)
                if batch_live(b + 2): turn0(b + 2)

            run_batches(pe, batch)
            end_phase(pe, 4)
            pe.wait_ge(f_zero, 1)

            def turn_x(m):
                pe.wait_ge(f_xc, m + 1)
                if later(m):
                    pe.wait_ge(f_hT, m)
                if later(m - 1):
                    pe.wait_ge(f_trs, m * 4 - 4)
                for t in range(TB):
                    mm = pe.transpose(bank(5)[:, t * P:(t + 1) * P], xc[:, t, :], ident[:])
                mm.then_inc(f_xT, 1)

            def project1(m, s, i):
                if i == 0:
                    pe.wait_ge(f_wqk, m + 1)
                    pe.wait_ge(f_hT, m + 1)
                if later(m * 4 + i):
                    pe.wait_ge(f_rot, m * 4 + i)
                if i == 3 and later(m):
                    pe.wait_ge(f_v, m * 2 - 1)
                j, t = 1 - i // 2, i % 2
                pe.matmul(bank(4), hT[s][:, t * P:(t + 1) * P], wqkv1[:, j * INNER:(j + 1) * INNER],
                          start=True, stop=True).then_inc(f_qk, 1)

            def project_v(m, s, t):
                if t == 0:
                    pe.wait_ge(f_wv, m + 1)
                    pe.wait_ge(f_rot, m * 4 + (7 if live(m + 1) else 4))
                else:
                    pe.wait_ge(f_trs, m * 4 + 3)
                pe.matmul(bank(4 + t), hT[s][:, t * P:(t + 1) * P], wqkv1[:, 2 * INNER:],
                          start=True, stop=True).then_inc(f_vps, 1)

            def turn_qk(m, s, u):
                if u == 0:
                    pe.wait_ge(f_kn, m + 1)
                    if live(m + 1):
                        pe.wait_ge(f_hT, m + 2)
                    if later(m):
                        pe.wait_ge(f_trs, m * 4)
                if u == 1:
                    pe.wait_ge(f_add, m * 4 + 4)
                if u in (1, 2):
                    pe.wait_ge(f_trs, m * 4 + u)
                if u == 3:
                    pe.wait_ge(f_v, m * 2 + 2)
                j, a = 1 - u % 2, 2 * (u // 2)
                for b_ in range(2):
                    for t in range(TB):
                        o = j * INNER + (a + b_) * P
                        mm = pe.transpose(bank(5)[:, b_ * S + t * P:b_ * S + (t + 1) * P],
                                          qk[s][t][:, o:o + P], ident[:])
                mm.then_inc(f_tr, 1)

            def scores1(m, s, a):
                if a % 2 == 0:
                    pe.wait_ge(f_trs, m * 4 + a + 2)
                if later(m * 4 + a):
                    pe.wait_ge(f_e, m * 4 + a)
                o = bank(0)[:, 0:2 * P].rearrange("p (h n) -> p h n", h=2)
                pe.matmul(o, q1T[s][:, a, 0:P], k1Z[s][:, a, :, 0:P], start=True, stop=False)
                pe.matmul(o, identb[:], band0[:], start=False, stop=True)
                o = bank(1)[:, 0:384].rearrange("p (h n) -> p h n", h=2)
                pe.matmul(o, q1T[s][:, a, P:S], k1Z[s][:, a, :, WIN:S], start=True, stop=False)
                pe.matmul(o, identb[:], band1[:], start=False, stop=True).then_inc(f_s, 1)

            def turn_probs1(m, a):
                pe.wait_ge(f_p, m * 4 + a + 1)
                if later(m * 4 + a):
                    pe.wait_ge(f_zsb, m * 4 + a)
                k = a % 2
                for h in range(2):
                    pe.transpose(bank(2 + h)[:, 0:P], p0[k][:, h, :], ident[:])
                    for kt in range(TB):
                        mm = pe.transpose(bank(2 + h)[:, (kt + 1) * P:(kt + 2) * P],
                                          p1[k][:, h, kt * P:(kt + 1) * P], ident[:])
                mm.then_inc(f_t, 1)

            def values1(m, s, a):
                pe.wait_ge(f_pt0, m * 4 + a + 1)
                pe.wait_ge(f_pt1, m * 4 + a + 1)
                if a == 0:
                    pe.wait_ge(f_v, m * 2 + 2)
                for h in range(2):
                    v = v1[s][:, :, (2 * a + h) * DH:(2 * a + h + 1) * DH]
                    o = bank(2)[h * 64:(h + 1) * 64]
                    pe.matmul(o[:, 0:S], v[:, 0, :], pt1[h][:, 0:S], start=True, stop=False,
                              skip_group_check=True)
                    mm = pe.matmul(o[:, P:S], v[:, 1, :], pt1[h][:, S:3 * P], start=False, stop=True,
                                   skip_group_check=True)
                mm.then_inc(f_z, 1)

            def attn_out(m, s):
                pe.wait_ge(f_wwo, m + 1)
                pe.wait_ge(f_zsb, m * 4 + 4)
                if later(m):
                    pe.wait_ge(f_hg, m)
                for t in range(TB):
                    for a in range(PAIRS1):
                        mm = pe.matmul(bank(6)[:, t * P:(t + 1) * P], oT1[s][:, a, t * P:(t + 1) * P], wo1[:, a, :],
                                       start=(a == 0), stop=(a == PAIRS1 - 1))
                mm.then_inc(f_wo, 1)

            def shift_mid(m, s):
                pe.wait_ge(f_xm, m + 1)
                o = bank(6)[:, S:2 * S].rearrange("p (t d) -> p t d", t=TB)
                pe.matmul(o[:, :, 0:64], ident[:], xm[s][:, :, 0:64], start=True, stop=True, skip_group_check=True)
                pe.matmul(o[:, :, 64:P], shift[:], xm[s][:, :, 64:P], start=True, stop=False, skip_group_check=True)
                pe.matmul(o[:, 1, 64:P], carry[:], xm[s][:, 0, 64:P], start=False, stop=True,
                          skip_group_check=True).then_inc(f_sh, 1)

            def turn_normed(m):
                pe.wait_ge(f_hn, m + 1)
                for t in range(TB):
                    mm = pe.transpose(bank(6)[:, t * P:(t + 1) * P], hn[:, t, :], ident[:])
                mm.then_inc(f_h2ps, 1)

            def hidden(m, half_):
                if half_ == 1:
                    pe.wait_ge(f_wf1, m + 1)
                    pe.wait_ge(f_h2, m + 1)
                    pe.wait_ge(f_x, m + B)
                else:
                    pe.wait_ge(f_gl, m + 1)
                for c, (o, w) in enumerate(FCH):
                    mm = pe.matmul(hidden_bank(half_, c), wf1[:, half_ * HID + o:half_ * HID + o + w], h2T[:],
                                   start=True, stop=True)
                mm.then_inc((f_a, f_g)[half_], 1)

            def ffn_out(m):
                pe.wait_ge(f_wf2, m + 1)
                pe.wait_ge(f_hg, m + 1)
                for t in range(TB):
                    for c in range(3):
                        w = P if c < 2 else HID - 255
                        mm = pe.matmul(bank(7)[:, t * P:(t + 1) * P], hg[0:w, c, t * P:(t + 1) * P],
                                       wf2[0:w, c, :], start=(c == 0), stop=(c == 2))
                mm.then_inc(f_w2, 1)

            def step(n, s):
                if live(n + 2): project1(n + 2, s, 0)
                if live(n + 1): turn_qk(n + 1, 1 - s, 0)
                if live(n): scores1(n, s, 1)
                if live(n - 1): attn_out(n - 1, 1 - s)
                if live(n): turn_probs1(n, 0)
                if live(n): values1(n, s, 0)
                if live(n): scores1(n, s, 2)
                if live(n + 2): project1(n + 2, s, 1)
                if live(n + 1): turn_qk(n + 1, 1 - s, 1)
                if live(n): turn_probs1(n, 1)
                if live(n - 1): shift_mid(n - 1, 1 - s)
                if live(n - 2): ffn_out(n - 2)
                if live(n): values1(n, s, 1)
                if live(n): scores1(n, s, 3)
                if live(n + 2): project1(n + 2, s, 2)
                if live(n + 1): turn_qk(n + 1, 1 - s, 2)
                if live(n): turn_probs1(n, 2)
                if live(n - 1): turn_normed(n - 1)
                if live(n + 1): project_v(n + 1, 1 - s, 0)
                if live(n + 1): project_v(n + 1, 1 - s, 1)
                if live(n): values1(n, s, 2)
                if live(n + 1): scores1(n + 1, 1 - s, 0)
                if live(n + 2): project1(n + 2, s, 3)
                if live(n + 1): turn_qk(n + 1, 1 - s, 3)
                if live(n - 1): hidden(n - 1, 1)
                if live(n): turn_probs1(n, 3)
                if live(n): values1(n, s, 3)
                if live(n - 1): hidden(n - 1, 0)
                if live(n + 3): turn_x(n + 3)

            run_steps(pe, step)
            end_phase(pe, 5)

        @block.vector
        def _(dve):
            def ln_stats(src, n, k, ready):
                for t in range(n):
                    dve.bn_stats(st[:, k, t, :], src(t))
                dve.drain()
                for t in range(n):
                    dve.bn_aggr(mv[:, k, t, :], st[:, k, t, :])
                dve.drain()
                dve.tensor_scalar(ve[:, k, 0:n], mv[:, k, 0:n, 1], EPS, None, ALU.add).then_inc(ready, 1)

            def ln_apply(dst, src, n, k):
                for t in range(n):
                    last = dve.tensor_scalar(dst(t), src(t), mv[:, k, t, 0:1], rstd[:, k, t:t + 1],
                                             ALU.subtract, ALU.mult)
                return last

            dve.memset(vrows[:], 0.0).then_inc(rows_zero, 1)
            dve.wait_ge(w_in, 16 * N_W)
            for la in range(LAYERS):
                for j in range(2):
                    for t in range(TB):
                        dve.tensor_tensor(rot[:, la, 2 * j, t, :], tab[:, 2 * j, t, :], qks[:, j, la, :], ALU.mult)
                        for a, b_ in ((0, 32), (32, 0)):
                            dve.tensor_tensor(rot[:, la, 2 * j + 1, t, a:a + 32], tab[:, 2 * j + 1, t, a:a + 32],
                                              qks[:, j, la, b_:b_ + 32], ALU.mult)
            dve.wait_ge(bo_ps, 2)
            dve.tensor_tensor(bo_all[:], bo_all[:], bank(1)[:, 0:D], ALU.add).then_inc(bo_ready, 1)
            dve.wait_ge(x_in, 16)
            with dve.Fori(0, NC) as c:
                ln_stats(lambda t: x0[:, c * CH + t, :], CH, 0, a_var)
                dve.wait_ge(a_rstd, c + 1)
                dve.wait_ge(a_tr, c + FREE)
                ln_apply(lambda t: xn[:, t, :], lambda t: x0[:, c * CH + t, :], CH, 0).then_inc(a_xn, 1)
            end_phase(dve, 1)
            for s in range(2):
                dve.memset(score_bank(s, 0).rearrange("p (h n) -> p h n", h=2)[:, :, P:S], 0.0)
            dve.drain().then_inc(b_zero, 1)
            mask = causal[:].unsqueeze(1).to_broadcast([P, 2, P])

            def neg_max(g, s):
                dve.wait_ge(b_s, g + 1)
                s0, s1 = (score_bank(s, t).rearrange("p (h n) -> p h n", h=2) for t in range(TB))
                dve.tensor_tensor(s0[:, :, 0:P], s0[:, :, 0:P], mask, ALU.mult)
                dve.tensor_tensor(s1[:, :, P:S], s1[:, :, P:S], mask, ALU.mult)
                dve.drain()
                dve.tensor_reduce(mx[:, 0:2], s0[:, :, 0:P], AX.X, ALU.max)
                dve.tensor_reduce(mx[:, 2:4], s1, AX.X, ALU.max)
                dve.drain()
                dve.tensor_scalar(nb[s][:, 0:2], mx[:, 0:2], -DH ** -0.5, 0.0, ALU.mult, ALU.min)
                dve.tensor_scalar(nb[s][:, 2:4], mx[:, 2:4], -DH ** -0.5, None, ALU.mult).then_inc(b_nb, 1)

            def normalise(g, s):
                dve.wait_ge(b_e, g * 2 + 2)
                dve.reciprocal(rs[:], sm[s][:])
                dve.drain()
                for t in range(TB):
                    for h in range(2):
                        last = dve.tensor_scalar(pr[s][:, t, h, :], pr[s][:, t, h, :], rs[:, 2 * t + h:2 * t + h + 1],
                                                 None, ALU.mult)
                last.then_inc(b_p, 1)

            def probs_out(g):
                dve.wait_ge(b_t1, g + 1)
                if later(g):
                    dve.wait_ge(b_z, g)
                dve.tensor_copy(pt[1][:], bank(5)).then_inc(b_pt1, 1)

            def v_out(g, s):
                dve.wait_ge(b_v, g + 1)
                if later(g - 1):
                    dve.wait_ge(b_z, g - 1)
                dve.tensor_copy(vS[s][:].rearrange("p t n -> p (t n)"), bank(7)[:, 0:S]).then_inc(b_vsb, 1)

            def slot(g, s, h):
                if slot_live(g): probs_out(g)
                if slot_live(g + 1): normalise(g + 1, 1 - s)
                if slot_live(g + 2): neg_max(g + 2, s)
                if slot_live(g + 2): v_out(g + 2, s)

            run_slots(dve, slot)
            end_phase(dve, 2)
            dve.wait_ge(c_x0, 1)

            def mid_stats(c):
                dve.wait_ge(c_o, c + 1)
                dve.tensor_tensor(mid[c % 2], bank(6 + c % 2).rearrange("p (t d) -> p t d", t=CH),
                                  x3[:, c * CH:(c + 1) * CH, :], ALU.add)
                dve.drain().then_inc(c_mid, 1)
                ln_stats(lambda t: mid[c % 2][:, t, :], CH, 2 * (c % 2), c_var)

            def post_stats(c):
                y = acc[:, c * CH:(c + 1) * CH, :]
                dve.wait_ge(c_rstd, c_count(c, 0))
                ln_apply(lambda t: y[:, t, :], lambda t: mid[c % 2][:, t, :], CH, 2 * (c % 2))
                dve.drain()
                dve.tensor_tensor(y, y, ln2w[:].unsqueeze(1).to_broadcast([P, CH, D]), ALU.mult)
                dve.drain()
                dve.wait_ge(c_u, c + 1)
                dve.tensor_tensor(y, y, uC[c % 2], ALU.add)
                dve.drain()
                ln_stats(lambda t: y[:, t, :], CH, 2 * (c % 2) + 1, c_var)

            def post_apply(c):
                y = acc[:, c * CH:(c + 1) * CH, :]
                dve.wait_ge(c_rstd, c_count(c, 1))
                ln_apply(lambda t: y[:, t, :], lambda t: y[:, t, :], CH, 2 * (c % 2) + 1).then_inc(c_x1, 1)

            mid_stats(0)
            for c in range(NC):
                if c + 1 < NC:
                    mid_stats(c + 1)
                if c >= 1:
                    post_apply(c - 1)
                post_stats(c)
            post_apply(NC - 1)
            bc = lambda v: v.unsqueeze(2).to_broadcast([P, NT, NE])
            dve.wait_ge(c_top, 1)
            dve.wait_ge(c_lg, 1)
            dve.tensor_tensor(lg[:], bank(6)[:, 0:NT * NE].rearrange("p (t e) -> p t e", t=NT),
                              br[:].unsqueeze(1).to_broadcast([P, NT, NE]), ALU.add)
            dve.drain()
            dve.tensor_reduce(rmax[:], lg[:], AX.X, ALU.max)
            dve.drain()
            dve.tensor_tensor(lg[:], lg[:], bc(rmax[:]), ALU.subtract).then_inc(c_sub, 1)
            dve.wait_ge(c_exp, 1)
            dve.tensor_reduce(rsum[:], ex[:], AX.X, ALU.add)
            dve.drain()
            dve.reciprocal(rsum[:], rsum[:])
            dve.drain()
            dve.tensor_tensor(ex[:], ex[:], bc(rsum[:]), ALU.mult)
            dve.drain()
            for t in range(NT):
                dve.max(m8[:, t, :], ex[:, t, :])
            dve.drain()
            dve.tensor_copy(top2[:, :, 0:2], m8[:, :, 0:2])
            dve.tensor_tensor(rsum[:], m8[:, :, 0], m8[:, :, 1], ALU.add)
            dve.drain()
            dve.tensor_scalar(rsum[:], rsum[:], 1e-9, None, ALU.max)
            for t in range(NT):
                dve.match_replace(rest[:, t, :], top2[:, t, :], ex[:, t, :], 0.0)
            dve.drain()
            dve.reciprocal(rsum[:], rsum[:])
            dve.tensor_tensor(rest[:], ex[:], rest[:], ALU.subtract)
            dve.drain()
            dve.tensor_tensor(comb[:], rest[:], bc(rsum[:]), ALU.mult).then_inc(c_comb, 1)
            for c in range(NC):
                y = acc[:, c * CH:(c + 1) * CH, :].rearrange("p t d -> p (t d)")
                dve.wait_ge(c_yb, c + 1)
                dve.scalar_tensor_tensor(y, y, 2.0, bank(4 + c % 2), ALU.mult, ALU.add).then_inc(c_acc, 1)
            dve.drain()
            dve.sem_inc(acc_done, 2)
            with dve.Fori(0, NE // 2) as i:
                for u in range(2 * NC):
                    dve.wait_ge(y_ready, i * 2 * NC + u + 1 + 2)
                    for t in range(CH):
                        tt = (u % NC) * CH + t
                        last = dve.scalar_tensor_tensor(
                            acc[:, tt, :], bank(4 + u % 2)[:, t * P:(t + 1) * P],
                            comb[:, tt, bass.ds(i * 2 + u // NC, 1)], acc[:, tt, :], ALU.mult, ALU.add)
                    dve.drain().then_inc(acc_done, 1)
            end_phase(dve, 3)
            def norm_stats(b):
                ln_stats(lambda t: acc[:, b * TB + t, :], TB, b % 2, e_var)

            def normed(b):
                dve.wait_ge(e_rstd, b + 1)
                ln_apply(lambda t: x2[b % 4][:, t, :], lambda t: acc[:, b * TB + t, :], TB, b % 2).then_inc(e_x2, 1)

            def square_floor(b):
                dve.wait_ge(e_ssq, b + 1)
                dve.tensor_scalar(mq[b % 2][:], ssq[b % 2][:], 1e-12, None, ALU.max).then_inc(e_mq, 1)

            def unit_rows(b):
                dve.wait_ge(e_rn, b + 1)
                if b >= 2:
                    dve.wait_ge(e_xnps, b - 1)
                for t in range(TB):
                    last = dve.tensor_scalar(nrm[b % 2][:, t, :], x2[b % 4][:, t, :], rn[b % 2][:, t:t + 1], None, ALU.mult)
                last.then_inc(e_nrm, 1)

            def softplus(b):
                dve.wait_ge(e_log, b + 1)
                if b >= 2:
                    dve.wait_ge(e_o, b - 1)
                dve.scalar_tensor_tensor(sp[b % 2][:], zb[b % 2][:], 0.0, az[b % 2][:], ALU.max, ALU.add).then_inc(e_sp, 1)

            def end_stats(b):
                y = x2[b % 4]
                dve.wait_ge(e_o, b + 1)
                dve.tensor_tensor(y[:], y[:], bank(6 + b % 2)[:, 0:S].rearrange("p (t d) -> p t d", t=TB), ALU.add)
                dve.drain().then_inc(e_y, 1)
                ln_stats(lambda t: y[:, t, :], TB, 2 + b % 2, e_yvar)

            def end_apply(b):
                dve.wait_ge(e_yrstd, b + 1)
                ln_apply(lambda t: x3[:, b * TB + t, :], lambda t: x2[b % 4][:, t, :], TB, 2 + b % 2).then_inc(e_x3, 1)

            def batch(b):
                if batch_live(b + 2): norm_stats(b + 2)
                if batch_live(b): softplus(b)
                if batch_live(b + 2): normed(b + 2)
                if batch_live(b): end_stats(b)
                if batch_live(b + 2): square_floor(b + 2)
                if batch_live(b + 2): unit_rows(b + 2)
                if batch_live(b): end_apply(b)

            run_batches(dve, batch)
            end_phase(dve, 4)
            dve.wait_ge(f_zero, 1)
            dve.sem_inc(f_x, B)

            def rotate(m, i):
                j, t = 1 - i // 2, i % 2
                dve.wait_ge(f_sq, m * 4 + i + 1)
                if i % 2 == 0 and later(m):
                    dve.wait_ge((f_rk, f_rq)[i // 2], m)
                o3 = lambda v: v.rearrange("p (h k) -> p h k", k=DH)
                dve.tensor_reduce(ss[:, t, j * H1:(j + 1) * H1], o3(sq1[i % 2]), AX.X, ALU.add)
                if later(m * 4 + i - 1):
                    dve.wait_ge(f_add, m * 4 + i - 1)
                src = o3(bank(4))
                o1, o2 = o3(t1[i % 2]), o3(t2[i % 2])
                ca = rotc[:, 2 * j, t, :].unsqueeze(1).to_broadcast([P, H1, DH])
                cb = rotc[:, 2 * j + 1, t, :].unsqueeze(1).to_broadcast([P, H1, DH])
                dve.tensor_tensor(o1, src, ca, ALU.mult)
                dve.tensor_tensor(o2[:, :, 0:32], src[:, :, 32:64], cb[:, :, 0:32], ALU.mult)
                dve.tensor_tensor(o2[:, :, 32:64], src[:, :, 0:32], cb[:, :, 32:64], ALU.mult).then_inc(f_rot, 1)
                if i % 2 == 1:
                    dve.drain()
                    dve.tensor_scalar(ss[:, :, j * H1:(j + 1) * H1], ss[:, :, j * H1:(j + 1) * H1], 1e-24, None,
                                      ALU.max).then_inc(f_ss, 1)

            def query_scales(m, s):
                dve.wait_ge(f_rq, m + 1)
                dve.tensor_scalar(rq8[s][:], rqk[:, :, 0:H1], 8.0, None, ALU.mult)
                dve.tensor_scalar(nrq8[s][:], rqk[:, :, 0:H1], -8.0, None, ALU.mult).then_inc(f_rq8, 1)

            def neg_max(m, s, a):
                k = a % 2
                dve.wait_ge(f_s, m * 4 + a + 1)
                dve.tensor_reduce(mx1[k][:, 0, :], bank(0)[:, 0:2 * P].rearrange("p (h n) -> p h n", h=2), AX.X, ALU.max)
                dve.tensor_reduce(mx1[k][:, 1, :], bank(1)[:, 0:384].rearrange("p (h n) -> p h n", h=2), AX.X, ALU.max)
                dve.drain()
                dve.tensor_tensor(nb1[k][:], mx1[k][:], nrq8[s][:, :, 2 * a:2 * a + 2], ALU.mult).then_inc(f_nb, 1)

            def normalise1(m, a):
                k = a % 2
                dve.wait_ge(f_e, m * 4 + a + 1)
                dve.reciprocal(rs1[k][:], sm1[k][:])
                dve.drain()
                for h in range(2):
                    dve.tensor_scalar(p0[k][:, h, :], p0[k][:, h, :], rs1[k][:, 0, h:h + 1], None, ALU.mult)
                    last = dve.tensor_scalar(p1[k][:, h, WIN:S], p1[k][:, h, WIN:S], rs1[k][:, 1, h:h + 1], None, ALU.mult)
                last.then_inc(f_p, 1)

            def probs_out(m, a):
                dve.wait_ge(f_t, m * 4 + a + 1)
                dve.tensor_copy(pt1[1][:], bank(3)[:, 0:3 * P]).then_inc(f_pt1, 1)

            def residual_mid(m, s):
                dve.wait_ge(f_wo, m + 1)
                dve.tensor_tensor(xm[s][:], stream[:, bass.ds(m * TB, TB), :],
                                  bank(6)[:, 0:S].rearrange("p (t d) -> p t d", t=TB), ALU.add).then_inc(f_xm, 1)

            def residual_out(m, s):
                dve.wait_ge(f_w2, m + 1)
                dve.tensor_tensor(stream[:, bass.ds(m * TB + NT, TB), :], xm[s][:],
                                  bank(7)[:, 0:S].rearrange("p (t d) -> p t d", t=TB), ALU.add).then_inc(f_x, 1)

            def stats_mid(m):
                dve.wait_ge(f_sh, m + 1)
                ln_stats(lambda t: bank(6)[:, S + t * P:S + (t + 1) * P], TB, 0, f_var)

            def normed_mid(m):
                dve.wait_ge(f_rstd, m + 1)
                ln_apply(lambda t: hn[:, t, :], lambda t: bank(6)[:, S + t * P:S + (t + 1) * P],
                         TB, 0).then_inc(f_hn, 1)

            def gate(m):
                dve.wait_ge(f_a, m + 1)
                if later(m):
                    dve.wait_ge(f_w2, m)
                for c, (o, w) in enumerate(FCH):
                    last = dve.scalar_tensor_tensor(hg[0:w, c, :], hidden_bank(0, c), lv[0:w, 2 + c:3 + c],
                                                    gl[0:w, c, :], ALU.add, ALU.mult)
                last.then_inc(f_hg, 1)

            def step(n, s):
                if live(n): normalise1(n, 0)
                if live(n): neg_max(n, s, 1)
                if live(n + 2): rotate(n + 2, 0)
                if live(n): probs_out(n, 0)
                if live(n - 1): residual_mid(n - 1, 1 - s)
                if live(n): normalise1(n, 1)
                if live(n): neg_max(n, s, 2)
                if live(n): probs_out(n, 1)
                if live(n - 1): stats_mid(n - 1)
                if live(n - 2): residual_out(n - 2, s)
                if live(n + 2): rotate(n + 2, 1)
                if live(n): normalise1(n, 2)
                if live(n): neg_max(n, s, 3)
                if live(n - 1): normed_mid(n - 1)
                if live(n + 2): rotate(n + 2, 2)
                if live(n): probs_out(n, 2)
                if live(n + 1): query_scales(n + 1, 1 - s)
                if live(n): normalise1(n, 3)
                if live(n + 1): neg_max(n + 1, 1 - s, 0)
                if live(n + 2): rotate(n + 2, 3)
                if live(n): probs_out(n, 3)
                if live(n - 1): gate(n - 1)

            run_steps(dve, step)
            end_phase(dve, 5)
            for c in range(NC):
                x5c = x5[:, c * CH:(c + 1) * CH, :]
                dve.tensor_tensor(x5c, x5c, x3[:, c * CH:(c + 1) * CH, :], ALU.add)
            dve.drain()
            for c in range(NC + 1):
                if c < NC:
                    ln_stats(lambda t: x5[:, c * CH + t, :], CH, c % 2, h_var)
                if c > 0:
                    dve.wait_ge(h_rstd, c)
                    ln_apply(lambda t: x5[:, (c - 1) * CH + t, :], lambda t: x5[:, (c - 1) * CH + t, :], CH,
                             (c - 1) % 2).then_inc(h_out, 1)


N_W = 25


_INS = ['L0_attn_resid_pre', 'L0_attn_W_Q', 'L0_attn_b_Q', 'L0_attn_W_K', 'L0_attn_b_K', 'L0_attn_W_V',
        'L0_attn_b_V', 'L0_attn_W_O', 'L0_attn_b_O', 'L0_attn_ln1_w', 'L0_attn_ln1_b', 'L0_attn_ln2_w',
        'L0_attn_ln2_b', 'L0_ffn_Wr', 'L0_ffn_br', 'L0_ffn_W1', 'L0_ffn_b1', 'L0_ffn_W2', 'L0_ffn_b2',
        'L1_attn_W1', 'L1_attn_b1', 'L1_attn_W2', 'L1_ffn_wqkv', 'L1_ffn_q_scale', 'L1_ffn_k_scale',
        'L1_ffn_wo', 'L1_ffn_ln_g', 'L1_ffn_ln_b', 'L1_ffn_w1', 'L1_ffn_b1', 'L1_ffn_w2', 'L1_ffn_b2']


def rotary_tables():
    import numpy as np
    half = np.arange(0, DH, 2, dtype=np.float32)
    inv = (1.0 / np.float32(10000.0) ** (half / np.float32(DH))).astype(np.float32)
    t = np.arange(S, dtype=np.float32)
    freqs = t[:, None] * inv[None, :]
    base = ((half + np.float32(0.4 * DH)) / np.float32(1.4 * DH)).astype(np.float32)
    power = ((t - S // 2) / np.float32(WIN // 2)).astype(np.float32)
    scale = (base[None, :] ** power[:, None]).astype(np.float32)
    cos, sin = np.cos(freqs), np.sin(freqs)
    return np.stack([np.concatenate([cos * scale, cos * scale], -1),
                     np.concatenate([-sin * scale, sin * scale], -1),
                     np.concatenate([cos / scale, cos / scale], -1),
                     np.concatenate([-sin / scale, sin / scale], -1)]).astype(np.float32)


def kernel(**inputs):
    import numpy as np
    import concourse.bacc as bacc
    from concourse.bass_utils import run_bass_kernel_spmd

    nc = bacc.Bacc("TRN2", target_bir_lowering=False, num_devices=1)
    arrays, A = {}, {}
    for name in _INS + ["tables"]:
        a = rotary_tables() if name == "tables" else np.ascontiguousarray(inputs[name])
        arrays[f"in_{name}"] = a
        A[name] = nc.dram_tensor(f"in_{name}", a.shape, mybir.dt.from_np(a.dtype), kind="ExternalInput").ap()
    out = nc.dram_tensor("out_0", (B, S, D), F32, kind="ExternalOutput").ap()
    build_program(nc, A, out)
    r = run_bass_kernel_spmd(nc, [arrays], core_ids=[0])
    return r.results[0]["out_0"]
```
